# Optimizing a Trainium2 kernel written in Bass

```python
import numpy as np
import jax
import jax.numpy as jnp

def _softmax(x, axis=-1):
    return jax.nn.softmax(x, axis=axis)

def _gelu(x):
    return jax.nn.gelu(x, approximate=True)

def _silu(x):
    return jax.nn.silu(x)

def _sigmoid(x):
    return jax.nn.sigmoid(x)

def _layernorm(x, axis=-1, eps=1e-05):
    m = jnp.mean(x, axis=axis, keepdims=True)
    v = jnp.var(x, axis=axis, keepdims=True)
    return (x - m) / jnp.sqrt(v + eps)

def _scatter_add(tgt, idx, src, axis=0):
    return tgt.at[idx].add(src)

def _segment_sum(src, seg, n):
    return jax.ops.segment_sum(src, seg, n)
kernel_name = 'mk_audio_tower_d1_tok_audfeat256_r4_74fbc4'

def setup_inputs(seed: int=0):
    np.random.seed(seed)
    _w = jnp.asarray

    def _rec_inputs():
        import jax
        import jax.numpy as jnp
        _rk = jax.random.key(seed)
        x = -7.10856e-05 + 0.999911 * jax.random.normal(jax.random.fold_in(_rk, 1), (32, 2048, 64), jnp.float32)
        return x
    x = _rec_inputs()

    def _L0_tok_setup():
        import jax, jax.numpy as jnp
        import numpy as np
        key = jax.random.key(seed)
        k1, k2 = jax.random.split(key)
        N, L, F = (32, 2048, 64)
        x = jax.random.normal(k1, (N, L, F), dtype=jnp.float32)
        W = jax.random.normal(k2, (F, F), dtype=jnp.float32) * (1.0 / np.sqrt(F))
        return {'x': x, 'W': W, 'pool_size': 4}
    _L0_tok_all = _L0_tok_setup()
    _L0_tok_in = {k: v for k, v in _L0_tok_all.items() if k in ('W',)}
    del _L0_tok_all

    def _L0_attn_setup():
        import jax, jax.numpy as jnp
        import numpy as np
        NUM_HEADS = 8

        def _to_heads(y, R, C, H, hd):
            y = y.reshape(R, C, H, hd).transpose(0, 2, 1, 3)
            y = jnp.transpose(y, (2, 1, 0, 3)).reshape(1, H, C, R * hd)
            return y

        def _reference_tuple_inner(x, Wq, bq, Wk, bk, Wv, bv):
            R, C, E = x.shape
            H = NUM_HEADS
            hd = E // H
            q = _to_heads(x @ Wq.T + bq, R, C, H, hd)
            k = _to_heads(x @ Wk.T + bk, R, C, H, hd)
            v = _to_heads(x @ Wv.T + bv, R, C, H, hd)
            d = q.shape[-1]
            q = jax.nn.softmax(q, axis=-1)
            k = jax.nn.softmax(k, axis=-2)
            q = q * jnp.asarray(float(d) ** 0.5, dtype=q.dtype)
            attn_weights = jnp.einsum('bhnd,bhmd->bhnm', q, k).sum(0)
            context = jnp.einsum('bhnd,bhne->bhde', k, v)
            out = jnp.einsum('bhnd,bhde->hbne', q, context)
            out = out.reshape(H, C, R, hd)
            out = jnp.transpose(out, (2, 1, 0, 3)).reshape(R, C, E)
            return (out, attn_weights)
        key = jax.random.key(seed)
        ks = jax.random.split(key, 7)
        R, C, E = (16, 512, 64)
        x = jax.random.normal(ks[0], (R, C, E), dtype=jnp.float32)
        s = 0.02
        Wq = jax.random.normal(ks[1], (E, E), dtype=jnp.float32) * s
        bq = jax.random.normal(ks[2], (E,), dtype=jnp.float32) * s
        Wk = jax.random.normal(ks[3], (E, E), dtype=jnp.float32) * s
        bk = jax.random.normal(ks[4], (E,), dtype=jnp.float32) * s
        Wv = jax.random.normal(ks[5], (E, E), dtype=jnp.float32) * s
        bv = jax.random.normal(ks[6], (E,), dtype=jnp.float32) * s
        return {'x': x, 'Wq': Wq, 'bq': bq, 'Wk': Wk, 'bk': bk, 'Wv': Wv, 'bv': bv}
    _L0_attn_all = _L0_attn_setup()
    _L0_attn_in = {k: v for k, v in _L0_attn_all.items() if k in ('Wq', 'bq', 'Wk', 'bk', 'Wv', 'bv')}
    del _L0_attn_all

    def _L0_ffn_setup():
        import jax, jax.numpy as jnp
        import numpy as np
        DIM = 64
        HEADS = 8
        NUM_KEYS = 64
        NUM_KV = NUM_KEYS ** 2
        PK_TOPK = 16
        FINAL_TOPK = 16
        DIM_KEY = DIM // 2
        P = 2

        def _pk(x, Wq_pk, pk_keys):
            b, n, _ = x.shape
            q = (x @ Wq_pk).reshape(b, n, P, HEADS, DIM_KEY).transpose(2, 0, 1, 3, 4)
            sim = jnp.einsum('pbnhd,pkhd->pbnhk', q, pk_keys)
            scores, idx = jax.lax.top_k(sim, PK_TOPK)
            idx0 = idx[0]
            idx1 = idx[1] * NUM_KEYS
            index = (idx0[..., :, None] + idx1[..., None, :]).reshape(b, n, HEADS, PK_TOPK * PK_TOPK)
            score = (scores[0][..., :, None] + scores[1][..., None, :]).reshape(b, n, HEADS, PK_TOPK * PK_TOPK)
            final_scores, pk_idx = jax.lax.top_k(score, FINAL_TOPK)
            final_indices = jnp.take_along_axis(index, pk_idx, axis=-1)
            final_scores = jax.nn.softmax(final_scores, axis=-1)
            return (final_scores, final_indices)
        key = jax.random.key(seed)
        ks = jax.random.split(key, 7)
        b, n = (2, 256)
        std = 0.02
        x = jax.random.normal(ks[0], (b, n, DIM), dtype=jnp.float32)
        Wq_pk = jax.random.normal(ks[1], (DIM, P * HEADS * DIM_KEY), dtype=jnp.float32) * std
        pk_keys = jax.random.normal(ks[2], (P, NUM_KEYS, HEADS, DIM_KEY), dtype=jnp.float32) * std
        Wq = jax.random.normal(ks[3], (DIM, HEADS * DIM), dtype=jnp.float32) * std
        keys_table = jax.random.normal(ks[4], (NUM_KV * HEADS, DIM), dtype=jnp.float32) * std
        values_table = jax.random.normal(ks[5], (NUM_KV * HEADS, DIM), dtype=jnp.float32) * std
        Wo = jax.random.normal(ks[6], (DIM * HEADS, DIM), dtype=jnp.float32) * std
        return {'x': x, 'Wq_pk': Wq_pk, 'pk_keys': pk_keys, 'Wq': Wq, 'keys_table': keys_table, 'values_table': values_table, 'Wo': Wo}
    _L0_ffn_all = _L0_ffn_setup()
    _L0_ffn_in = {k: v for k, v in _L0_ffn_all.items() if k in ('Wq_pk', 'pk_keys', 'Wq', 'keys_table', 'values_table', 'Wo')}
    del _L0_ffn_all
    return {'x': x, 'L0_tok_W': _L0_tok_in['W'], 'L0_attn_Wq': _L0_attn_in['Wq'], 'L0_attn_bq': _L0_attn_in['bq'], 'L0_attn_Wk': _L0_attn_in['Wk'], 'L0_attn_bk': _L0_attn_in['bk'], 'L0_attn_Wv': _L0_attn_in['Wv'], 'L0_attn_bv': _L0_attn_in['bv'], 'L0_ffn_Wq_pk': _L0_ffn_in['Wq_pk'], 'L0_ffn_pk_keys': _L0_ffn_in['pk_keys'], 'L0_ffn_Wq': _L0_ffn_in['Wq'], 'L0_ffn_keys_table': _L0_ffn_in['keys_table'], 'L0_ffn_values_table': _L0_ffn_in['values_table'], 'L0_ffn_Wo': _L0_ffn_in['Wo']}

def reference(x, L0_tok_W, L0_attn_Wq, L0_attn_bq, L0_attn_Wk, L0_attn_bk, L0_attn_Wv, L0_attn_bv, L0_ffn_Wq_pk, L0_ffn_pk_keys, L0_ffn_Wq, L0_ffn_keys_table, L0_ffn_values_table, L0_ffn_Wo):
    import jax
    import jax.numpy as jnp

    def _L0_tok_ref(x, W, pool_size):
        import jax, jax.numpy as jnp
        import numpy as np
        N, L, F = x.shape
        p = int(pool_size)
        Lc = L - L % p
        xr = x[:, :Lc, :].reshape(N, Lc // p, p, F)
        raw = jnp.einsum('nlpf,fg->nlpg', xr, W)
        att = jax.nn.softmax(raw, axis=-2)
        return jnp.sum(xr * att, axis=-2)

    def _L0_attn_ref(x, Wq, bq, Wk, bk, Wv, bv):
        import jax, jax.numpy as jnp
        import numpy as np
        NUM_HEADS = 8

        def _to_heads(y, R, C, H, hd):
            y = y.reshape(R, C, H, hd).transpose(0, 2, 1, 3)
            y = jnp.transpose(y, (2, 1, 0, 3)).reshape(1, H, C, R * hd)
            return y

        def _reference_tuple_inner(x, Wq, bq, Wk, bk, Wv, bv):
            R, C, E = x.shape
            H = NUM_HEADS
            hd = E // H
            q = _to_heads(x @ Wq.T + bq, R, C, H, hd)
            k = _to_heads(x @ Wk.T + bk, R, C, H, hd)
            v = _to_heads(x @ Wv.T + bv, R, C, H, hd)
            d = q.shape[-1]
            q = jax.nn.softmax(q, axis=-1)
            k = jax.nn.softmax(k, axis=-2)
            q = q * jnp.asarray(float(d) ** 0.5, dtype=q.dtype)
            attn_weights = jnp.einsum('bhnd,bhmd->bhnm', q, k).sum(0)
            context = jnp.einsum('bhnd,bhne->bhde', k, v)
            out = jnp.einsum('bhnd,bhde->hbne', q, context)
            out = out.reshape(H, C, R, hd)
            out = jnp.transpose(out, (2, 1, 0, 3)).reshape(R, C, E)
            return (out, attn_weights)
        return _reference_tuple_inner(x, Wq, bq, Wk, bk, Wv, bv)[0]

    def _L0_ffn_ref(x, Wq_pk, pk_keys, Wq, keys_table, values_table, Wo):
        import jax, jax.numpy as jnp
        import numpy as np
        DIM = 64
        HEADS = 8
        NUM_KEYS = 64
        NUM_KV = NUM_KEYS ** 2
        PK_TOPK = 16
        FINAL_TOPK = 16
        DIM_KEY = DIM // 2
        P = 2

        def _pk(x, Wq_pk, pk_keys):
            b, n, _ = x.shape
            q = (x @ Wq_pk).reshape(b, n, P, HEADS, DIM_KEY).transpose(2, 0, 1, 3, 4)
            sim = jnp.einsum('pbnhd,pkhd->pbnhk', q, pk_keys)
            scores, idx = jax.lax.top_k(sim, PK_TOPK)
            idx0 = idx[0]
            idx1 = idx[1] * NUM_KEYS
            index = (idx0[..., :, None] + idx1[..., None, :]).reshape(b, n, HEADS, PK_TOPK * PK_TOPK)
            score = (scores[0][..., :, None] + scores[1][..., None, :]).reshape(b, n, HEADS, PK_TOPK * PK_TOPK)
            final_scores, pk_idx = jax.lax.top_k(score, FINAL_TOPK)
            final_indices = jnp.take_along_axis(index, pk_idx, axis=-1)
            final_scores = jax.nn.softmax(final_scores, axis=-1)
            return (final_scores, final_indices)
        b, n, d = x.shape
        q = (x @ Wq).reshape(b, n, HEADS, DIM) * DIM ** (-0.5)
        kv_scores, indices = _pk(x, Wq_pk, pk_keys)
        offsets = jnp.arange(HEADS, dtype=indices.dtype) * NUM_KV
        ind = indices + offsets[None, None, :, None]
        k = jnp.einsum('bnhk,bnhkd->bnhd', kv_scores, keys_table[ind])
        v = jnp.einsum('bnhk,bnhkd->bnhd', kv_scores, values_table[ind])
        sim = jnp.einsum('bihd,bjhd->bhij', q, k)
        neg = -jnp.finfo(sim.dtype).max
        causal = jnp.tril(jnp.ones((n, n), dtype=bool))
        sim = jnp.where(causal, sim, neg)
        attn = jax.nn.softmax(sim, axis=-1)
        out = jnp.einsum('bhij,bjhd->bhid', attn, v)
        out = out.transpose(0, 2, 1, 3).reshape(b, n, HEADS * DIM)
        return out @ Wo
    h = _L0_tok_ref(x, L0_tok_W, 4)
    h = h + _L0_attn_ref(_layernorm(h, axis=-1), L0_attn_Wq, L0_attn_bq, L0_attn_Wk, L0_attn_bk, L0_attn_Wv, L0_attn_bv)
    h = h + _L0_ffn_ref(_layernorm(h, axis=-1), L0_ffn_Wq_pk, L0_ffn_pk_keys, L0_ffn_Wq, L0_ffn_keys_table, L0_ffn_values_table, L0_ffn_Wo)
    return h

_drawn_inputs = setup_inputs


def setup_inputs(seed=0):
    import zlib

    import numpy as np

    out = dict(_drawn_inputs(seed))
    spreads = {}
    factors = {'L0_attn_Wq': 8.0,
     'L0_attn_bq': 55.234,
     'L0_attn_Wk': 8.0,
     'L0_attn_bk': 30.634,
     'L0_ffn_Wq_pk': 8.0,
     'L0_ffn_pk_keys': 8.0,
     'L0_ffn_Wq': 64.0,
     'L0_ffn_keys_table': 64.0,
     'L0_ffn_values_table': 8.0,
     'L0_ffn_Wo': 8.0}
    for name, (base, spread) in spreads.items():
        noise = np.random.default_rng([zlib.crc32(name.encode()), seed]).standard_normal(out[name].shape)
        drawn = base * np.exp(spread * noise) if base else spread * noise
        out[name] = jnp.asarray(drawn.astype(out[name].dtype))
    for name, factor in factors.items():
        out[name] = (out[name] * factor).astype(out[name].dtype)
    return out
```

```python
from contextlib import ExitStack

import concourse.bass as bass
import numpy as np
from concourse import mybir
from concourse.alu_op_type import AluOpType as ALU

F32 = mybir.dt.float32
U32 = mybir.dt.uint32
I32 = mybir.dt.int32
ACT = mybir.ActivationFunctionType
AX = mybir.AxisListType

P = 128
R, N, E, POOL = 32, 512, 64, 4
H = 8
HD = E // H
NB = N // P
NK, TOP, DK = 64, 16, 32
SIDES = 2
NKV = NK * NK
KV = 2 * E
EPS = 1e-5
LOWEST = -3.4028235e38
MASKED = -1e30
CELLS = [(0, 1, 16), (1, 1, 8), (2, 2, 5), (4, 4, 3), (8, 8, 1)]
NC_ = sum(ni * nj for _, ni, nj in CELLS)
ENGINES = 5


def build(nc, x, keysvals, w_tok, w_qkv, b_qkv, wqpk_t, pk_t, w_q, w_o, out):
    ctx = ExitStack()
    with ctx:
        def sb(name, shape, dt=F32):
            return ctx.enter_context(nc.sbuf_tensor(name, shape, dt))

        def sem(name):
            return ctx.enter_context(nc.semaphore(name))

        tokens = sb("tokens", [P, R, NB, E])
        gathered = sb("gathered", [P, H, TOP, KV])
        g_flat = gathered[:].rearrange("x h s d -> x (h s d)")
        pooled = g_flat[:, 0:8192].rearrange("x (r b e) -> x r b e", r=R, b=NB)
        qkv = g_flat[:, 8192:14336].rearrange("x (t h r d) -> x t h r d", t=3, h=H, r=R)
        normed = g_flat[:, 14336:16384].rearrange("x (r e) -> x r e", r=R)
        work = sb("work", [P, 12288])
        raw = work[:, 0:2048].rearrange("x (u c) -> x u c", u=2)
        raw_t = work[:, 2048:4096].rearrange("x (u c) -> x u c", u=2)
        shifted = work[:, 4096:6144].rearrange("x (u c) -> x u c", u=2)
        expd = work[:, 6144:8192].rearrange("x (u c) -> x u c", u=2)
        weighted = work[:, 8192:10240].rearrange("x (u c) -> x u c", u=2)
        q_t = work[:, 0:2048].rearrange("x (m c h) -> x m c h", m=2, c=P)
        context = work[:, 2048:3072].rearrange("x (f m e) -> x f m e", f=2, m=2)
        norm_t = work[:, 3072:4096].rearrange("x (u c) -> x u c", u=2)
        k_headmax = work[:, 4096:4352]
        diag_max = work[:, 4352:4864].rearrange("x (m f c) -> x m f c", m=2, f=2)
        squares = work[:, 4864:6912].rearrange("x (r e) -> x r e", r=R)
        qt = work[:, 0:2048].rearrange("x (g n) -> x g n", g=4)
        kt = work[:, 2048:4096].rearrange("x (g n) -> x g n", g=4)
        kv = work[:, 4096:8192].rearrange("x (b t h d) -> x b t h d", b=NB, t=2, h=H)
        probs = work[:, 8192:9216].rearrange("x (u c) -> x u c", u=2)
        probs_t = work[:, 9216:10240].rearrange("x (u c) -> x u c", u=2)
        sides = work[:, 10240:11264].rearrange("x (s h k) -> x s h k", s=SIDES, h=H)
        sides_rest = work[:, 11264:12288].rearrange("x (s h k) -> x s h k", s=SIDES, h=H)

        small = sb("small", [P, 1024])
        group_max = small[:, 0:512].rearrange("x (u c) -> x u c", u=2)
        group_den = small[:, 512:1024].rearrange("x (u c) -> x u c", u=2)
        ln_a = small[:, 512:544]
        ln_b = small[:, 544:576]
        max_t = small[:, 576:580].rearrange("x (m f) -> x m f", m=2)
        q_max = small[:, 584:592]
        q_sum = small[:, 592:600]
        k_rsum = small[:, 600:604]
        group_num = sb("group_num", [P, 2, 256])

        top = sb("top", [P, SIDES, H, TOP])
        top_at = sb("top_at", [P, SIDES, H, TOP], U32)
        code = sb("code", [P, SIDES, H, TOP])
        cand = sb("cand", [P, H, NC_])
        cand_code = sb("cand_code", [P, H, NC_])
        cand_rest = sb("cand_rest", [P, H, NC_])
        best = sb("best", [P, H, TOP])
        best_at = sb("best_at", [P, H, TOP], U32)
        best_atf = sb("best_atf", [P, H, TOP])
        onehot = sb("onehot", [P, TOP, NC_])
        best_code = sb("best_code", [P, H, TOP])
        rows = sb("rows", [P, 2, H * TOP], U32)
        weight_in = sb("weight_in", [P, H, TOP])
        weight_sum = sb("weight_sum", [P, H])
        weight = sb("weight", [P, 2, H, TOP])
        normed2 = sb("normed2", [P, NB, E])
        sq2 = sb("sq2", [P, NB, E])
        ln2 = sb("ln2", [P, 2, NB])
        norm2_t = sb("norm2_t", [E, N])
        neg_max = sb("neg_max", [P, 4])
        den = sb("den", [P, 2, H])
        rden = sb("rden", [P, H])
        attended = sb("attended", [P, H, E])
        attended_t = sb("attended_t", [P, 4, P])
        result = sb("result", [P, NB, E])

        w_tok2 = sb("w_tok2", [P, P])
        wqkv_s = sb("wqkv_s", [E, 3 * E])
        bqkv_s = sb("bqkv_s", [P, 3 * E])
        wqpk_s = sb("wqpk_s", [P, 4, E])
        pk_s = sb("pk_s", [P, 4, NK])
        w_side = sb("w_side", [E, SIDES * H * NK])
        wq_s = sb("wq_s", [E, H * E])
        wo_s = sb("wo_s", [P, 4, E])
        ident = sb("ident", [P, P])
        causal = sb("causal", [P, P])
        ones = sb("ones", [P, E])
        cell_i = sb("cell_i", [P, NC_], I32)
        cell_no = sb("cell_no", [P, NC_])
        head_i = sb("head_i", [P, H, TOP], I32)
        head_base = sb("head_base", [P, H, TOP])

        ps = ctx.enter_context(nc.psum_tensor("ps", [P, 8, 512], F32))
        SC, SIM, PT, O, MISC = 0, 2, 4, 6, 7

        weights_in = sem("weights_in")
        const_made = sem("const_made")
        const_cast = sem("const_cast")
        side_ps = sem("side_ps")
        side_sb = sem("side_sb")
        done_a = sem("done_a")
        done_b = sem("done_b")

        a_raw_in = [sem(f"a_raw_in{u}") for u in range(2)]
        a_raw_free = sem("a_raw_free")
        a_t_ps = sem("a_t_ps")
        a_t_sb = sem("a_t_sb")
        a_scores = sem("a_scores")
        a_shifted = sem("a_shifted")
        a_exp = sem("a_exp")
        a_weighted = sem("a_weighted")
        a_pooled = sem("a_pooled")

        b_var = sem("b_var")
        b_std = sem("b_std")
        b_normed = sem("b_normed")
        b_t_ps = sem("b_t_ps")
        b_t_sb = sem("b_t_sb")
        b_qkv_ps = sem("b_qkv_ps")
        b_qkv_sb = sem("b_qkv_sb")
        b_headmax = sem("b_headmax")
        b_headmax_t = sem("b_headmax_t")
        b_diag = sem("b_diag")
        b_kmax = sem("b_kmax")
        b_kshift = sem("b_kshift")
        b_kexp = sem("b_kexp")
        b_qshift = sem("b_qshift")
        b_qexp = sem("b_qexp")
        b_qnormed = sem("b_qnormed")
        b_ctx_ps = sem("b_ctx_ps")
        b_ctx_sb = sem("b_ctx_sb")
        b_qt_ps = sem("b_qt_ps")
        b_qt_sb = sem("b_qt_sb")
        b_out_ps = sem("b_out_ps")

        c_var = sem("c_var")
        c_std = sem("c_std")
        c_normed = sem("c_normed")
        c_t_ps = sem("c_t_ps")
        c_t_sb = sem("c_t_sb")
        c_q_ps = sem("c_q_ps")
        c_q_sb = sem("c_q_sb")
        c_side_ps = sem("c_side_ps")
        c_side_sb = sem("c_side_sb")
        c_side_used = sem("c_side_used")
        c_best = sem("c_best")
        c_wexp = sem("c_wexp")
        c_rows = sem("c_rows")
        c_landed = [sem(f"c_landed{h}") for h in range(H)]
        c_gather_used = sem("c_gather_used")
        c_kv = sem("c_kv")
        c_kt_ps = sem("c_kt_ps")
        c_kt_sb = sem("c_kt_sb")
        c_sim = sem("c_sim")
        c_max = sem("c_max")
        c_probs = sem("c_probs")
        c_pt_ps = sem("c_pt_ps")
        c_pt_sb = sem("c_pt_sb")
        c_o_ps = sem("c_o_ps")
        c_o_sb = sem("c_o_sb")
        c_ot_ps = sem("c_ot_ps")
        c_ot_sb = sem("c_ot_sb")
        c_y_ps = sem("c_y_ps")
        c_y_sb = sem("c_y_sb")
        c_result_free = sem("c_result_free")
        c_stored = sem("c_stored")

        block = ctx.enter_context(nc.Block())
        NW = 10

        @block.sync
        def _(sp):
            sp.wait_ge(const_made, 1)
            sp.dma_start(w_tok2[0:E, 0:E], w_tok).then_inc(weights_in, 16)
            sp.dma_start(w_tok2[E:P, E:P], w_tok).then_inc(weights_in, 16)
            sp.dma_start(wqkv_s[:], w_qkv).then_inc(weights_in, 16)
            sp.dma_start(bqkv_s[:], b_qkv.to_broadcast([P, 3 * E])).then_inc(weights_in, 16)
            sp.dma_start(wqpk_s[:], wqpk_t.rearrange("(a p) e -> p a e", p=P)).then_inc(weights_in, 16)
            sp.dma_start(pk_s[:], pk_t.rearrange("(a p) e -> p a e", p=P)).then_inc(weights_in, 16)
            sp.dma_start(wq_s[:], w_q).then_inc(weights_in, 16)
            sp.dma_start(wo_s[:], w_o.rearrange("(a p) e -> p a e", p=P)).then_inc(weights_in, 16)
            with sp.Fori(0, R // 2) as r2:
                for u in range(2):
                    sp.wait_ge(a_raw_free, r2 * 2 + (u + 1))
                    sp.dma_start(raw[:, u].rearrange("x (b c) -> x b c", b=NB),
                                 x[r2 * 2 + u, :, :].rearrange("(b p q) f -> p b (q f)", b=NB, p=P)
                                 ).then_inc(a_raw_in[u], 16)
            for _ in range(NB):
                sp.nop(nofuse=True).then_inc(c_result_free, 1)
            with sp.Fori(0, R) as r:
                for b in range(NB):
                    sp.wait_ge(c_y_sb, r * NB + (b + 1))
                    sp.dma_start(out[r, b * P:(b + 1) * P, :], result[:, b, :]).then_inc(c_stored, 16)
                    sp.wait_ge(c_stored, r * (16 * NB) + 16 * (b + 1))
                    sp.nop(nofuse=True).then_inc(c_result_free, 1)

        @block.gpsimd
        def _(pool):
            nc.gpsimd.memset(w_tok2[:], 0.0).then_inc(const_made, 1)
            nc.gpsimd.memset(ident[:], 0.0)
            nc.gpsimd.memset(causal[:], 0.0)
            nc.gpsimd.memset(ones[:], 1.0)
            nc.gpsimd.iota(cell_i[:], pattern=[[1, NC_]], base=0, channel_multiplier=0)
            nc.gpsimd.iota(head_i[:], pattern=[[NKV, H], [0, TOP]], base=0,
                           channel_multiplier=0).then_inc(const_made, 1)
            pool.wait_ge(const_made, 2)
            nc.gpsimd.affine_select(out=ident[:], in_=ident[:], compare_op=ALU.not_equal, fill=1.0, base=0,
                                    pattern=[[-1, P]], channel_multiplier=1)
            nc.gpsimd.affine_select(out=causal[:], in_=causal[:], compare_op=ALU.is_ge, fill=MASKED, base=0,
                                    pattern=[[-1, P]], channel_multiplier=1).then_inc(const_made, 1)
            with pool.Fori(0, R // 2) as r2:
                for u in range(2):
                    pool.wait_ge(a_exp, r2 * 2 + (u + 1))
                    pool.nop(nofuse=True)
                    nc.gpsimd.tensor_tensor(weighted[:, u], expd[:, u], raw[:, u], ALU.mult
                                            ).then_inc(a_weighted, 1)
            pool.wait_ge(done_b, 3)
            with pool.Fori(0, R * NB // 2) as t2:
                for u in range(2):
                    pool.wait_ge(c_rows, t2 * 2 + (u + 1))
                    pool.nop(nofuse=True)
                    for h in range(H):
                        pool.wait_ge(c_gather_used, t2 * (2 * H) + (u * H + h + 1))
                        pool.nop(nofuse=True)
                        for s in range(TOP):
                            at = h * TOP + s
                            pool.indirect_dma_start(
                                gathered[:, h, s, :], None, keysvals[:, :],
                                bass.IndirectOffsetOnAxis(ap=rows[:, u, at:at + 1], axis=0)
                            ).then_inc(c_landed[h], 16)

        @block.tensor
        def _(pe):
            pe.wait_ge(const_made, 3)
            pe.wait_ge(weights_in, 16 * 8)
            for a in range(SIDES * H * DK // P):
                for g in range(P // DK):
                    lo = g * DK
                    last = nc.tensor.matmul(ps[0:E, g, a * NK:(a + 1) * NK], wqpk_s[lo:lo + DK, a, :],
                                            pk_s[lo:lo + DK, a, :], start=True, stop=True)
            last.then_inc(side_ps, 1)
            pe.wait_ge(side_sb, 1)

            with pe.Fori(0, R // 2) as r2:
                for u in range(2):
                    pe.wait_ge(a_raw_in[u], r2 * 16 + 16)
                    pe.nop(nofuse=True)
                    for j in range(8):
                        last = nc.tensor.transpose(ps[:, 4 * u + j // 4, (j % 4) * P:(j % 4 + 1) * P],
                                                   raw[:, u, j * P:(j + 1) * P], ident[:])
                    last.then_inc(a_t_ps, 1)
                    pe.wait_ge(a_t_sb, r2 * 2 + (u + 1))
                    pe.nop(nofuse=True)
                    pe.wait_ge(a_shifted, r2 * 2 + (u + 1))
                    pe.nop(nofuse=True)
                    for j in range(8):
                        last = nc.tensor.matmul(ps[:, 4 * u + 2 + j // 4, (j % 4) * P:(j % 4 + 1) * P],
                                                raw_t[:, u, j * P:(j + 1) * P], w_tok2[:],
                                                start=True, stop=True)
                    last.then_inc(a_scores, 1)

            pe.wait_ge(done_a, 1)
            with pe.Fori(0, NB) as cb:
                pe.wait_ge(b_normed, cb + 1)
                pe.nop(nofuse=True)
                for g in range(8):
                    if g >= 2:
                        pe.wait_ge(b_t_sb, cb * 8 + (g - 1))
                        pe.nop(nofuse=True)
                    for i in range(4):
                        last = nc.tensor.transpose(ps[0:E, g % 2, i * P:(i + 1) * P], normed[:, 4 * g + i, :],
                                                   ident[:])
                    last.then_inc(b_t_ps, 1)
                    pe.wait_ge(b_t_sb, cb * 8 + (g + 1))
                    pe.nop(nofuse=True)
                    if g >= 2:
                        pe.wait_ge(b_qkv_sb, cb * 8 + (g - 1))
                        pe.nop(nofuse=True)
                    for i in range(4):
                        o = ps[:, 2 + 2 * (g % 2) + i // 2, (i % 2) * 192:(i % 2 + 1) * 192]
                        last = nc.tensor.matmul(o, norm_t[0:E, g % 2, i * P:(i + 1) * P], wqkv_s[:],
                                                start=True, stop=True)
                    last.then_inc(b_qkv_ps, 1)
                pe.wait_ge(b_headmax, cb + 1)
                pe.nop(nofuse=True)
                for m in range(2):
                    last = nc.tensor.transpose(ps[:, 6, m * P:(m + 1) * P], k_headmax[:, m * P:(m + 1) * P],
                                               ident[:])
                last.then_inc(b_headmax_t, 1)
                pe.wait_ge(b_diag, cb + 1)
                pe.nop(nofuse=True)
                for f in range(2):
                    for m in range(2):
                        last = nc.tensor.matmul(ps[f * E:(f + 1) * E, 7, m * P:(m + 1) * P], ones[:],
                                                diag_max[:, m, f, :], start=True, stop=True)
                last.then_inc(b_kmax, 1)
                pe.wait_ge(b_kexp, cb + 1)
                pe.nop(nofuse=True)
                for f in range(2):
                    half = slice(f * E, (f + 1) * E)
                    for m in range(2):
                        for h in range(H):
                            keys = qkv[half, 1, h, 16 * m:16 * (m + 1), :].rearrange("x r d -> x (r d)")
                            nc.tensor.matmul(ps[:, f, m * 256:(m + 1) * 256], keys,
                                             qkv[half, 2, h].rearrange("x r d -> x (r d)"),
                                             start=(h == 0), stop=(h == H - 1))
                        for h in range(H):
                            keys = qkv[half, 1, h, 16 * m:16 * (m + 1), :].rearrange("x r d -> x (r d)")
                            last = nc.tensor.matmul(ps[:, [2, 7][f], m:m + 1], keys, ones[half, 0:1],
                                                    start=(h == 0), stop=(h == H - 1))
                last.then_inc(b_ctx_ps, 1)
                pe.wait_ge(b_qnormed, cb + 1)
                pe.nop(nofuse=True)
                for m in range(2):
                    for hh in range(2):
                        for i in range(4):
                            h = 4 * hh + i
                            last = nc.tensor.transpose(ps[:, 3 + 2 * m + hh, i * P:(i + 1) * P],
                                                       qkv[:, 0, h, 16 * m:16 * (m + 1), :].rearrange("x r d -> x (r d)"),
                                                       ident[:])
                        last.then_inc(b_qt_ps, 1)
                pe.wait_ge(b_qt_sb, cb * 4 + 4)
                pe.nop(nofuse=True)
                pe.wait_ge(b_ctx_sb, cb + 1)
                pe.nop(nofuse=True)
                for f in range(2):
                    for b in range(NB):
                        bank = [[0, 1], [2, 7]][f][b // 2]
                        for m in range(2):
                            lo = f * E + 16 * b
                            last = nc.tensor.matmul(ps[:, bank, (b % 2) * 256:(b % 2 + 1) * 256],
                                                    q_t[:, m, lo:lo + 16, :].rearrange("x c h -> x (c h)"),
                                                    context[:, f, m, :], start=(m == 0), stop=(m == 1))
                last.then_inc(b_out_ps, 1)
            pe.wait_ge(done_b, 3)

            def transpose_tokens(k):
                pe.wait_ge(c_normed, k + 1)
                pe.nop(nofuse=True)
                for b in range(NB):
                    last = nc.tensor.transpose(ps[0:E, MISC, b * P:(b + 1) * P], normed2[:, b, :], ident[:])
                last.then_inc(c_t_ps, 1)
                pe.wait_ge(c_t_sb, k + 1)
                pe.nop(nofuse=True)

            def score_sides(k, b):
                pe.wait_ge(c_side_sb, k * NB + (b + 1))
                pe.nop(nofuse=True)
                for s in range(SIDES):
                    last = nc.tensor.matmul(ps[:, SC + s, :], norm2_t[:, b * P:(b + 1) * P],
                                            w_side[:, s * 512:(s + 1) * 512], start=True, stop=True)
                last.then_inc(c_side_ps, 1)

            def project_queries(k):
                for g in range(4):
                    if g >= 2:
                        pe.wait_ge(c_q_sb, k * 4 + (g - 1))
                        pe.nop(nofuse=True)
                    nc.tensor.matmul(ps[:, SIM + g % 2, :], wq_s[:, g * P:(g + 1) * P], norm2_t[:],
                                     start=True, stop=True).then_inc(c_q_ps, 1)

            def transpose_keys(k, b):
                pe.wait_ge(c_kv, k * NB + (b + 1))
                pe.nop(nofuse=True)
                for g in range(4):
                    last = nc.tensor.transpose(ps[:, MISC, g * P:(g + 1) * P], kv[:, b, 0, 2 * g:2 * g + 2, :].rearrange("x h d -> x (h d)"),
                                               ident[:])
                last.then_inc(c_kt_ps, 1)
                pe.wait_ge(c_kt_sb, k * NB + (b + 1))
                pe.nop(nofuse=True)

            def attention(k):
                steps = [(b, h) for b in range(NB) for h in range(H)]
                n = len(steps)
                pe.wait_ge(c_q_sb, k * 4 + 4)
                pe.nop(nofuse=True)

                def similarities(s):
                    b, h = steps[s]
                    half = slice((h % 2) * E, (h % 2 + 1) * E)
                    w = (b + 1) * P
                    if s >= 2:
                        pe.wait_ge(c_probs, k * n + (s - 1))
                        pe.nop(nofuse=True)
                    nc.tensor.matmul(ps[:, SIM + s % 2, 0:w], qt[half, h // 2, b * P:w], kt[half, h // 2, 0:w],
                                     start=True, stop=False)
                    nc.tensor.matmul(ps[:, SIM + s % 2, b * P:w], ident[:], causal[:],
                                     start=False, stop=True).then_inc(c_sim, 1)

                def transpose_probs(s):
                    b, h = steps[s]
                    pe.wait_ge(c_probs, k * n + (s + 1))
                    pe.nop(nofuse=True)
                    if s >= 2:
                        pe.wait_ge(c_pt_sb, k * n + (s - 1))
                        pe.nop(nofuse=True)
                    for j in range(b + 1):
                        last = nc.tensor.transpose(ps[:, PT + s % 2, j * P:(j + 1) * P],
                                                   probs[:, s % 2, j * P:(j + 1) * P], ident[:])
                    last.then_inc(c_pt_ps, 1)

                def attend(s):
                    b, h = steps[s]
                    pe.wait_ge(c_pt_sb, k * n + (s + 1))
                    pe.nop(nofuse=True)
                    if h == 0 and b > 0:
                        pe.wait_ge(c_o_sb, k * NB + b)
                        pe.nop(nofuse=True)
                    for j in range(b + 1):
                        last = nc.tensor.matmul(ps[:, O, h * E:(h + 1) * E], probs_t[:, s % 2, j * P:(j + 1) * P],
                                                kv[:, j, 1, h, :], start=(j == 0), stop=(j == b))
                    if h == H - 1:
                        last.then_inc(c_o_ps, 1)

                def project(b, part):
                    if part == 0:
                        pe.wait_ge(c_o_sb, k * NB + (b + 1))
                        pe.nop(nofuse=True)
                        for g in range(4):
                            last = nc.tensor.transpose(
                                ps[:, MISC, g * P:(g + 1) * P],
                                attended[:, 2 * g:2 * g + 2, :].rearrange("x h d -> x (h d)"), ident[:])
                        last.then_inc(c_ot_ps, 1)
                    else:
                        pe.wait_ge(c_ot_sb, k * NB + (b + 1))
                        pe.nop(nofuse=True)
                        for g in range(4):
                            last = nc.tensor.matmul(ps[:, MISC, 0:E], attended_t[:, g, :], wo_s[:, g, :],
                                                    start=(g == 0), stop=(g == 3))
                        last.then_inc(c_y_ps, 1)

                for s in range(n + 5):
                    if s < n:
                        similarities(s)
                    if 1 <= s <= n:
                        transpose_probs(s - 1)
                    if 2 <= s <= n + 1:
                        attend(s - 2)
                    if s >= H + 3 and (s - 3) % H == 0:
                        project((s - 3) // H - 1, 0)
                    if s >= H + 4 and (s - 4) % H == 0:
                        project((s - 4) // H - 1, 1)
                pe.wait_ge(c_y_sb, k * NB + NB)
                pe.nop(nofuse=True)

            def row(k, more):
                project_queries(k)
                score_sides(k, 1)
                transpose_keys(k, 0)
                score_sides(k, 2)
                transpose_keys(k, 1)
                score_sides(k, 3)
                transpose_keys(k, 2)
                if more:
                    transpose_tokens(k + 1)
                    score_sides(k + 1, 0)
                transpose_keys(k, 3)
                attention(k)

            transpose_tokens(0)
            score_sides(0, 0)
            with pe.Fori(0, R - 1) as k:
                row(k, True)
            row(R - 1, False)

        @block.scalar
        def _(act):
            act.wait_ge(side_ps, 1)
            nc.scalar.copy(w_side[:].rearrange("x (a g k) -> x a g k", a=4, g=4),
                           ps[0:E, 0:4, 0:4 * NK].rearrange("x g (a k) -> x a g k", a=4)).then_inc(side_sb, 1)

            with act.Fori(0, R // 2) as r2:
                for u in range(2):
                    act.wait_ge(a_t_ps, r2 * 2 + (u + 1))
                    act.nop(nofuse=True)
                    nc.scalar.copy(raw_t[:, u], ps[:, 4 * u:4 * u + 2, :].rearrange("x s c -> x (s c)")
                                   ).then_inc(a_t_sb, 1)
                for u in range(2):
                    act.wait_ge(a_shifted, r2 * 2 + (u + 3))
                    act.nop(nofuse=True)
                    nc.scalar.activation(expd[:, u], shifted[:, u], ACT.Exp).then_inc(a_exp, 1)

            act.wait_ge(done_a, 1)
            with act.Fori(0, NB) as cb:
                act.wait_ge(b_var, cb + 1)
                act.nop(nofuse=True)
                nc.scalar.activation(ln_b, ln_a, ACT.Sqrt).then_inc(b_std, 1)
                for g in range(8):
                    act.wait_ge(b_t_ps, cb * 8 + (g + 1))
                    act.nop(nofuse=True)
                    nc.scalar.copy(norm_t[0:E, g % 2, :], ps[0:E, g % 2, :]).then_inc(b_t_sb, 1)
                act.wait_ge(b_kshift, cb + 1)
                act.nop(nofuse=True)
                nc.scalar.activation(qkv[:, 1], qkv[:, 1], ACT.Exp).then_inc(b_kexp, 1)
                act.wait_ge(b_qshift, cb + 1)
                act.nop(nofuse=True)
                nc.scalar.activation(qkv[:, 0], qkv[:, 0], ACT.Exp).then_inc(b_qexp, 1)
                for m in range(2):
                    for hh in range(2):
                        act.wait_ge(b_qt_ps, cb * 4 + (2 * m + hh + 1))
                        act.nop(nofuse=True)
                        nc.scalar.copy(q_t[:, m, :, 4 * hh:4 * hh + 4].rearrange("x c h -> x h c"),
                                       ps[:, 3 + 2 * m + hh, :].rearrange("x (h c) -> x h c", h=4)
                                       ).then_inc(b_qt_sb, 1)

            act.wait_ge(done_b, 3)
            nc.scalar.nop(nofuse=True).then_inc(c_side_sb, 1)

            def norm_and_transpose(k):
                act.wait_ge(c_var, k + 1)
                act.nop(nofuse=True)
                nc.scalar.activation(ln2[:, 1], ln2[:, 0], ACT.Sqrt).then_inc(c_std, 1)
                act.wait_ge(c_t_ps, k + 1)
                act.nop(nofuse=True)
                nc.scalar.copy(norm2_t[:], ps[0:E, MISC, :]).then_inc(c_t_sb, 1)

            def score_sides(k, b):
                act.wait_ge(c_side_ps, k * NB + (b + 1))
                act.nop(nofuse=True)
                act.wait_ge(c_side_used, k * NB + (b + 1))
                act.nop(nofuse=True)
                nc.scalar.copy(sides[:].rearrange("x s h k -> x (s h k)"),
                               ps[:, SC:SC + 2, :].rearrange("x s c -> x (s c)")).then_inc(c_side_sb, 1)

            def weights(k, b):
                act.wait_ge(c_best, k * NB + (b + 1))
                act.nop(nofuse=True)
                nc.scalar.activation(weight_in[:], weight_in[:], ACT.Exp).then_inc(c_wexp, 1)

            def project_queries(k):
                for g in range(4):
                    act.wait_ge(c_q_ps, k * 4 + (g + 1))
                    act.nop(nofuse=True)
                    nc.scalar.mul(qt[:, g, :], ps[:, SIM + g % 2, :], float(E) ** -0.5).then_inc(c_q_sb, 1)

            def transpose_keys(k, b):
                act.wait_ge(c_kt_ps, k * NB + (b + 1))
                act.nop(nofuse=True)
                nc.scalar.copy(kt[:, :, b * P:(b + 1) * P], ps[:, MISC, :].rearrange("x (g c) -> x g c", g=4)
                               ).then_inc(c_kt_sb, 1)

            def attention(k):
                steps = [(b, h) for b in range(NB) for h in range(H)]
                n = len(steps)
                for s in range(n + 5):
                    if s < n:
                        b, h = steps[s]
                        w = (b + 1) * P
                        act.wait_ge(c_max, k * n + (s + 1))
                        act.nop(nofuse=True)
                        if s >= 2:
                            act.wait_ge(c_pt_ps, k * n + (s - 1))
                            act.nop(nofuse=True)
                        nc.scalar.activation(probs[:, s % 2, 0:w], ps[:, SIM + s % 2, 0:w], ACT.Exp,
                                             bias=neg_max[:, s % 4:s % 4 + 1],
                                             accum_out=den[:, b % 2, h:h + 1]).then_inc(c_probs, 1)
                    if 1 <= s <= n:
                        b, h = steps[s - 1]
                        w = (b + 1) * P
                        act.wait_ge(c_pt_ps, k * n + s)
                        act.nop(nofuse=True)
                        nc.scalar.copy(probs_t[:, (s - 1) % 2, 0:w], ps[:, PT + (s - 1) % 2, 0:w]
                                       ).then_inc(c_pt_sb, 1)
                    if s >= H + 3 and (s - 3) % H == 0:
                        b = (s - 3) // H - 1
                        act.wait_ge(c_ot_ps, k * NB + (b + 1))
                        act.nop(nofuse=True)
                        nc.scalar.copy(attended_t[:].rearrange("x g c -> x (g c)"), ps[:, MISC, :]
                                       ).then_inc(c_ot_sb, 1)

            def row(k, more):
                project_queries(k)
                score_sides(k, 1)
                weights(k, 1)
                transpose_keys(k, 0)
                score_sides(k, 2)
                weights(k, 2)
                transpose_keys(k, 1)
                score_sides(k, 3)
                weights(k, 3)
                transpose_keys(k, 2)
                if more:
                    norm_and_transpose(k + 1)
                    score_sides(k + 1, 0)
                    weights(k + 1, 0)
                transpose_keys(k, 3)
                attention(k)

            norm_and_transpose(0)
            score_sides(0, 0)
            weights(0, 0)
            with act.Fori(0, R - 1) as k:
                row(k, True)
            row(R - 1, False)

        @block.vector
        def _(dve):
            tt, ts, red = nc.vector.tensor_tensor, nc.vector.tensor_scalar, nc.vector.tensor_reduce
            drain = nc.vector.drain
            dve.wait_ge(const_made, 3)
            nc.vector.tensor_copy(cell_no[:], cell_i[:])
            nc.vector.tensor_copy(head_base[:], head_i[:])
            drain().then_inc(a_raw_free, 2)
            drain().then_inc(a_shifted, 2)

            with dve.Fori(0, R // 2) as r2:
                for u in range(2):
                    scores = ps[:, 4 * u + 2:4 * u + 4, :].rearrange("x s (b c) -> x (s b) c", c=256)
                    dve.wait_ge(a_scores, r2 * 2 + (u + 1))
                    dve.nop(nofuse=True)
                    gmax = group_max[:, u].rearrange("x (b g) -> x b g", b=NB)
                    red(gmax, scores.rearrange("x b (q g) -> x b g q", q=POOL), AX.X, ALU.max)
                    drain()
                    tt(shifted[:, u].rearrange("x (b q g) -> x b q g", b=NB, q=POOL),
                       scores.rearrange("x b (q g) -> x b q g", q=POOL),
                       gmax.unsqueeze(2).to_broadcast([P, NB, POOL, E]), ALU.subtract).then_inc(a_shifted, 1)
                for u in range(2):
                    dve.wait_ge(a_exp, r2 * 2 + (u + 1))
                    dve.nop(nofuse=True)
                    gden = group_den[:, u].rearrange("x (b g) -> x b g", b=NB)
                    gnum = group_num[:, u].rearrange("x (b g) -> x b g", b=NB)
                    red(gden, expd[:, u].rearrange("x (b q g) -> x b g q", b=NB, q=POOL), AX.X, ALU.add)
                    drain()
                    nc.vector.reciprocal(gden, gden)
                    dve.wait_ge(a_weighted, r2 * 2 + (u + 1))
                    dve.nop(nofuse=True)
                    red(gnum, weighted[:, u].rearrange("x (b q g) -> x b g q", b=NB, q=POOL), AX.X, ALU.add
                        ).then_inc(a_raw_free, 1)
                    drain()
                    tt(pooled[:, r2 * 2 + u, :, :], gnum, gden, ALU.mult)
            drain().then_inc(done_a, 1)

            def wide(v, shape, axis):
                return v.unsqueeze(axis).to_broadcast(shape)

            with dve.Fori(0, NB) as cb:
                src = pooled[:, :, bass.ds(cb, 1), :].rearrange("x r o e -> x r (o e)")
                red(ln_a, src, AX.X, ALU.add)
                drain()
                ts(ln_a, ln_a, 1.0 / E, None, ALU.mult)
                drain()
                tt(normed[:], src, wide(ln_a, [P, R, E], 2), ALU.subtract)
                drain()
                tt(squares, normed[:], normed[:], ALU.mult)
                drain()
                red(ln_a, squares, AX.X, ALU.add)
                drain()
                ts(ln_a, ln_a, 1.0 / E, EPS, ALU.mult, ALU.add).then_inc(b_var, 1)
                dve.wait_ge(b_std, cb + 1)
                dve.nop(nofuse=True)
                nc.vector.reciprocal(ln_b, ln_b)
                drain()
                tt(normed[:], normed[:], wide(ln_b, [P, R, E], 2), ALU.mult).then_inc(b_normed, 1)
                for g in range(8):
                    dve.wait_ge(b_qkv_ps, cb * 8 + (g + 1))
                    dve.nop(nofuse=True)
                    bank = 2 + 2 * (g % 2)
                    for t in range(3):
                        for s in range(2):
                            r0 = 4 * g + 2 * s
                            last = tt(qkv[:, t, :, r0:r0 + 2, :].rearrange("x h r d -> x r h d"),
                                      ps[:, bank + s, 0:384].rearrange("x (i t h d) -> x i t h d", i=2, t=3, h=H)
                                      [:, :, t],
                                      bqkv_s[:, t * E:(t + 1) * E].rearrange("x (h d) -> x h d", h=H)
                                      .unsqueeze(1).to_broadcast([P, 2, H, HD]), ALU.add)
                    last.then_inc(b_qkv_sb, 1)
                drain()
                keys = qkv[:, 1].rearrange("x h r d -> x h (r d)")
                red(k_headmax, qkv[:, 1].rearrange("x h r d -> x (r d) h"), AX.X, ALU.max).then_inc(b_headmax, 1)
                queries = qkv[:, 0].rearrange("x h r d -> x h (r d)")
                red(q_max, queries, AX.X, ALU.max)
                drain()
                tt(queries, queries, wide(q_max, [P, H, R * HD], 2),
                   ALU.subtract).then_inc(b_qshift, 1)
                dve.wait_ge(b_headmax_t, cb + 1)
                dve.nop(nofuse=True)
                red(max_t, ps[:, 6, 0:256].rearrange("x (m f c) -> x m f c", m=2, f=2), AX.X, ALU.max)
                drain()
                tt(diag_max.rearrange("x m f c -> x (m f) c"), wide(ident[:], [P, 4, P], 1),
                   wide(max_t.rearrange("x m f -> x (m f)"), [P, 4, P], 2), ALU.mult).then_inc(b_diag, 1)
                dve.wait_ge(b_kmax, cb + 1)
                dve.nop(nofuse=True)
                tt(keys, keys, wide(ps[:, 7, 0:256], [P, H, R * HD], 1),
                   ALU.subtract).then_inc(b_kshift, 1)
                dve.wait_ge(b_qexp, cb + 1)
                dve.nop(nofuse=True)
                red(q_sum, queries, AX.X, ALU.add)
                drain()
                nc.vector.reciprocal(q_sum, q_sum)
                drain()
                tt(queries, queries, wide(q_sum, [P, H, R * HD], 2),
                   ALU.mult).then_inc(b_qnormed, 1)
                dve.wait_ge(b_ctx_ps, cb + 1)
                dve.nop(nofuse=True)
                for f in range(2):
                    nc.vector.reciprocal(k_rsum[:, 2 * f:2 * f + 2], ps[:, [2, 7][f], 0:2])
                drain()
                for f in range(2):
                    for m in range(2):
                        last = ts(context[:, f, m, :], ps[:, f, m * 256:(m + 1) * 256],
                                  k_rsum[:, 2 * f + m:2 * f + m + 1], float(R * HD) ** 0.5, ALU.mult, ALU.mult)
                last.then_inc(b_ctx_sb, 1)
                dve.wait_ge(b_out_ps, cb + 1)
                dve.nop(nofuse=True)
                for f in range(2):
                    for b in range(NB):
                        bank = [[0, 1], [2, 7]][f][b // 2]
                        lo = cb * (2 * HD) + f * HD
                        tt(tokens[:, :, b, bass.ds(lo, HD)],
                           ps[:, bank, (b % 2) * 256:(b % 2 + 1) * 256].rearrange("x (r d) -> x r d", r=R),
                           pooled[:, :, b, bass.ds(lo, HD)], ALU.add)
            drain().then_inc(done_b, 3)
            drain().then_inc(c_gather_used, H)
            drain().then_inc(c_side_used, 1)

            def layer_norm(k):
                src = tokens[:, bass.ds(k, 1), :, :].rearrange("x o b e -> x (o b) e")
                mean = ln2[:, 0]
                red(mean, src, AX.X, ALU.add)
                drain()
                ts(mean, mean, 1.0 / E, None, ALU.mult)
                drain()
                tt(normed2[:], src, wide(mean, [P, NB, E], 2), ALU.subtract)
                drain()
                tt(sq2[:], normed2[:], normed2[:], ALU.mult)
                drain()
                red(mean, sq2[:], AX.X, ALU.add)
                drain()
                ts(mean, mean, 1.0 / E, EPS, ALU.mult, ALU.add).then_inc(c_var, 1)
                dve.wait_ge(c_std, k + 1)
                dve.nop(nofuse=True)
                nc.vector.reciprocal(ln2[:, 1], ln2[:, 1])
                drain()
                tt(normed2[:], normed2[:], wide(ln2[:, 1], [P, NB, E], 2), ALU.mult).then_inc(c_normed, 1)

            def top_16(values, rest, best8, best8_at):
                lists = range(len(values))
                for i in lists:
                    nc.vector.max(best8[i][:, 0:8], values[i])
                drain()
                for i in lists:
                    nc.vector.match_replace(out=rest[i], in_to_replace=best8[i][:, 0:8], in_values=values[i],
                                            imm_value=LOWEST)
                    nc.vector.max_index(best8_at[i][:, 0:8], best8[i][:, 0:8], values[i])
                drain()
                for i in lists:
                    nc.vector.max(best8[i][:, 8:16], rest[i])
                drain()
                for i in lists:
                    last = nc.vector.max_index(best8_at[i][:, 8:16], best8[i][:, 8:16], rest[i])
                drain()
                return last

            def choose(k, b):
                u = b % 2
                dve.wait_ge(c_side_sb, k * NB + (b + 2))
                dve.nop(nofuse=True)
                sh = [(s, h) for s in range(SIDES) for h in range(H)]
                top_16([sides[:, s, h, :] for s, h in sh], [sides_rest[:, s, h, :] for s, h in sh],
                       [top[:, s, h, :] for s, h in sh], [top_at[:, s, h, :] for s, h in sh])
                nc.vector.tensor_copy(code[:], top_at[:]).then_inc(c_side_used, 1)
                drain()
                ts(code[:, 1], code[:, 1], float(NK), None, ALU.mult)
                tt(code[:, 0], code[:, 0], head_base[:], ALU.add)
                drain()
                at = 0
                for i0, ni, nj in CELLS:
                    for out_, in_ in ((cand, top), (cand_code, code)):
                        tt(out_[:, :, at:at + ni * nj].rearrange("x h (i j) -> x h i j", i=ni),
                           in_[:, 0, :, i0:i0 + ni].unsqueeze(3).to_broadcast([P, H, ni, nj]),
                           in_[:, 1, :, 0:nj].unsqueeze(2).to_broadcast([P, H, ni, nj]), ALU.add)
                    at += ni * nj
                drain()
                top_16([cand[:, h, :] for h in range(H)], [cand_rest[:, h, :] for h in range(H)],
                       [best[:, h, :] for h in range(H)], [best_at[:, h, :] for h in range(H)])
                tt(weight_in[:], best[:], best[:, :, 0:1].to_broadcast([P, H, TOP]),
                   ALU.subtract).then_inc(c_best, 1)
                nc.vector.tensor_copy(best_atf[:], best_at[:])
                drain()
                for h in range(H):
                    tt(onehot[:], best_atf[:, h, :].unsqueeze(2).to_broadcast([P, TOP, NC_]),
                       wide(cell_no[:], [P, TOP, NC_], 1), ALU.is_equal)
                    drain()
                    tt(onehot[:], onehot[:], wide(cand_code[:, h, :], [P, TOP, NC_], 1), ALU.mult)
                    drain()
                    red(best_code[:, h, :], onehot[:], AX.X, ALU.add)
                    drain()
                nc.vector.tensor_copy(rows[:, u], best_code[:].rearrange("x h s -> x (h s)")
                                      ).then_inc(c_rows, 1)
                dve.wait_ge(c_wexp, k * NB + (b + 1))
                dve.nop(nofuse=True)
                red(weight_sum[:], weight_in[:], AX.X, ALU.add)
                drain()
                nc.vector.reciprocal(weight_sum[:], weight_sum[:])
                drain()
                tt(weight[:, u], weight_in[:], wide(weight_sum[:], [P, H, TOP], 2), ALU.mult)
                drain()

            def mix(k, b):
                for h in range(H):
                    dve.wait_ge(c_landed[h], k * (NB * TOP * 16) + (b + 1) * TOP * 16)
                    dve.nop(nofuse=True)
                    tt(gathered[:, h], gathered[:, h], wide(weight[:, b % 2, h, :], [P, TOP, KV], 2), ALU.mult)
                    drain()
                    last = red(kv[:, b, :, h, :], gathered[:, h].rearrange("x s (t d) -> x t d s", t=2), AX.X, ALU.add)
                    if h < H - 1:
                        last.then_inc(c_gather_used, 1)
                last.then_inc(c_kv, 1)
                drain().then_inc(c_gather_used, 1)

            def attention(k):
                steps = [(b, h) for b in range(NB) for h in range(H)]
                n = len(steps)
                for s in range(n + 5):
                    if s < n:
                        b, h = steps[s]
                        dve.wait_ge(c_sim, k * n + (s + 1))
                        dve.nop(nofuse=True)
                        red(neg_max[:, s % 4:s % 4 + 1], ps[:, SIM + s % 2, 0:(b + 1) * P], AX.X, ALU.max,
                            negate=True).then_inc(c_max, 1)
                    if s >= H + 2 and (s - 2) % H == 0:
                        b = (s - 2) // H - 1
                        dve.wait_ge(c_o_ps, k * NB + (b + 1))
                        dve.nop(nofuse=True)
                        nc.vector.reciprocal(rden[:], den[:, b % 2, :])
                        drain()
                        tt(attended[:], ps[:, O, :].rearrange("x (h d) -> x h d", h=H),
                           wide(rden[:], [P, H, E], 2), ALU.mult).then_inc(c_o_sb, 1)
                    if s >= H + 4 and (s - 4) % H == 0:
                        b = (s - 4) // H - 1
                        dve.wait_ge(c_y_ps, k * NB + (b + 1))
                        dve.nop(nofuse=True)
                        dve.wait_ge(c_result_free, k * NB + (b + 1))
                        dve.nop(nofuse=True)
                        tt(result[:, b, :], ps[:, MISC, 0:E],
                           tokens[:, bass.ds(k, 1), b, :].rearrange("x o e -> x (o e)"), ALU.add
                           ).then_inc(c_y_sb, 1)

            def row(k, more):
                choose(k, 1)
                mix(k, 0)
                choose(k, 2)
                mix(k, 1)
                choose(k, 3)
                mix(k, 2)
                if more:
                    layer_norm(k + 1)
                    choose(k + 1, 0)
                mix(k, 3)
                attention(k)

            layer_norm(0)
            choose(0, 0)
            with dve.Fori(0, R - 1) as k:
                row(k, True)
            row(R - 1, False)


def kernel(**inputs):
    import concourse.bacc as bacc
    from concourse.bass_utils import run_bass_kernel_spmd

    def arr(name):
        return np.asarray(inputs[name])

    arrays = {
        "x": arr("x"),
        "keysvals": np.concatenate([arr("L0_ffn_keys_table"), arr("L0_ffn_values_table")], axis=1),
        "w_tok": arr("L0_tok_W"),
        "w_qkv": np.concatenate([arr("L0_attn_Wq").T, arr("L0_attn_Wk").T, arr("L0_attn_Wv").T], axis=1),
        "b_qkv": np.concatenate([arr("L0_attn_bq"), arr("L0_attn_bk"), arr("L0_attn_bv")])[None, :],
        "wqpk_t": arr("L0_ffn_Wq_pk").T,
        "pk_t": arr("L0_ffn_pk_keys").transpose(0, 2, 3, 1).reshape(SIDES * H * DK, NK),
        "w_q": arr("L0_ffn_Wq"),
        "w_o": arr("L0_ffn_Wo"),
    }
    arrays = {n: np.ascontiguousarray(a) for n, a in arrays.items()}
    nc = bacc.Bacc("TRN2", target_bir_lowering=False, num_devices=1)
    args = [nc.dram_tensor(n, a.shape, F32, kind="ExternalInput").ap() for n, a in arrays.items()]
    out = nc.dram_tensor("out", (R, N, E), F32, kind="ExternalOutput").ap()
    build(nc, *args, out)
    return run_bass_kernel_spmd(nc, [arrays], core_ids=[0]).results[0]["out"]
```

```python
from contextlib import ExitStack

import concourse.bass as bass
import numpy as np
from concourse import mybir
from concourse.alu_op_type import AluOpType as ALU

F32 = mybir.dt.float32
U32 = mybir.dt.uint32
I32 = mybir.dt.int32
ACT = mybir.ActivationFunctionType
AX = mybir.AxisListType

P = 128
R, N, E, POOL = 32, 512, 64, 4
H = 8
HD = E // H
NB = N // P
NK, TOP, DK = 64, 16, 32
SIDES = 2
NKV = NK * NK
KV = 2 * E
EPS = 1e-5
LOWEST = -3.4028235e38
MASKED = -1e30
D, G = 4, 4
CH = NKV // P
PIECE = 8
STEPS = D * CH
QUARTER = STEPS // NB
SLACK = 2.0 ** -23
SUM_ERROR = 0.25
SUM_LIMIT = 2.5e5
BF16 = mybir.dt.bfloat16
U16 = mybir.dt.uint16
CELLS = [(0, 1, 16), (1, 1, 8), (2, 2, 5), (4, 4, 3), (8, 8, 1)]
NC_ = sum(ni * nj for _, ni, nj in CELLS)
READERS = 4


def build(nc, x, keysvals, tables, w_tok, w_qkv, b_qkv, wqpk_t, pk_t, w_q, w_o, kept, out):
    ctx = ExitStack()
    with ctx:
        def sb(name, shape, dt=F32):
            return ctx.enter_context(nc.sbuf_tensor(name, shape, dt))

        def sem(name):
            return ctx.enter_context(nc.semaphore(name))

        arena = sb("arena", [P, 8192])
        tokens = arena[:].rearrange("x (r b e) -> x r b e", r=R, b=NB)
        r_norm_t = arena[0:E, 0:N]
        parts = arena[:, 0:3072].bitcast(BF16).rearrange("x (h t n) -> x h t n", h=D, t=3)
        table = arena[:, 3072:5120].rearrange("x (u c d) -> x u c d", u=2, c=PIECE)
        expo = arena[:, 5120:6656].rearrange("x (u n) -> x u n", u=3)
        dense_w = arena[:, 6656:8192].rearrange("x (u n) -> x u n", u=3)

        gathered = sb("gathered", [P, 2, G, TOP, KV])
        g_flat = gathered[:].rearrange("x u h s d -> x (u h s d)")
        pooled = g_flat[:, 0:8192].rearrange("x (r b e) -> x r b e", r=R, b=NB)
        group_max = g_flat[:, 8192:8704].rearrange("x (u c) -> x u c", u=2)
        group_den = g_flat[:, 8704:9216].rearrange("x (u c) -> x u c", u=2)
        group_num = g_flat[:, 9216:9728].rearrange("x (u c) -> x u c", u=2)
        wqpk_s = g_flat[:, 10240:10496].rearrange("x (a e) -> x a e", a=4)
        pk_s = g_flat[:, 10496:10752].rearrange("x (a e) -> x a e", a=4)
        qkv = g_flat[:, 8192:14336].rearrange("x (t h r d) -> x t h r d", t=3, h=H, r=R)
        normed = g_flat[:, 14336:16384].rearrange("x (r e) -> x r e", r=R)
        work = sb("work", [P, 11264])
        raw = work[:, 0:2048].rearrange("x (u c) -> x u c", u=2)
        raw_t = work[:, 2048:4096].rearrange("x (u c) -> x u c", u=2)
        shifted = work[:, 4096:6144].rearrange("x (u c) -> x u c", u=2)
        expd = work[:, 6144:8192].rearrange("x (u c) -> x u c", u=2)
        weighted = work[:, 8192:10240].rearrange("x (u c) -> x u c", u=2)
        q_t = work[:, 0:2048].rearrange("x (m c h) -> x m c h", m=2, c=P)
        context = work[:, 2048:3072].rearrange("x (f m e) -> x f m e", f=2, m=2)
        norm_t = work[:, 3072:4096].rearrange("x (u c) -> x u c", u=2)
        k_headmax = work[:, 4096:4352]
        diag_max = work[:, 4352:4864].rearrange("x (m f c) -> x m f c", m=2, f=2)
        squares = work[:, 4864:6912].rearrange("x (r e) -> x r e", r=R)
        ln_a = work[:, 7168:7200]
        ln_b = work[:, 7200:7232]
        max_t = work[:, 7232:7236].rearrange("x (m f) -> x m f", m=2)
        q_max = work[:, 7240:7248]
        q_sum = work[:, 7248:7256]
        k_rsum = work[:, 7256:7260]
        qt = work[:, 0:2048].rearrange("x (g n) -> x g n", g=4)
        kt = work[:, 2048:4096].rearrange("x (g n) -> x g n", g=4)
        kk = work[:, 4096:5120].rearrange("x (b h d) -> x b h d", b=NB, h=G)
        vv = work[:, 5120:7168].rearrange("x (b h d) -> x b h d", b=NB, h=H)
        probs = work[:, 7168:8192].rearrange("x (u c) -> x u c", u=2)
        probs_t = work[:, 8192:9216].rearrange("x (u c) -> x u c", u=2)
        sides = work[:, 9216:10240].rearrange("x (s h k) -> x s h k", s=SIDES, h=H)
        sides_rest = work[:, 10240:11264].rearrange("x (s h k) -> x s h k", s=SIDES, h=H)

        top = sb("top", [P, SIDES, H, TOP])
        top_at = sb("top_at", [P, SIDES, G, TOP], U32)
        code = sb("code", [P, SIDES, G, TOP])
        cand = sb("cand", [P, H, NC_])
        cand_code = sb("cand_code", [P, G, NC_])
        cand_rest = sb("cand_rest", [P, H, NC_])
        best = sb("best", [P, H, TOP])
        best_at = sb("best_at", [P, G, TOP], U32)
        best_atf = sb("best_atf", [P, G, TOP])
        onehot = sb("onehot", [P, TOP, NC_])
        best_code = sb("best_code", [P, G, TOP])
        rows = sb("rows", [P, NB, G * TOP], U32)
        size = sb("size", [P, D])
        base = sb("base", [P, H])
        weight_in = sb("weight_in", [P, H, TOP])
        weight_sum = sb("weight_sum", [P, H])
        weight = sb("weight", [P, NB, G, TOP])
        neg_thr = sb("neg_thr", [P, D, NB])
        rsum = sb("rsum", [P, D, NB])
        rsum_next = sb("rsum_next", [P, D, NB])
        dense_sum = sb("dense_sum", [P, STEPS])
        sums = sb("sums", [P, 2, D])
        chosen_sum = sb("chosen_sum", [P, 2, D, NB])
        checks = sb("checks", [1, 3, D])
        flags = sb("flags", [1, 2 * D], I32)
        r_weight = sb("r_weight", [P, NB, TOP])
        r_rows = sb("r_rows", [P, NB * TOP], U32)
        row_ln = sb("row_ln", [P, NB, E])
        row_add = sb("row_add", [P, NB, E])
        normed2 = sb("normed2", [P, NB, E])
        sq2 = sb("sq2", [P, NB, E])
        ln2 = sb("ln2", [P, 2, NB])
        norm2_t = sb("norm2_t", [E, N])
        neg_max = sb("neg_max", [P, 4])
        den = sb("den", [P, 2, H])
        rden = sb("rden", [P, H])
        attended = sb("attended", [P, H, E])
        attended_t = sb("attended_t", [P, 4, P])
        result = sb("result", [P, NB, E])
        diag = sb("diag", [P, 2, NB, P])
        rsum_wide = sb("rsum_wide", [P, N])
        v_dense = sb("v_dense", [P, N])

        w_tok2 = sb("w_tok2", [P, P])
        wqkv_s = sb("wqkv_s", [E, 3 * E])
        bqkv_s = sb("bqkv_s", [P, 3 * E])
        w_side = sb("w_side", [E, SIDES * H * NK])
        w_pair = sb("w_pair", [E, D, SIDES, NK])
        wq_s = sb("wq_s", [E, H * E])
        wo_s = sb("wo_s", [P, 4, E])
        ident = sb("ident", [P, P])
        ident16 = sb("ident16", [P, P], BF16)
        causal = sb("causal", [P, P], BF16)
        ones = sb("ones", [P, P])
        first_side = sb("first_side", [P, P])
        pick = sb("pick", [P, CH, P], BF16)
        cell_i = sb("cell_i", [P, NC_], I32)
        cell_no = sb("cell_no", [P, NC_])
        head_i = sb("head_i", [P, G, TOP], I32)
        head_base = sb("head_base", [P, G, TOP])

        ps = ctx.enter_context(nc.psum_tensor("ps", [P, 8, 512], F32))
        SC, SIM, PT, O, MISC = 0, 2, 4, 6, 7
        U, ACC, AUX = SIM, PT, O

        weights_in = sem("weights_in")
        const_made = sem("const_made")
        const_cast = sem("const_cast")
        side_ps = sem("side_ps")
        side_sb = sem("side_sb")
        done_a = sem("done_a")
        done_b = sem("done_b")

        a_raw_in = [sem(f"a_raw_in{u}") for u in range(2)]
        a_raw_free = sem("a_raw_free")
        a_t_ps = sem("a_t_ps")
        a_t_sb = sem("a_t_sb")
        a_scores = sem("a_scores")
        a_shifted = sem("a_shifted")
        a_exp = sem("a_exp")
        a_weighted = sem("a_weighted")
        a_pooled = sem("a_pooled")

        b_var = sem("b_var")
        b_std = sem("b_std")
        b_normed = sem("b_normed")
        b_t_ps = sem("b_t_ps")
        b_t_sb = sem("b_t_sb")
        b_qkv_ps = sem("b_qkv_ps")
        b_qkv_sb = sem("b_qkv_sb")
        b_headmax = sem("b_headmax")
        b_headmax_t = sem("b_headmax_t")
        b_diag = sem("b_diag")
        b_kmax = sem("b_kmax")
        b_kshift = sem("b_kshift")
        b_kexp = sem("b_kexp")
        b_qshift = sem("b_qshift")
        b_qexp = sem("b_qexp")
        b_qnormed = sem("b_qnormed")
        b_ctx_ps = sem("b_ctx_ps")
        b_ctx_sb = sem("b_ctx_sb")
        b_qt_ps = sem("b_qt_ps")
        b_qt_sb = sem("b_qt_sb")
        b_out_ps = sem("b_out_ps")

        c_var = sem("c_var")
        c_std = sem("c_std")
        c_normed = sem("c_normed")
        c_t_ps = sem("c_t_ps")
        c_t_sb = sem("c_t_sb")
        c_q_ps = sem("c_q_ps")
        c_q_sb = sem("c_q_sb")
        c_side_ps = sem("c_side_ps")
        c_side_sb = sem("c_side_sb")
        c_side_used = sem("c_side_used")
        c_best = sem("c_best")
        c_wexp = sem("c_wexp")
        c_rows = sem("c_rows")
        c_landed = [[sem(f"c_landed{u}{h}") for h in range(G)] for u in range(2)]
        c_scaled = sem("c_scaled")
        c_diag = sem("c_diag")
        c_diag_used = sem("c_diag_used")
        c_pair_ps = sem("c_pair_ps")
        c_part1 = sem("c_part1")
        c_rest1 = sem("c_rest1")
        c_part2 = sem("c_part2")
        c_parts = sem("c_parts")
        c_table_in = [sem(f"c_table_in{u}") for u in range(2)]
        c_u = sem("c_u")
        c_expo = sem("c_expo")
        c_w = sem("c_w")
        c_mm = sem("c_mm")
        c_rsum_ps = sem("c_rsum_ps")
        c_rsum_sb = sem("c_rsum_sb")
        c_dense = sem("c_dense")
        c_vt_ps = sem("c_vt_ps")
        c_vt_sb = sem("c_vt_sb")
        b_kept = sem("b_kept")
        c_ln_in = sem("c_ln_in")
        c_add_in = sem("c_add_in")
        c_gather_used = sem("c_gather_used")
        c_kv = sem("c_kv")
        c_kt_ps = sem("c_kt_ps")
        c_kt_sb = sem("c_kt_sb")
        c_sim = sem("c_sim")
        c_max = sem("c_max")
        c_probs = sem("c_probs")
        c_pt_ps = sem("c_pt_ps")
        c_pt_sb = sem("c_pt_sb")
        c_o_ps = sem("c_o_ps")
        c_o_sb = sem("c_o_sb")
        c_ot_ps = sem("c_ot_ps")
        c_ot_sb = sem("c_ot_sb")
        c_y_ps = sem("c_y_ps")
        c_y_sb = sem("c_y_sb")
        c_stored = [sem(f"c_stored{b}") for b in range(NB)]

        c_sums = sem("c_sums")
        c_sums_ps = sem("c_sums_ps")
        c_flags = sem("c_flags")
        c_flags_read = sem("c_flags_read")
        r_var = sem("r_var")
        r_std = sem("r_std")
        r_normed = sem("r_normed")
        r_t_ps = sem("r_t_ps")
        r_t_sb = sem("r_t_sb")
        r_side_ps = sem("r_side_ps")
        r_side_sb = sem("r_side_sb")
        r_best = sem("r_best")
        r_wexp = sem("r_wexp")
        r_rows_out = sem("r_rows_out")
        r_landed = [sem(f"r_landed{b}") for b in range(NB)]
        r_kv = sem("r_kv")
        r_kt_ps = sem("r_kt_ps")
        r_kt_sb = sem("r_kt_sb")

        block = ctx.enter_context(nc.Block())

        def repair(eng, k, counts, start, head):
            eng.wait_ge(c_flags, k + 1)
            eng.nop(nofuse=True)
            with eng.If(eng.value_load(flags[0:1, D:D + 1], min_val=0, max_val=1) > 0):
                start(eng.snap(counts[0]))
                eng.reg_add(counts[0], counts[0], 1)
                for hd in range(D):
                    with eng.If(eng.value_load(flags[0:1, hd:hd + 1], min_val=0, max_val=1) > 0):
                        head(hd, eng.snap(counts[1]))
                        eng.reg_add(counts[1], counts[1], 1)
            eng.nop(nofuse=True).then_inc(c_flags_read, 1)

        def repair_counts(eng):
            counts = [eng.alloc_register("repaired_rows"), eng.alloc_register("repaired_heads")]
            for c in counts:
                eng.reg_mov(c, 0)
            return counts
        NW = 10

        @block.sync
        def _(sp):
            sp.wait_ge(const_made, 1)
            sp.dma_start(w_tok2[0:E, 0:E], w_tok).then_inc(weights_in, 16)
            sp.dma_start(w_tok2[E:P, E:P], w_tok).then_inc(weights_in, 16)
            sp.dma_start(wqkv_s[:], w_qkv).then_inc(weights_in, 16)
            sp.dma_start(bqkv_s[:], b_qkv.to_broadcast([P, 3 * E])).then_inc(weights_in, 16)
            sp.dma_start(wqpk_s[:], wqpk_t.rearrange("(a p) e -> p a e", p=P)).then_inc(weights_in, 16)
            sp.dma_start(pk_s[:], pk_t.rearrange("(a p) e -> p a e", p=P)).then_inc(weights_in, 16)
            sp.dma_start(wq_s[:], w_q).then_inc(weights_in, 16)
            sp.dma_start(wo_s[:], w_o.rearrange("(a p) e -> p a e", p=P)).then_inc(weights_in, 16)
            with sp.Fori(0, R // 2) as r2:
                for u in range(2):
                    sp.wait_ge(a_raw_free, r2 * 2 + (u + 1))
                    sp.dma_start(raw[:, u].rearrange("x (b c) -> x b c", b=NB),
                                 x[r2 * 2 + u, :, :].rearrange("(b p q) f -> p b (q f)", b=NB, p=P)
                                 ).then_inc(a_raw_in[u], 16)
            sp.wait_ge(done_b, 3)
            sp.dma_start(kept.rearrange("r p c -> p r c"), arena[:].rearrange("x (r c) -> x r c", r=R)
                         ).then_inc(b_kept, 16)
            sp.wait_ge(b_kept, 16)
            with sp.Fori(0, R) as k:
                for n in range(D * CH // PIECE):
                    sp.wait_ge(c_mm, k * STEPS + PIECE * (n + 1))
                    hd, j = divmod(n, CH // PIECE)
                    sp.dma_start(table[:, n % 2], tables[hd, :, j * PIECE:(j + 1) * PIECE, :]
                                 ).then_inc(c_table_in[n % 2], 16)

        @block.gpsimd
        def _(pool):
            nc.gpsimd.memset(w_tok2[:], 0.0).then_inc(const_made, 1)
            nc.gpsimd.memset(ident[:], 0.0)
            nc.gpsimd.memset(causal[:], 0.0)
            nc.gpsimd.memset(ident16[:], 0.0)
            nc.gpsimd.memset(pick[:], 0.0)
            nc.gpsimd.memset(ones[:], 1.0)
            nc.gpsimd.memset(first_side[:, 0:NK], 1.0)
            nc.gpsimd.memset(first_side[:, NK:P], 0.0)
            nc.gpsimd.iota(cell_i[:], pattern=[[1, NC_]], base=0, channel_multiplier=0)
            nc.gpsimd.iota(head_i[:], pattern=[[NKV, G], [0, TOP]], base=D * NKV,
                           channel_multiplier=0).then_inc(const_made, 1)
            pool.wait_ge(const_made, 2)
            nc.gpsimd.affine_select(out=ident[:], in_=ident[:], compare_op=ALU.not_equal, fill=1.0, base=0,
                                    pattern=[[-1, P]], channel_multiplier=1).then_inc(const_made, 1)
            pool.wait_ge(const_made, 3)
            nc.gpsimd.affine_select(out=ident16[:], in_=ident16[:], compare_op=ALU.not_equal, fill=1.0, base=0,
                                    pattern=[[-1, P]], channel_multiplier=1).then_inc(const_made, 1)
            pool.wait_ge(const_made, 4)
            nc.gpsimd.affine_select(out=pick[0:NK], in_=pick[0:NK], compare_op=ALU.not_equal, fill=1.0, base=0,
                                    pattern=[[0, 2 * CH], [-1, NK]], channel_multiplier=1).then_inc(const_made, 1)
            pool.wait_ge(const_made, 5)
            nc.gpsimd.affine_select(out=pick[NK:P], in_=pick[NK:P], compare_op=ALU.not_equal, fill=1.0, base=0,
                                    pattern=[[-1, 2 * CH], [0, NK]], channel_multiplier=1).then_inc(const_made, 1)
            pool.wait_ge(const_made, 6)
            nc.gpsimd.affine_select(out=causal[:], in_=causal[:], compare_op=ALU.is_ge, fill=MASKED, base=0,
                                    pattern=[[-1, P]], channel_multiplier=1).then_inc(const_made, 1)
            with pool.Fori(0, R // 2) as r2:
                for u in range(2):
                    pool.wait_ge(a_exp, r2 * 2 + (u + 1))
                    pool.nop(nofuse=True)
                    nc.gpsimd.tensor_tensor(weighted[:, u], expd[:, u], raw[:, u], ALU.mult
                                            ).then_inc(a_weighted, 1)
            pool.wait_ge(done_b, 3)
            counts = repair_counts(pool)

            def repair_head(hd, n):
                pool.wait_ge(r_rows_out, n + 1)
                pool.nop(nofuse=True)
                for b in range(NB):
                    for s in range(TOP):
                        at = b * TOP + s
                        pool.indirect_dma_start(
                            gathered[:, 0, b, s, :], None, keysvals[:, :],
                            bass.IndirectOffsetOnAxis(ap=r_rows[:, at:at + 1], axis=0)
                        ).then_inc(r_landed[b], 16)
                pool.wait_ge(r_kv, n + 1)
                pool.nop(nofuse=True)

            with pool.Fori(0, R) as k:
                for b in range(NB):
                    pool.wait_ge(c_rows, k * NB + (b + 1))
                    pool.nop(nofuse=True)
                    for h in range(G):
                        pool.wait_ge(c_gather_used, k * (NB * G) + (b * G + h + 1))
                        pool.nop(nofuse=True)
                        for s in range(TOP):
                            at = h * TOP + s
                            pool.indirect_dma_start(
                                gathered[:, b % 2, h, s, :], None, keysvals[:, :],
                                bass.IndirectOffsetOnAxis(ap=rows[:, b, at:at + 1], axis=0)
                            ).then_inc(c_landed[b % 2][h], 16)
                repair(pool, k, counts, lambda n: None, repair_head)

        @block.tensor
        def _(pe):
            pe.wait_ge(const_made, 7)
            pe.wait_ge(weights_in, 16 * 8)
            for a in range(SIDES * H * DK // P):
                for g in range(P // DK):
                    lo = g * DK
                    last = nc.tensor.matmul(ps[0:E, g, a * NK:(a + 1) * NK], wqpk_s[lo:lo + DK, a, :],
                                            pk_s[lo:lo + DK, a, :], start=True, stop=True)
            last.then_inc(side_ps, 1)
            pe.wait_ge(side_sb, 1)

            with pe.Fori(0, R // 2) as r2:
                for u in range(2):
                    pe.wait_ge(a_raw_in[u], r2 * 16 + 16)
                    pe.nop(nofuse=True)
                    for j in range(8):
                        last = nc.tensor.transpose(ps[:, 4 * u + j // 4, (j % 4) * P:(j % 4 + 1) * P],
                                                   raw[:, u, j * P:(j + 1) * P], ident[:])
                    last.then_inc(a_t_ps, 1)
                    pe.wait_ge(a_t_sb, r2 * 2 + (u + 1))
                    pe.nop(nofuse=True)
                    pe.wait_ge(a_shifted, r2 * 2 + (u + 1))
                    pe.nop(nofuse=True)
                    for j in range(8):
                        last = nc.tensor.matmul(ps[:, 4 * u + 2 + j // 4, (j % 4) * P:(j % 4 + 1) * P],
                                                raw_t[:, u, j * P:(j + 1) * P], w_tok2[:],
                                                start=True, stop=True)
                    last.then_inc(a_scores, 1)

            pe.wait_ge(done_a, 1)
            with pe.Fori(0, NB) as cb:
                pe.wait_ge(b_normed, cb + 1)
                pe.nop(nofuse=True)
                for g in range(8):
                    if g >= 2:
                        pe.wait_ge(b_t_sb, cb * 8 + (g - 1))
                        pe.nop(nofuse=True)
                    for i in range(4):
                        last = nc.tensor.transpose(ps[0:E, g % 2, i * P:(i + 1) * P], normed[:, 4 * g + i, :],
                                                   ident[:])
                    last.then_inc(b_t_ps, 1)
                    pe.wait_ge(b_t_sb, cb * 8 + (g + 1))
                    pe.nop(nofuse=True)
                    if g >= 2:
                        pe.wait_ge(b_qkv_sb, cb * 8 + (g - 1))
                        pe.nop(nofuse=True)
                    for i in range(4):
                        o = ps[:, 2 + 2 * (g % 2) + i // 2, (i % 2) * 192:(i % 2 + 1) * 192]
                        last = nc.tensor.matmul(o, norm_t[0:E, g % 2, i * P:(i + 1) * P], wqkv_s[:],
                                                start=True, stop=True)
                    last.then_inc(b_qkv_ps, 1)
                pe.wait_ge(b_headmax, cb + 1)
                pe.nop(nofuse=True)
                for m in range(2):
                    last = nc.tensor.transpose(ps[:, 6, m * P:(m + 1) * P], k_headmax[:, m * P:(m + 1) * P],
                                               ident[:])
                last.then_inc(b_headmax_t, 1)
                pe.wait_ge(b_diag, cb + 1)
                pe.nop(nofuse=True)
                for f in range(2):
                    for m in range(2):
                        last = nc.tensor.matmul(ps[f * E:(f + 1) * E, 7, m * P:(m + 1) * P], ones[:, 0:E],
                                                diag_max[:, m, f, :], start=True, stop=True)
                last.then_inc(b_kmax, 1)
                pe.wait_ge(b_kexp, cb + 1)
                pe.nop(nofuse=True)
                for f in range(2):
                    half = slice(f * E, (f + 1) * E)
                    for m in range(2):
                        for h in range(H):
                            keys = qkv[half, 1, h, 16 * m:16 * (m + 1), :].rearrange("x r d -> x (r d)")
                            nc.tensor.matmul(ps[:, f, m * 256:(m + 1) * 256], keys,
                                             qkv[half, 2, h].rearrange("x r d -> x (r d)"),
                                             start=(h == 0), stop=(h == H - 1))
                        for h in range(H):
                            keys = qkv[half, 1, h, 16 * m:16 * (m + 1), :].rearrange("x r d -> x (r d)")
                            last = nc.tensor.matmul(ps[:, [2, 7][f], m:m + 1], keys, ones[half, 0:1],
                                                    start=(h == 0), stop=(h == H - 1))
                last.then_inc(b_ctx_ps, 1)
                pe.wait_ge(b_qnormed, cb + 1)
                pe.nop(nofuse=True)
                for m in range(2):
                    for hh in range(2):
                        for i in range(4):
                            h = 4 * hh + i
                            last = nc.tensor.transpose(ps[:, 3 + 2 * m + hh, i * P:(i + 1) * P],
                                                       qkv[:, 0, h, 16 * m:16 * (m + 1), :].rearrange("x r d -> x (r d)"),
                                                       ident[:])
                        last.then_inc(b_qt_ps, 1)
                pe.wait_ge(b_qt_sb, cb * 4 + 4)
                pe.nop(nofuse=True)
                pe.wait_ge(b_ctx_sb, cb + 1)
                pe.nop(nofuse=True)
                for f in range(2):
                    for b in range(NB):
                        bank = [[0, 1], [2, 7]][f][b // 2]
                        for m in range(2):
                            lo = f * E + 16 * b
                            last = nc.tensor.matmul(ps[:, bank, (b % 2) * 256:(b % 2 + 1) * 256],
                                                    q_t[:, m, lo:lo + 16, :].rearrange("x c h -> x (c h)"),
                                                    context[:, f, m, :], start=(m == 0), stop=(m == 1))
                last.then_inc(b_out_ps, 1)
            pe.wait_ge(done_b, 3)

            def transpose_tokens(k):
                pe.wait_ge(c_normed, k + 1)
                pe.nop(nofuse=True)
                for b in range(NB):
                    last = nc.tensor.transpose(ps[0:E, MISC, b * P:(b + 1) * P], normed2[:, b, :], ident[:])
                last.then_inc(c_t_ps, 1)
                pe.wait_ge(c_t_sb, k + 1)
                pe.nop(nofuse=True)

            def score_sides(k, b):
                pe.wait_ge(c_side_sb, k * NB + (b + 1))
                pe.nop(nofuse=True)
                for s in range(SIDES):
                    last = nc.tensor.matmul(ps[:, SC + s, :], norm2_t[:, b * P:(b + 1) * P],
                                            w_side[:, s * 512:(s + 1) * 512], start=True, stop=True)
                last.then_inc(c_side_ps, 1)

            def project_queries(k):
                for g in range(4):
                    if g >= 2:
                        pe.wait_ge(c_q_sb, k * 4 + (g - 1))
                        pe.nop(nofuse=True)
                    nc.tensor.matmul(ps[:, SIM + g % 2, :], wq_s[:, g * P:(g + 1) * P], norm2_t[:],
                                     start=True, stop=True).then_inc(c_q_ps, 1)

            def transpose_keys(k, b):
                pe.wait_ge(c_kv, k * NB + (b + 1))
                pe.nop(nofuse=True)
                if b > 0:
                    pe.wait_ge(c_kt_sb, k * NB + b)
                    pe.nop(nofuse=True)
                for g in range(G // 2):
                    last = nc.tensor.transpose(ps[:, MISC, g * P:(g + 1) * P],
                                               kk[:, b, 2 * g:2 * g + 2, :].rearrange("x h d -> x (h d)"), ident[:])
                last.then_inc(c_kt_ps, 1)

            def score_pairs(k):
                for hd in range(D):
                    if hd < 2:
                        pe.wait_ge(c_q_sb, k * 4 + (hd + 3))
                        pe.nop(nofuse=True)
                    else:
                        pe.wait_ge(c_rest1, k * D + (hd - 1))
                        pe.nop(nofuse=True)
                    nc.tensor.matmul(ps[:, U + hd % 2, :], w_pair[:, hd, :, :].rearrange("x s k -> x (s k)"),
                                     norm2_t[:], start=True, stop=False)
                    pe.wait_ge(c_diag, k * (2 * D) + (hd + 1))
                    pe.nop(nofuse=True)
                    for b in range(NB):
                        last = nc.tensor.matmul(ps[:, U + hd % 2, b * P:(b + 1) * P], first_side[:],
                                                diag[:, hd % 2, b, :], start=False, stop=(b == NB - 1))
                    last.then_inc(c_pair_ps, 1)

            def sum_scores(k, c):
                if c == 0:
                    pe.wait_ge(c_parts, k * D + D)
                    pe.nop(nofuse=True)
                if c >= 2:
                    pe.wait_ge(c_expo, k * STEPS + (c - 1))
                    pe.nop(nofuse=True)
                for t in range(3):
                    last = nc.tensor.matmul(ps[:, U + c % 2, :], pick[:, c % CH, :], parts[:, c // CH, t, :],
                                            start=(t == 0), stop=(t == 2))
                last.then_inc(c_u, 1)

            def mix_dense(k, c):
                hd, n = c // CH, c // PIECE
                if c % PIECE == 0:
                    pe.wait_ge(c_table_in[n % 2], k * (8 * D * CH // PIECE) + 16 * (n // 2 + 1))
                    pe.nop(nofuse=True)
                if c % CH == 0 and hd >= 2:
                    pe.wait_ge(c_dense, k * D + (hd - 1))
                    pe.nop(nofuse=True)
                pe.wait_ge(c_w, k * STEPS + (c + 1))
                pe.nop(nofuse=True)
                nc.tensor.matmul(ps[:, ACC + hd % 2, :], table[:, n % 2, c % PIECE, :], dense_w[:, c % 3, :],
                                 start=(c % CH == 0), stop=(c % CH == CH - 1)).then_inc(c_mm, 1)

            def spread_sums(k, hd):
                pe.wait_ge(c_diag, k * (2 * D) + (D + hd + 1))
                pe.nop(nofuse=True)
                if hd > 0:
                    pe.wait_ge(c_vt_sb, k * D + hd)
                    pe.nop(nofuse=True)
                for b in range(NB):
                    last = nc.tensor.matmul(ps[:, AUX, b * P:(b + 1) * P], ones[:], diag[:, hd % 2, b, :],
                                            start=True, stop=True)
                last.then_inc(c_rsum_ps, 1)

            def transpose_values(k, hd):
                pe.wait_ge(c_dense, k * D + (hd + 1))
                pe.nop(nofuse=True)
                half = slice(E, P) if hd % 2 == 0 else slice(0, E)
                for b in range(NB):
                    last = nc.tensor.transpose(ps[:, AUX, b * E:(b + 1) * E], v_dense[half, b * P:(b + 1) * P],
                                               ident[half, half])
                last.then_inc(c_vt_ps, 1)

            def sum_over_tokens(k):
                pe.wait_ge(c_sums, k + 1)
                pe.nop(nofuse=True)
                nc.tensor.matmul(ps[0:1, SIM + 1, 0:2 * D], ones[:, 0:1], sums[:].rearrange("x t h -> x (t h)"),
                                 start=True, stop=True).then_inc(c_sums_ps, 1)

            def repair_row(n):
                pe.wait_ge(r_normed, n + 1)
                pe.nop(nofuse=True)
                for b in range(NB):
                    last = nc.tensor.transpose(ps[0:E, MISC, b * P:(b + 1) * P], normed2[:, b, :], ident[:])
                last.then_inc(r_t_ps, 1)
                pe.wait_ge(r_t_sb, n + 1)
                pe.nop(nofuse=True)

            def repair_head(hd, n):
                for b in range(NB):
                    last = nc.tensor.matmul(ps[:, MISC, b * P:(b + 1) * P], r_norm_t[:, b * P:(b + 1) * P],
                                            w_pair[:, hd, :, :].rearrange("x s k -> x (s k)"),
                                            start=True, stop=True)
                last.then_inc(r_side_ps, 1)
                pe.wait_ge(r_kv, n + 1)
                pe.nop(nofuse=True)
                for b in range(NB):
                    last = nc.tensor.transpose(ps[0:E, MISC, b * P:(b + 1) * P], kk[:, b, 0, :], ident[:])
                last.then_inc(r_kt_ps, 1)
                pe.wait_ge(r_kt_sb, n + 1)
                pe.nop(nofuse=True)

            def attention(k):
                steps = [(b, h) for b in range(NB) for h in range(H)]
                n = len(steps)
                pe.wait_ge(c_kt_sb, k * NB + NB)
                pe.nop(nofuse=True)
                pe.wait_ge(c_vt_sb, k * D + D)
                pe.nop(nofuse=True)
                repair(pe, k, counts, repair_row, repair_head)

                def similarities(s):
                    b, h = steps[s]
                    half = slice((h % 2) * E, (h % 2 + 1) * E)
                    w = (b + 1) * P
                    if s >= 2:
                        pe.wait_ge(c_probs, k * n + (s - 1))
                        pe.nop(nofuse=True)
                    nc.tensor.matmul(ps[:, SIM + s % 2, 0:w], qt[half, h // 2, b * P:w], kt[half, h // 2, 0:w],
                                     start=True, stop=False)
                    nc.tensor.matmul(ps[:, SIM + s % 2, b * P:w], ident16[:], causal[:],
                                     start=False, stop=True).then_inc(c_sim, 1)

                def transpose_probs(s):
                    b, h = steps[s]
                    pe.wait_ge(c_probs, k * n + (s + 1))
                    pe.nop(nofuse=True)
                    if s >= 2:
                        pe.wait_ge(c_pt_sb, k * n + (s - 1))
                        pe.nop(nofuse=True)
                    for j in range(b + 1):
                        last = nc.tensor.transpose(ps[:, PT + s % 2, j * P:(j + 1) * P],
                                                   probs[:, s % 2, j * P:(j + 1) * P], ident[:])
                    last.then_inc(c_pt_ps, 1)

                def attend(s):
                    b, h = steps[s]
                    pe.wait_ge(c_pt_sb, k * n + (s + 1))
                    pe.nop(nofuse=True)
                    if h == 0 and b > 0:
                        pe.wait_ge(c_o_sb, k * NB + b)
                        pe.nop(nofuse=True)
                    for j in range(b + 1):
                        last = nc.tensor.matmul(ps[:, O, h * E:(h + 1) * E], probs_t[:, s % 2, j * P:(j + 1) * P],
                                                vv[:, j, h, :], start=(j == 0), stop=(j == b))
                    if h == H - 1:
                        last.then_inc(c_o_ps, 1)

                def project(b, part):
                    if part == 0:
                        pe.wait_ge(c_o_sb, k * NB + (b + 1))
                        pe.nop(nofuse=True)
                        for g in range(4):
                            last = nc.tensor.transpose(
                                ps[:, MISC, g * P:(g + 1) * P],
                                attended[:, 2 * g:2 * g + 2, :].rearrange("x h d -> x (h d)"), ident[:])
                        last.then_inc(c_ot_ps, 1)
                    else:
                        pe.wait_ge(c_ot_sb, k * NB + (b + 1))
                        pe.nop(nofuse=True)
                        for g in range(4):
                            last = nc.tensor.matmul(ps[:, MISC, 0:E], attended_t[:, g, :], wo_s[:, g, :],
                                                    start=(g == 0), stop=(g == 3))
                        last.then_inc(c_y_ps, 1)

                for s in range(n + 5):
                    if s < n:
                        similarities(s)
                    if 1 <= s <= n:
                        transpose_probs(s - 1)
                    if 2 <= s <= n + 1:
                        attend(s - 2)
                    if s >= H + 3 and (s - 3) % H == 0:
                        project((s - 3) // H - 1, 0)
                    if s >= H + 4 and (s - 4) % H == 0:
                        project((s - 4) // H - 1, 1)
                pe.wait_ge(c_y_sb, k * NB + NB)
                pe.nop(nofuse=True)

            def row(k, more):
                project_queries(k)
                score_pairs(k)
                if more:
                    transpose_tokens(k + 1)
                for c in range(STEPS + 14):
                    if more and c < STEPS and c % QUARTER == 0:
                        score_sides(k + 1, c // QUARTER)
                    if c < STEPS:
                        sum_scores(k, c)
                    if 2 <= c < STEPS + 2:
                        mix_dense(k, c - 2)
                    if c < STEPS and c % CH == 20:
                        spread_sums(k, c // CH)
                    if c >= CH and c % CH == 6:
                        transpose_values(k, c // CH - 1)
                    if c >= QUARTER and c % QUARTER == 12:
                        transpose_keys(k, c // QUARTER - 1)
                    if c == STEPS + 5:
                        sum_over_tokens(k)
                attention(k)

            counts = repair_counts(pe)
            transpose_tokens(0)
            for b in range(NB):
                score_sides(0, b)
            with pe.Fori(0, R - 1) as k:
                row(k, True)
            row(R - 1, False)

        @block.scalar
        def _(act):
            act.wait_ge(side_ps, 1)
            nc.scalar.copy(w_side[:].rearrange("x (a g k) -> x a g k", a=4, g=4),
                           ps[0:E, 0:4, 0:4 * NK].rearrange("x g (a k) -> x a g k", a=4))
            nc.scalar.drain()
            nc.scalar.copy(w_pair[:], w_side[:].rearrange("x (s h k) -> x h s k", s=SIDES, h=H)[:, 0:D]
                           ).then_inc(side_sb, 1)

            with act.Fori(0, R // 2) as r2:
                for u in range(2):
                    act.wait_ge(a_t_ps, r2 * 2 + (u + 1))
                    act.nop(nofuse=True)
                    nc.scalar.copy(raw_t[:, u], ps[:, 4 * u:4 * u + 2, :].rearrange("x s c -> x (s c)")
                                   ).then_inc(a_t_sb, 1)
                for u in range(2):
                    act.wait_ge(a_shifted, r2 * 2 + (u + 3))
                    act.nop(nofuse=True)
                    nc.scalar.activation(expd[:, u], shifted[:, u], ACT.Exp).then_inc(a_exp, 1)

            act.wait_ge(done_a, 1)
            with act.Fori(0, NB) as cb:
                act.wait_ge(b_var, cb + 1)
                act.nop(nofuse=True)
                nc.scalar.activation(ln_b, ln_a, ACT.Sqrt).then_inc(b_std, 1)
                for g in range(8):
                    act.wait_ge(b_t_ps, cb * 8 + (g + 1))
                    act.nop(nofuse=True)
                    nc.scalar.copy(norm_t[0:E, g % 2, :], ps[0:E, g % 2, :]).then_inc(b_t_sb, 1)
                act.wait_ge(b_kshift, cb + 1)
                act.nop(nofuse=True)
                nc.scalar.activation(qkv[:, 1], qkv[:, 1], ACT.Exp).then_inc(b_kexp, 1)
                act.wait_ge(b_qshift, cb + 1)
                act.nop(nofuse=True)
                nc.scalar.activation(qkv[:, 0], qkv[:, 0], ACT.Exp).then_inc(b_qexp, 1)
                for m in range(2):
                    for hh in range(2):
                        act.wait_ge(b_qt_ps, cb * 4 + (2 * m + hh + 1))
                        act.nop(nofuse=True)
                        nc.scalar.copy(q_t[:, m, :, 4 * hh:4 * hh + 4].rearrange("x c h -> x h c"),
                                       ps[:, 3 + 2 * m + hh, :].rearrange("x (h c) -> x h c", h=4)
                                       ).then_inc(b_qt_sb, 1)

            act.wait_ge(done_b, 3)
            nc.scalar.nop(nofuse=True).then_inc(c_side_sb, 1)
            act.wait_ge(b_kept, 16)

            def load_row(k, dst, landed):
                act.dma_start(dst.rearrange("x b e -> x (b e)"),
                              kept[bass.ds(k, 1), :, :].rearrange("r p c -> (r p) c")).then_inc(landed, 16)

            def norm_and_transpose(k):
                act.wait_ge(c_var, k + 1)
                nc.scalar.activation(ln2[:, 1], ln2[:, 0], ACT.Sqrt).then_inc(c_std, 1)
                act.wait_ge(c_t_ps, k + 1)
                nc.scalar.copy(norm2_t[:], ps[0:E, MISC, :]).then_inc(c_t_sb, 1)

            def score_sides(k, b):
                act.wait_ge(c_side_ps, k * NB + (b + 1))
                act.wait_ge(c_side_used, k * NB + (b + 1))
                nc.scalar.copy(sides[:].rearrange("x s h k -> x (s h k)"),
                               ps[:, SC:SC + 2, :].rearrange("x s c -> x (s c)")).then_inc(c_side_sb, 1)

            def weights(k, b):
                act.wait_ge(c_best, k * NB + (b + 1))
                nc.scalar.activation(weight_in[:], weight_in[:], ACT.Exp).then_inc(c_wexp, 1)

            def project_queries(k):
                for g in range(4):
                    act.wait_ge(c_q_ps, k * 4 + (g + 1))
                    nc.scalar.mul(qt[:, g, :], ps[:, SIM + g % 2, :], float(E) ** -0.5).then_inc(c_q_sb, 1)

            def split_pair(k, hd):
                act.wait_ge(c_pair_ps, k * D + (hd + 1))
                nc.scalar.copy(parts[:, hd, 0, :], ps[:, U + hd % 2, :]).then_inc(c_part1, 1)
                act.wait_ge(c_rest1, k * D + (hd + 1))
                nc.scalar.copy(parts[:, hd, 1, :], expo[:, hd % 2, :]).then_inc(c_part2, 1)

            def exponentials(k, c):
                act.wait_ge(c_u, k * STEPS + (c + 1))
                if c >= 3:
                    act.wait_ge(c_w, k * STEPS + (c - 2))
                nc.scalar.activation(expo[:, c % 3, :], ps[:, U + c % 2, :], ACT.Exp).then_inc(c_expo, 1)

            def weigh(k, b, h, s):
                if s == 0:
                    act.wait_ge(c_landed[b % 2][h], k * (2 * TOP * 16) + (b // 2 + 1) * TOP * 16)
                g = nc.scalar.mul(gathered[:, b % 2, h, s, :], gathered[:, b % 2, h, s, :], weight[:, b, h, s:s + 1])
                if s == TOP - 1:
                    g.then_inc(c_scaled, 1)

            def transpose_keys(k, b):
                act.wait_ge(c_kt_ps, k * NB + (b + 1))
                nc.scalar.copy(kt[:, D // 2:, b * P:(b + 1) * P],
                               ps[:, MISC, 0:256].rearrange("x (g c) -> x g c", g=2)).then_inc(c_kt_sb, 1)

            def spread_sums(k, hd):
                act.wait_ge(c_rsum_ps, k * D + (hd + 1))
                if hd > 0:
                    act.wait_ge(c_dense, k * D + hd)
                nc.scalar.copy(rsum_wide[:], ps[:, AUX, :]).then_inc(c_rsum_sb, 1)

            def transpose_values(k, hd):
                act.wait_ge(c_vt_ps, k * D + (hd + 1))
                nc.scalar.copy(vv[:, :, hd, :], ps[:, AUX, 0:256].rearrange("x (b d) -> x b d", b=NB)
                               ).then_inc(c_vt_sb, 1)

            def attention(k):
                steps = [(b, h) for b in range(NB) for h in range(H)]
                n = len(steps)
                for s in range(n + 6):
                    if s < n:
                        b, h = steps[s]
                        w = (b + 1) * P
                        act.wait_ge(c_max, k * n + (s + 1))
                        act.nop(nofuse=True)
                        if s >= 2:
                            act.wait_ge(c_pt_ps, k * n + (s - 1))
                            act.nop(nofuse=True)
                        nc.scalar.activation(probs[:, s % 2, 0:w], ps[:, SIM + s % 2, 0:w], ACT.Exp,
                                             bias=neg_max[:, s % 4:s % 4 + 1],
                                             accum_out=den[:, b % 2, h:h + 1]).then_inc(c_probs, 1)
                    if 1 <= s <= n:
                        b, h = steps[s - 1]
                        w = (b + 1) * P
                        act.wait_ge(c_pt_ps, k * n + s)
                        act.nop(nofuse=True)
                        nc.scalar.copy(probs_t[:, (s - 1) % 2, 0:w], ps[:, PT + (s - 1) % 2, 0:w]
                                       ).then_inc(c_pt_sb, 1)
                    if s >= H + 3 and (s - 3) % H == 0:
                        b = (s - 3) // H - 1
                        act.wait_ge(c_ot_ps, k * NB + (b + 1))
                        act.nop(nofuse=True)
                        nc.scalar.copy(attended_t[:].rearrange("x g c -> x (g c)"), ps[:, MISC, :]
                                       ).then_inc(c_ot_sb, 1)
                    if s >= H + 5 and (s - 5) % H == 0:
                        b = (s - 5) // H - 1
                        act.wait_ge(c_y_sb, k * NB + (b + 1))
                        act.dma_start(out[bass.ds(k, 1), b * P:(b + 1) * P, :].rearrange("o p e -> (o p) e"),
                                      result[:, b, :]).then_inc(c_stored[b], 16)

            def repair_row(n):
                act.wait_ge(r_var, n + 1)
                act.nop(nofuse=True)
                nc.scalar.activation(ln2[:, 1], ln2[:, 0], ACT.Sqrt).then_inc(r_std, 1)
                act.wait_ge(r_t_ps, n + 1)
                act.nop(nofuse=True)
                nc.scalar.copy(r_norm_t, ps[0:E, MISC, :]).then_inc(r_t_sb, 1)

            def repair_head(hd, n):
                act.wait_ge(r_side_ps, n + 1)
                act.nop(nofuse=True)
                for s in range(SIDES):
                    last = nc.scalar.copy(sides[:, s, D:H, :],
                                          ps[:, MISC, :].rearrange("x (b s k) -> x b s k", b=NB, s=SIDES)[:, :, s])
                last.then_inc(r_side_sb, 1)
                act.wait_ge(r_best, n + 1)
                act.nop(nofuse=True)
                nc.scalar.activation(weight_in[:, D:H], weight_in[:, D:H], ACT.Exp).then_inc(r_wexp, 1)
                act.wait_ge(r_kt_ps, n + 1)
                act.nop(nofuse=True)
                half = slice((hd % 2) * E, (hd % 2 + 1) * E)
                nc.scalar.copy(kt[half, hd // 2, :], ps[0:E, MISC, :]).then_inc(r_kt_sb, 1)

            def row(k, more):
                if more:
                    load_row(k + 1, row_ln[:], c_ln_in)
                load_row(k, row_add[:], c_add_in)
                project_queries(k)
                for hd in range(D):
                    split_pair(k, hd)
                if more:
                    norm_and_transpose(k + 1)
                for c in range(STEPS + 14):
                    b, j = divmod(c, QUARTER)
                    if c < STEPS:
                        exponentials(k, c)
                        for s in range(2 * j, 2 * j + 2):
                            weigh(k, b, s // TOP, s % TOP)
                    if more and c < STEPS and j == 1:
                        score_sides(k + 1, b)
                    if more and c < STEPS and j == 24:
                        weights(k + 1, b)
                    if c < STEPS and c % CH == 21:
                        spread_sums(k, c // CH)
                    if c >= CH and c % CH == 7:
                        transpose_values(k, c // CH - 1)
                    if c >= QUARTER and j == 13:
                        transpose_keys(k, b - 1)
                repair(act, k, counts, repair_row, repair_head)
                attention(k)

            counts = repair_counts(act)
            load_row(0, row_ln[:], c_ln_in)
            norm_and_transpose(0)
            for b in range(NB):
                score_sides(0, b)
                weights(0, b)
            with act.Fori(0, R - 1) as k:
                row(k, True)
            row(R - 1, False)
            for b in range(NB):
                act.wait_ge(c_stored[b], 16 + 16 * R)

        @block.vector
        def _(dve):
            tt, ts, red = nc.vector.tensor_tensor, nc.vector.tensor_scalar, nc.vector.tensor_reduce
            drain = nc.vector.drain
            dve.wait_ge(const_made, 7)
            nc.vector.tensor_copy(cell_no[:], cell_i[:])
            nc.vector.tensor_copy(head_base[:], head_i[:])
            drain().then_inc(a_raw_free, 2)
            drain().then_inc(a_shifted, 2)

            with dve.Fori(0, R // 2) as r2:
                for u in range(2):
                    scores = ps[:, 4 * u + 2:4 * u + 4, :].rearrange("x s (b c) -> x (s b) c", c=256)
                    dve.wait_ge(a_scores, r2 * 2 + (u + 1))
                    dve.nop(nofuse=True)
                    gmax = group_max[:, u].rearrange("x (b g) -> x b g", b=NB)
                    red(gmax, scores.rearrange("x b (q g) -> x b g q", q=POOL), AX.X, ALU.max)
                    drain()
                    tt(shifted[:, u].rearrange("x (b q g) -> x b q g", b=NB, q=POOL),
                       scores.rearrange("x b (q g) -> x b q g", q=POOL),
                       gmax.unsqueeze(2).to_broadcast([P, NB, POOL, E]), ALU.subtract).then_inc(a_shifted, 1)
                for u in range(2):
                    dve.wait_ge(a_exp, r2 * 2 + (u + 1))
                    dve.nop(nofuse=True)
                    gden = group_den[:, u].rearrange("x (b g) -> x b g", b=NB)
                    gnum = group_num[:, u].rearrange("x (b g) -> x b g", b=NB)
                    red(gden, expd[:, u].rearrange("x (b q g) -> x b g q", b=NB, q=POOL), AX.X, ALU.add)
                    drain()
                    nc.vector.reciprocal(gden, gden)
                    dve.wait_ge(a_weighted, r2 * 2 + (u + 1))
                    dve.nop(nofuse=True)
                    red(gnum, weighted[:, u].rearrange("x (b q g) -> x b g q", b=NB, q=POOL), AX.X, ALU.add
                        ).then_inc(a_raw_free, 1)
                    drain()
                    tt(pooled[:, r2 * 2 + u, :, :], gnum, gden, ALU.mult)
            drain().then_inc(done_a, 1)

            def wide(v, shape, axis):
                return v.unsqueeze(axis).to_broadcast(shape)

            with dve.Fori(0, NB) as cb:
                src = pooled[:, :, bass.ds(cb, 1), :].rearrange("x r o e -> x r (o e)")
                red(ln_a, src, AX.X, ALU.add)
                drain()
                ts(ln_a, ln_a, 1.0 / E, None, ALU.mult)
                drain()
                tt(normed[:], src, wide(ln_a, [P, R, E], 2), ALU.subtract)
                drain()
                tt(squares, normed[:], normed[:], ALU.mult)
                drain()
                red(ln_a, squares, AX.X, ALU.add)
                drain()
                ts(ln_a, ln_a, 1.0 / E, EPS, ALU.mult, ALU.add).then_inc(b_var, 1)
                dve.wait_ge(b_std, cb + 1)
                dve.nop(nofuse=True)
                nc.vector.reciprocal(ln_b, ln_b)
                drain()
                tt(normed[:], normed[:], wide(ln_b, [P, R, E], 2), ALU.mult).then_inc(b_normed, 1)
                for g in range(8):
                    dve.wait_ge(b_qkv_ps, cb * 8 + (g + 1))
                    dve.nop(nofuse=True)
                    bank = 2 + 2 * (g % 2)
                    for t in range(3):
                        for s in range(2):
                            r0 = 4 * g + 2 * s
                            last = tt(qkv[:, t, :, r0:r0 + 2, :].rearrange("x h r d -> x r h d"),
                                      ps[:, bank + s, 0:384].rearrange("x (i t h d) -> x i t h d", i=2, t=3, h=H)
                                      [:, :, t],
                                      bqkv_s[:, t * E:(t + 1) * E].rearrange("x (h d) -> x h d", h=H)
                                      .unsqueeze(1).to_broadcast([P, 2, H, HD]), ALU.add)
                    last.then_inc(b_qkv_sb, 1)
                drain()
                keys = qkv[:, 1].rearrange("x h r d -> x h (r d)")
                red(k_headmax, qkv[:, 1].rearrange("x h r d -> x (r d) h"), AX.X, ALU.max).then_inc(b_headmax, 1)
                queries = qkv[:, 0].rearrange("x h r d -> x h (r d)")
                red(q_max, queries, AX.X, ALU.max)
                drain()
                tt(queries, queries, wide(q_max, [P, H, R * HD], 2),
                   ALU.subtract).then_inc(b_qshift, 1)
                dve.wait_ge(b_headmax_t, cb + 1)
                dve.nop(nofuse=True)
                red(max_t, ps[:, 6, 0:256].rearrange("x (m f c) -> x m f c", m=2, f=2), AX.X, ALU.max)
                drain()
                tt(diag_max.rearrange("x m f c -> x (m f) c"), wide(ident[:], [P, 4, P], 1),
                   wide(max_t.rearrange("x m f -> x (m f)"), [P, 4, P], 2), ALU.mult).then_inc(b_diag, 1)
                dve.wait_ge(b_kmax, cb + 1)
                dve.nop(nofuse=True)
                tt(keys, keys, wide(ps[:, 7, 0:256], [P, H, R * HD], 1),
                   ALU.subtract).then_inc(b_kshift, 1)
                dve.wait_ge(b_qexp, cb + 1)
                dve.nop(nofuse=True)
                red(q_sum, queries, AX.X, ALU.add)
                drain()
                nc.vector.reciprocal(q_sum, q_sum)
                drain()
                tt(queries, queries, wide(q_sum, [P, H, R * HD], 2),
                   ALU.mult).then_inc(b_qnormed, 1)
                dve.wait_ge(b_ctx_ps, cb + 1)
                dve.nop(nofuse=True)
                for f in range(2):
                    nc.vector.reciprocal(k_rsum[:, 2 * f:2 * f + 2], ps[:, [2, 7][f], 0:2])
                drain()
                for f in range(2):
                    for m in range(2):
                        last = ts(context[:, f, m, :], ps[:, f, m * 256:(m + 1) * 256],
                                  k_rsum[:, 2 * f + m:2 * f + m + 1], float(R * HD) ** 0.5, ALU.mult, ALU.mult)
                last.then_inc(b_ctx_sb, 1)
                dve.wait_ge(b_out_ps, cb + 1)
                dve.nop(nofuse=True)
                for f in range(2):
                    for b in range(NB):
                        bank = [[0, 1], [2, 7]][f][b // 2]
                        lo = cb * (2 * HD) + f * HD
                        tt(tokens[:, :, b, bass.ds(lo, HD)],
                           ps[:, bank, (b % 2) * 256:(b % 2 + 1) * 256].rearrange("x (r d) -> x r d", r=R),
                           pooled[:, :, b, bass.ds(lo, HD)], ALU.add)
            drain().then_inc(done_b, 3)
            drain().then_inc(c_gather_used, 2 * G)
            drain().then_inc(c_mm, 2 * PIECE)
            for b in range(NB):
                drain().then_inc(c_stored[b], 16)
            drain().then_inc(c_side_used, 1)

            dve.wait_ge(b_kept, 16)

            def layer_norm(k):
                dve.wait_ge(c_ln_in, k * 16 + 16)
                normalise(row_ln, c_var, c_std, k, c_normed)

            def normalise(src, var, std, n, normed):
                mean = ln2[:, 0]
                red(mean, src[:], AX.X, ALU.add)
                drain()
                ts(mean, mean, 1.0 / E, None, ALU.mult)
                drain()
                tt(normed2[:], src[:], wide(mean, [P, NB, E], 2), ALU.subtract)
                drain()
                tt(sq2[:], normed2[:], normed2[:], ALU.mult)
                drain()
                red(mean, sq2[:], AX.X, ALU.add)
                drain()
                ts(mean, mean, 1.0 / E, EPS, ALU.mult, ALU.add).then_inc(var, 1)
                dve.wait_ge(std, n + 1)
                nc.vector.reciprocal(ln2[:, 1], ln2[:, 1])
                drain()
                tt(normed2[:], normed2[:], wide(ln2[:, 1], [P, NB, E], 2), ALU.mult).then_inc(normed, 1)

            def replace(lists, rest, largest, values):
                for at in lists:
                    nc.vector.match_replace(out=rest[(slice(None),) + at], imm_value=LOWEST,
                                            in_to_replace=largest[(slice(None),) + at][:, 0:8],
                                            in_values=values[(slice(None),) + at])

            def choose(k, b, n, repaired=None):
                first = D if repaired is not None else 0
                heads = slice(first, H)
                side = [[(s, h) for h in range(first, H)] for s in range(SIDES)]
                if n == 0 and repaired is None:
                    dve.wait_ge(c_side_sb, k * NB + (b + 2))
                    dve.nop(nofuse=True)
                if n in (0, 1):
                    for s, h in side[n]:
                        nc.vector.max(top[:, s, h, 0:8], sides[:, s, h, :])
                elif n in (2, 3):
                    if n == 2:
                        drain()
                    replace(side[n - 2], sides_rest, top, sides)
                elif n == 4:
                    for s in range(SIDES):
                        for g in range(G):
                            last = nc.vector.max_index(top_at[:, s, g, 0:8], top[:, s, D + g, 0:8],
                                                       sides[:, s, D + g, :])
                    if repaired is None:
                        last.then_inc(c_side_used, 1)
                elif n in (5, 6):
                    if n == 5:
                        drain()
                    for s, h in side[n - 5]:
                        nc.vector.max(top[:, s, h, 8:16], sides_rest[:, s, h, :])
                elif n == 7:
                    drain()
                    for s in range(SIDES):
                        for g in range(G):
                            nc.vector.max_index(top_at[:, s, g, 8:16], top[:, s, D + g, 8:16],
                                                sides_rest[:, s, D + g, :])
                elif n == 8:
                    drain()
                    if repaired is None:
                        tt(code[:, 0], top_at[:, 0], head_base[:], ALU.add)
                    else:
                        ts(code[:, 0], top_at[:, 0], float(repaired * NKV), None, ALU.add)
                    ts(code[:, 1], top_at[:, 1], float(NK), None, ALU.mult)
                elif n in (9, 10):
                    drain()
                    at = 0
                    nh = H - first if n == 9 else G
                    out_, in_ = (cand[:, heads], top[:, :, heads]) if n == 9 else (cand_code, code)
                    for i0, ni, nj in CELLS:
                        tt(out_[:, :, at:at + ni * nj].rearrange("x h (i j) -> x h i j", i=ni),
                           in_[:, 0, :, i0:i0 + ni].unsqueeze(3).to_broadcast([P, nh, ni, nj]),
                           in_[:, 1, :, 0:nj].unsqueeze(2).to_broadcast([P, nh, ni, nj]), ALU.add)
                        at += ni * nj
                elif n == 11:
                    drain()
                    for h in range(first, H):
                        nc.vector.max(best[:, h, 0:8], cand[:, h, :])
                elif n == 12:
                    drain()
                    replace([(h,) for h in range(first, H)], cand_rest, best, cand)
                elif n == 13:
                    for g in range(G):
                        nc.vector.max_index(best_at[:, g, 0:8], best[:, D + g, 0:8], cand[:, D + g, :])
                    drain()
                    for h in range(first, H):
                        nc.vector.max(best[:, h, 8:16], cand_rest[:, h, :])
                elif n == 14:
                    drain()
                    for g in range(G):
                        nc.vector.max_index(best_at[:, g, 8:16], best[:, D + g, 8:16], cand_rest[:, D + g, :])
                    if repaired is None:
                        red(size[:], top[:, :, 0:D, 0:TOP:TOP - 1].rearrange("x s h t -> x h s t"), AX.XY,
                            ALU.add, apply_absolute_value=True)
                    nc.vector.tensor_copy(base[:, D:H], best[:, D:H, 0])
                    drain()
                    nc.vector.tensor_copy(best_atf[:], best_at[:])
                elif n == 15 and repaired is None:
                    nc.vector.scalar_tensor_tensor(out=base[:, 0:D], in0=size[:], scalar=-SLACK,
                                                   in1=best[:, 0:D, TOP - 1], op0=ALU.mult, op1=ALU.add)
                    drain()
                    ts(neg_thr[:, :, b], base[:, 0:D], -1.0, None, ALU.mult)
                elif n == 16:
                    tt(weight_in[:, heads], best[:, heads], wide(base[:, heads], [P, H - first, TOP], 2),
                       ALU.subtract).then_inc(c_best if repaired is None else r_best, 1)
                elif n >= 17:
                    g, m = divmod(n - 17, 3)
                    if m == 0:
                        drain()
                        tt(onehot[:], best_atf[:, g, :].unsqueeze(2).to_broadcast([P, TOP, NC_]),
                           wide(cell_no[:], [P, TOP, NC_], 1), ALU.is_equal)
                    elif m == 1:
                        drain()
                        tt(onehot[:], onehot[:], wide(cand_code[:, g, :], [P, TOP, NC_], 1), ALU.mult)
                    else:
                        drain()
                        red(best_code[:, g, :], onehot[:], AX.X, ALU.add)

            CHOICES = 17 + 3 * G

            def settle(k, b):
                dve.wait_ge(c_wexp, k * NB + (b + 1))
                red(weight_sum[:], weight_in[:], AX.X, ALU.add)
                drain()
                nc.vector.tensor_copy(chosen_sum[:, 1, :, b], weight_sum[:, 0:D])
                drain()
                nc.vector.reciprocal(weight_sum[:], weight_sum[:])
                drain()
                tt(weight[:, b], weight_in[:, D:H], wide(weight_sum[:, D:H], [P, G, TOP], 2), ALU.mult)
                nc.vector.tensor_copy(rsum_next[:, :, b], weight_sum[:, 0:D])
                drain()
                nc.vector.tensor_copy(rows[:, b], best_code[:].rearrange("x h s -> x (h s)")).then_inc(c_rows, 1)

            def add_up(k, b, g, t):
                src = gathered[:, b % 2, g, :, t * E:(t + 1) * E].rearrange("x s d -> x d s")
                if t == 0:
                    dve.wait_ge(c_scaled, k * (NB * G) + (b * G + g + 1))
                    red(kk[:, b, g, :], src, AX.X, ALU.add)
                else:
                    red(vv[:, b, D + g, :], src, AX.X, ALU.add).then_inc(c_gather_used, 1)
                    if g == G - 1:
                        drain().then_inc(c_kv, 1)

            def spread(k, hd, v):
                tt(diag[:, hd % 2], wide(ident[:], [P, NB, P], 1), wide(v[:, hd, :], [P, NB, P], 2), ALU.mult
                   ).then_inc(c_diag, 1)

            def split_pairs(k):
                nc.vector.tensor_copy(rsum[:], rsum_next[:])
                nc.vector.tensor_copy(chosen_sum[:, 0], chosen_sum[:, 1])
                spread(k, 0, neg_thr)
                spread(k, 1, neg_thr)
                for hd in range(D):
                    dve.wait_ge(c_part1, k * D + (hd + 1))
                    tt(expo[:, hd % 2, :], ps[:, U + hd % 2, :], parts[:, hd, 0, :], ALU.subtract
                       ).then_inc(c_rest1, 1)
                    if hd + 2 < D:
                        spread(k, hd + 2, neg_thr)
                    dve.wait_ge(c_part2, k * D + (hd + 1))
                    tt(parts[:, hd, 2, :], expo[:, hd % 2, :], parts[:, hd, 1, :], ALU.subtract
                       ).then_inc(c_parts, 1)

            def select(k, c):
                dve.wait_ge(c_expo, k * STEPS + (c + 1))
                if c >= 3:
                    dve.wait_ge(c_mm, k * STEPS + (2 * PIECE + c - 2))
                nc.vector.scalar_tensor_tensor(out=dense_w[:, c % 3, :], in0=expo[:, c % 3, :], scalar=1.0,
                                               in1=expo[:, c % 3, :], op0=ALU.is_ge, op1=ALU.mult,
                                               accum_out=dense_sum[:, c:c + 1]).then_inc(c_w, 1)

            def check_sums(k, part):
                if part == 0:
                    drain()
                    red(sums[:, 0], dense_sum[:].rearrange("x (h c) -> x h c", h=D), AX.X, ALU.add)
                    red(sums[:, 1], chosen_sum[:, 0], AX.X, ALU.add).then_inc(c_sums, 1)
                else:
                    dve.wait_ge(c_sums_ps, k + 1)
                    nc.vector.tensor_copy(checks[:, 0:2].rearrange("x t h -> x (t h)"), ps[0:1, SIM + 1, 0:2 * D])
                    drain()
                    tt(checks[:, 0], checks[:, 0], checks[:, 1], ALU.subtract)
                    ts(checks[:, 2], checks[:, 1], SUM_LIMIT, None, ALU.is_lt)
                    drain()
                    tt(checks[:, 0], checks[:, 0], checks[:, 0], ALU.mult)
                    drain()
                    ts(checks[:, 0], checks[:, 0], SUM_ERROR ** 2, None, ALU.is_lt)
                    drain()
                    tt(checks[:, 2], checks[:, 2], checks[:, 0], ALU.mult)
                    drain()
                    red(checks[:, 1, 0:1], checks[:, 2], AX.X, ALU.min)
                    dve.wait_ge(c_flags_read, k * READERS + 2)
                    ts(flags[:, 0:D], checks[:, 2], 0.5, None, ALU.is_lt)
                    drain()
                    ts(flags[:, D:D + 1], checks[:, 1, 0:1], 0.5, None, ALU.is_lt).then_inc(c_flags, 1)

            def repair_row(n):
                dve.nop(nofuse=True)
                normalise(row_add, r_var, r_std, n, r_normed)

            def repair_head(hd, n):
                dve.wait_ge(r_side_sb, n + 1)
                dve.nop(nofuse=True)
                for part in range(CHOICES):
                    choose(None, None, part, repaired=hd)
                drain()
                nc.vector.tensor_copy(r_rows[:], best_code[:].rearrange("x h s -> x (h s)")).then_inc(r_rows_out, 1)
                dve.wait_ge(r_wexp, n + 1)
                dve.nop(nofuse=True)
                red(weight_sum[:, D:H], weight_in[:, D:H], AX.X, ALU.add)
                drain()
                nc.vector.reciprocal(weight_sum[:, D:H], weight_sum[:, D:H])
                drain()
                tt(r_weight[:], weight_in[:, D:H], wide(weight_sum[:, D:H], [P, G, TOP], 2), ALU.mult)
                for b in range(NB):
                    dve.wait_ge(r_landed[b], n * (TOP * 16) + TOP * 16)
                    dve.nop(nofuse=True)
                    drain()
                    tt(gathered[:, 0, b], gathered[:, 0, b], wide(r_weight[:, b], [P, TOP, KV], 2), ALU.mult)
                    drain()
                    red(kk[:, b, 0, :], gathered[:, 0, b, :, 0:E].rearrange("x s d -> x d s"), AX.X, ALU.add)
                    red(vv[:, b, hd, :], gathered[:, 0, b, :, E:KV].rearrange("x s d -> x d s"), AX.X, ALU.add)
                drain().then_inc(r_kv, 1)

            def finish_dense(k, hd):
                keys, vals = (slice(0, E), slice(E, P)) if hd % 2 == 0 else (slice(E, P), slice(0, E))
                dve.wait_ge(c_mm, k * STEPS + (2 * PIECE + CH * (hd + 1)))
                dve.wait_ge(c_rsum_sb, k * D + (hd + 1))
                tt(kt[keys, hd // 2, :], ps[keys, ACC + hd % 2, :], rsum_wide[keys, :], ALU.mult)
                if hd > 0:
                    dve.wait_ge(c_vt_ps, k * D + hd)
                tt(v_dense[vals, :], ps[vals, ACC + hd % 2, :], rsum_wide[vals, :], ALU.mult).then_inc(c_dense, 1)

            def attention(k):
                steps = [(b, h) for b in range(NB) for h in range(H)]
                n = len(steps)
                for s in range(n + 5):
                    if s < n:
                        b, h = steps[s]
                        dve.wait_ge(c_sim, k * n + (s + 1))
                        red(neg_max[:, s % 4:s % 4 + 1], ps[:, SIM + s % 2, 0:(b + 1) * P], AX.X, ALU.max,
                            negate=True).then_inc(c_max, 1)
                    if s >= H + 2 and (s - 2) % H == 0:
                        b = (s - 2) // H - 1
                        dve.wait_ge(c_o_ps, k * NB + (b + 1))
                        nc.vector.reciprocal(rden[:], den[:, b % 2, :])
                        drain()
                        tt(attended[:], ps[:, O, :].rearrange("x (h d) -> x h d", h=H),
                           wide(rden[:], [P, H, E], 2), ALU.mult).then_inc(c_o_sb, 1)
                    if s >= H + 4 and (s - 4) % H == 0:
                        b = (s - 4) // H - 1
                        dve.wait_ge(c_y_ps, k * NB + (b + 1))
                        dve.wait_ge(c_stored[b], k * 16 + 16)
                        tt(result[:, b, :], ps[:, MISC, 0:E], row_add[:, b, :], ALU.add).then_inc(c_y_sb, 1)

            def row(k, more):
                split_pairs(k)
                if more:
                    layer_norm(k + 1)
                for c in range(STEPS + 14):
                    b, j = divmod(c, QUARTER)
                    if c < STEPS:
                        select(k, c)
                    for h in range(G):
                        at = QUARTER // G * (h + 1)
                        for t in range(2):
                            if (c - at - 1 - 4 * t) % QUARTER == 0 and 0 <= (c - at - 1 - 4 * t) // QUARTER < NB:
                                add_up(k, (c - at - 1 - 4 * t) // QUARTER, h, t)
                    if c >= CH and c % CH == 3 and c // CH <= D:
                        finish_dense(k, c // CH - 1)
                    if more and c >= QUARTER and j == 3 and b <= NB:
                        settle(k + 1, b - 1)
                    if more and c < STEPS and 3 <= j:
                        choose(k + 1, b, j - 3)
                    if c < STEPS and c % CH == 12:
                        spread(k, c // CH, rsum)
                    if c in (STEPS + 1, STEPS + 6):
                        check_sums(k, c // (STEPS + 6))
                dve.wait_ge(c_add_in, k * 16 + 16)
                dve.nop(nofuse=True)
                repair(dve, k, counts, repair_row, repair_head)
                attention(k)

            counts = repair_counts(dve)
            dve.nop(nofuse=True).then_inc(c_flags_read, 2)
            layer_norm(0)
            for b in range(NB):
                for n in range(CHOICES):
                    choose(0, b, n)
                settle(0, b)
            with dve.Fori(0, R - 1) as k:
                row(k, True)
            row(R - 1, False)


def kernel(**inputs):
    import concourse.bacc as bacc
    from concourse.bass_utils import run_bass_kernel_spmd

    def arr(name):
        return np.asarray(inputs[name])

    arrays = {
        "x": arr("x"),
        "keysvals": np.concatenate([arr("L0_ffn_keys_table"), arr("L0_ffn_values_table")], axis=1),
        "tables": np.stack([
            np.concatenate([t[h * NKV:(h + 1) * NKV] for t in
                            ((arr("L0_ffn_keys_table"), arr("L0_ffn_values_table")) if h % 2 == 0 else
                             (arr("L0_ffn_values_table"), arr("L0_ffn_keys_table")))], axis=1)
            .reshape(CH, P, KV).transpose(1, 0, 2) for h in range(D)]),
        "w_tok": arr("L0_tok_W"),
        "w_qkv": np.concatenate([arr("L0_attn_Wq").T, arr("L0_attn_Wk").T, arr("L0_attn_Wv").T], axis=1),
        "b_qkv": np.concatenate([arr("L0_attn_bq"), arr("L0_attn_bk"), arr("L0_attn_bv")])[None, :],
        "wqpk_t": arr("L0_ffn_Wq_pk").T,
        "pk_t": arr("L0_ffn_pk_keys").transpose(0, 2, 3, 1).reshape(SIDES * H * DK, NK),
        "w_q": arr("L0_ffn_Wq"),
        "w_o": arr("L0_ffn_Wo"),
    }
    arrays = {n: np.ascontiguousarray(a) for n, a in arrays.items()}
    nc = bacc.Bacc("TRN2", target_bir_lowering=False, num_devices=1)
    args = [nc.dram_tensor(n, a.shape, F32, kind="ExternalInput").ap() for n, a in arrays.items()]
    out = nc.dram_tensor("out", (R, N, E), F32, kind="ExternalOutput").ap()
    kept = nc.dram_tensor("kept", (R, P, NB * E), F32, kind="Internal").ap()
    build(nc, *args, kept, out)
    return run_bass_kernel_spmd(nc, [arrays], core_ids=[0]).results[0]["out"]
```

```python
from contextlib import ExitStack

import concourse.bass as bass
import numpy as np
from concourse import mybir
from concourse.alu_op_type import AluOpType as ALU

F32 = mybir.dt.float32
U32 = mybir.dt.uint32
I32 = mybir.dt.int32
ACT = mybir.ActivationFunctionType
AX = mybir.AxisListType

P = 128
R, N, E, POOL = 32, 512, 64, 4
H = 8
HD = E // H
NB = N // P
NK, TOP, DK = 64, 16, 32
SIDES = 2
NKV = NK * NK
KV = 2 * E
EPS = 1e-5
LOWEST = -3.4028235e38
MASKED = -1e30
D, G = 4, 4
CH = NKV // P
PIECE = 8
STEPS = D * CH
QUARTER = STEPS // NB
SLACK = 2.0 ** -23
SUM_ERROR = 0.25
SUM_LIMIT = 2.5e5
BF16 = mybir.dt.bfloat16
CELLS = [(0, 1, 16), (1, 1, 8), (2, 2, 5), (4, 4, 3), (8, 8, 1)]
NC_ = sum(ni * nj for _, ni, nj in CELLS)
READERS = 4
ATTEND = NB * H
BUFS, WBUFS = 4, 8
LAG = 4
AHEAD = 1
WRAP = 17
CHOICES = 17 + 3 * G
CHOOSE = [16 + CHOICES * b for b in range(NB)]
PAIR = [STEPS - 6, STEPS - 3, STEPS, STEPS + 3]
KEYS = [47, 79, 111, STEPS + 5]
QUERY = [105, 107, 109, 118]
PAIRS_BEFORE = sum(p < STEPS for p in PAIR) - 1
HAND = STEPS - 15
HAND_REST = STEPS + 9
SUMS, REPAIR = STEPS + 6, STEPS + 10
NEXT_SUMS = CHOOSE[-1] + CHOICES + 1
KEEP = 11
AT = {16 + 11 * s // 4: s for s in range(ATTEND + 6)}


def build(nc, x, keysvals, tables, w_tok, w_qkv, b_qkv, wqpk_t, pk_t, w_q, w_o, kept, out):
    ctx = ExitStack()
    with ctx:
        def sb(name, shape, dt=F32):
            return ctx.enter_context(nc.sbuf_tensor(name, shape, dt))

        def sem(name):
            return ctx.enter_context(nc.semaphore(name))

        arena = sb("arena", [P, 31872])
        tokens = arena[:, 0:8192].rearrange("x (r b e) -> x r b e", r=R, b=NB)
        parts = arena[:, 0:3072].bitcast(BF16).rearrange("x (h t n) -> x h t n", h=D, t=3)
        table = arena[:, 3072:5120].rearrange("x (u c d) -> x u c d", u=2, c=PIECE)
        expo = arena[:, 5120:7168].rearrange("x (u n) -> x u n", u=BUFS)
        rest = arena[:, 7168:8192].rearrange("x (u n) -> x u n", u=2)

        pooled = arena[:, 8192:16384].rearrange("x (r b e) -> x r b e", r=R, b=NB)
        gathered = arena[:, 8192:16384].rearrange("x (h s d) -> x h s d", h=G, s=TOP)
        work = arena[:, 16384:31872]
        group_max = work[:, 10240:10752].rearrange("x (u c) -> x u c", u=2)
        group_den = work[:, 10752:11264].rearrange("x (u c) -> x u c", u=2)
        group_num = work[:, 11264:11776].rearrange("x (u c) -> x u c", u=2)
        wqpk_s = work[:, 11776:12032].rearrange("x (a e) -> x a e", a=4)
        pk_s = work[:, 12032:12288].rearrange("x (a e) -> x a e", a=4)
        raw = work[:, 0:2048].rearrange("x (u c) -> x u c", u=2)
        raw_t = work[:, 2048:4096].rearrange("x (u c) -> x u c", u=2)
        shifted = work[:, 4096:6144].rearrange("x (u c) -> x u c", u=2)
        expd = work[:, 6144:8192].rearrange("x (u c) -> x u c", u=2)
        weighted = work[:, 8192:10240].rearrange("x (u c) -> x u c", u=2)
        q_t = work[:, 0:2048].rearrange("x (m c h) -> x m c h", m=2, c=P)
        context = work[:, 2048:3072].rearrange("x (f m e) -> x f m e", f=2, m=2)
        norm_t = work[:, 3072:4096].rearrange("x (u c) -> x u c", u=2)
        k_headmax = work[:, 4096:4352]
        diag_max = work[:, 4352:4864].rearrange("x (m f c) -> x m f c", m=2, f=2)
        squares = work[:, 4864:6912].rearrange("x (r e) -> x r e", r=R)
        ln_a = work[:, 7168:7200]
        ln_b = work[:, 7200:7232]
        max_t = work[:, 7232:7236].rearrange("x (m f) -> x m f", m=2)
        q_max = work[:, 7240:7248]
        q_sum = work[:, 7248:7256]
        k_rsum = work[:, 7256:7260]
        qkv = work[:, 7296:13440].rearrange("x (t h r d) -> x t h r d", t=3, h=H, r=R)
        normed = work[:, 13440:15488].rearrange("x (r e) -> x r e", r=R)
        qt = work[:, 0:2048].rearrange("x (g n) -> x g n", g=4)
        kt = work[:, 2048:4096].rearrange("x (g n) -> x g n", g=4)
        vv = work[:, 4096:6144].rearrange("x (b h d) -> x b h d", b=NB, h=H)
        kt_next = work[:, 6144:8192].rearrange("x (g n) -> x g n", g=4)
        vv_next = work[:, 8192:10240].rearrange("x (b h d) -> x b h d", b=NB, h=H)
        kk = work[:, 10240:11264].rearrange("x (b h d) -> x b h d", b=NB, h=G)
        probs = work[:, 11264:12288].rearrange("x (u c) -> x u c", u=2)
        probs_t = work[:, 12288:13312].rearrange("x (u c) -> x u c", u=2)
        sides = work[:, 13312:14336].rearrange("x (s h k) -> x s h k", s=SIDES, h=H)
        sides_rest = work[:, 14336:15360].rearrange("x (s h k) -> x s h k", s=SIDES, h=H)

        top = sb("top", [P, SIDES, H, TOP])
        top_at = sb("top_at", [P, SIDES, G, TOP], U32)
        code = sb("code", [P, SIDES, G, TOP])
        cand = sb("cand", [P, H, NC_])
        cand_code = sb("cand_code", [P, G, NC_])
        cand_rest = sb("cand_rest", [P, H, NC_])
        best = sb("best", [P, H, TOP])
        best_at = sb("best_at", [P, G, TOP], U32)
        best_atf = sb("best_atf", [P, G, TOP])
        onehot = sb("onehot", [P, TOP, NC_])
        best_code = sb("best_code", [P, G, TOP])
        rows = sb("rows", [P, NB, G * TOP], U32)
        size = sb("size", [P, D])
        base = sb("base", [P, H])
        weight_in = sb("weight_in", [P, H, TOP])
        weight_sum = sb("weight_sum", [P, H])
        weight = sb("weight", [P, NB, G, TOP])
        neg_thr = sb("neg_thr", [P, D, NB])
        rsum = sb("rsum", [P, D, NB])
        rsum_next = sb("rsum_next", [P, D, NB])
        dense_sum = sb("dense_sum", [P, STEPS])
        sums = sb("sums", [P, 2, D])
        chosen_sum = sb("chosen_sum", [P, 2, D, NB])
        checks = sb("checks", [1, 3, D])
        flags = sb("flags", [1, 2 * D], I32)
        r_weight = sb("r_weight", [P, NB, TOP])
        r_rows = sb("r_rows", [P, NB * TOP], U32)
        row_ln = sb("row_ln", [P, NB, E])
        row_add = sb("row_add", [P, NB, E])
        normed2 = sb("normed2", [P, NB, E])
        sq2 = sb("sq2", [P, NB, E])
        ln2 = sb("ln2", [P, 2, NB])
        norm2_t = sb("norm2_t", [E, N])
        norm_now = sb("norm_now", [E, N])
        neg_max = sb("neg_max", [P, 4])
        den = sb("den", [P, 2, H])
        rden = sb("rden", [P, H])
        attended = sb("attended", [P, H, E])
        attended_t = sb("attended_t", [P, 4, P])
        result = sb("result", [P, NB, E])
        dense_w = sb("dense_w", [P, WBUFS, N])
        r_keys = sb("r_keys", [P, NB, E])
        diag = sb("diag", [P, 2, NB, P])
        rsum_wide = sb("rsum_wide", [P, N])
        v_dense = sb("v_dense", [P, N])

        w_tok2 = sb("w_tok2", [P, P])
        wqkv_s = sb("wqkv_s", [E, 3 * E])
        bqkv_s = sb("bqkv_s", [P, 3 * E])
        w_side = sb("w_side", [E, SIDES * H * NK])
        w_pair = sb("w_pair", [E, D, SIDES, NK])
        wq_s = sb("wq_s", [E, H * E])
        wo_s = sb("wo_s", [P, 4, E])
        ident = sb("ident", [P, P])
        ident16 = sb("ident16", [P, P], BF16)
        causal = sb("causal", [P, P], BF16)
        ones = sb("ones", [P, P])
        first_side = sb("first_side", [P, P])
        pick = sb("pick", [P, CH, P], BF16)
        cell_i = sb("cell_i", [P, NC_], I32)
        cell_no = sb("cell_no", [P, NC_])
        head_i = sb("head_i", [P, G, TOP], I32)
        head_base = sb("head_base", [P, G, TOP])

        ps = ctx.enter_context(nc.psum_tensor("ps", [P, 8, 512], F32))
        MISC, SIM, U, ACC, PT, O = 0, 1, 2, 4, 6, 7

        weights_in = sem("weights_in")
        const_made = sem("const_made")
        const_cast = sem("const_cast")
        side_ps = sem("side_ps")
        side_sb = sem("side_sb")
        done_a = sem("done_a")
        done_b = sem("done_b")

        a_raw_in = [sem(f"a_raw_in{u}") for u in range(2)]
        a_raw_free = sem("a_raw_free")
        a_t_ps = sem("a_t_ps")
        a_t_sb = sem("a_t_sb")
        a_scores = sem("a_scores")
        a_shifted = sem("a_shifted")
        a_exp = sem("a_exp")
        a_weighted = sem("a_weighted")
        a_pooled = sem("a_pooled")

        b_var = sem("b_var")
        b_std = sem("b_std")
        b_normed = sem("b_normed")
        b_t_ps = sem("b_t_ps")
        b_t_sb = sem("b_t_sb")
        b_qkv_ps = sem("b_qkv_ps")
        b_qkv_sb = sem("b_qkv_sb")
        b_headmax = sem("b_headmax")
        b_headmax_t = sem("b_headmax_t")
        b_diag = sem("b_diag")
        b_kmax = sem("b_kmax")
        b_kshift = sem("b_kshift")
        b_kexp = sem("b_kexp")
        b_qshift = sem("b_qshift")
        b_qexp = sem("b_qexp")
        b_qnormed = sem("b_qnormed")
        b_ctx_ps = sem("b_ctx_ps")
        b_ctx_sb = sem("b_ctx_sb")
        b_qt_ps = sem("b_qt_ps")
        b_qt_sb = sem("b_qt_sb")
        b_out_ps = sem("b_out_ps")

        c_var = sem("c_var")
        c_std = sem("c_std")
        c_normed = sem("c_normed")
        c_t_ps = sem("c_t_ps")
        c_t_sb = sem("c_t_sb")
        c_q_ps = sem("c_q_ps")
        c_q_sb = sem("c_q_sb")
        c_side_ps = sem("c_side_ps")
        c_side_sb = sem("c_side_sb")
        c_side_used = sem("c_side_used")
        c_best = sem("c_best")
        c_wexp = sem("c_wexp")
        c_rows = sem("c_rows")
        c_landed = [sem(f"c_landed{h}") for h in range(G)]
        c_scaled = sem("c_scaled")
        c_diag = sem("c_diag")
        c_diag_used = sem("c_diag_used")
        c_pair_ps = sem("c_pair_ps")
        c_part1 = sem("c_part1")
        c_rest1 = sem("c_rest1")
        c_part2 = sem("c_part2")
        c_parts = sem("c_parts")
        c_table_in = [sem(f"c_table_in{u}") for u in range(2)]
        c_u = sem("c_u")
        c_expo = sem("c_expo")
        c_w = sem("c_w")
        c_mm = sem("c_mm")
        c_rsum_ps = sem("c_rsum_ps")
        c_rsum_sb = sem("c_rsum_sb")
        c_dense = sem("c_dense")
        c_vt_ps = sem("c_vt_ps")
        c_vt_sb = sem("c_vt_sb")
        b_kept = sem("b_kept")
        c_ln_in = sem("c_ln_in")
        c_add_in = sem("c_add_in")
        c_gather_used = sem("c_gather_used")
        c_kv = sem("c_kv")
        c_kt_ps = sem("c_kt_ps")
        c_kt_sb = sem("c_kt_sb")
        c_sim = sem("c_sim")
        c_max = sem("c_max")
        c_probs = sem("c_probs")
        c_pt_ps = sem("c_pt_ps")
        c_pt_sb = sem("c_pt_sb")
        c_o_ps = sem("c_o_ps")
        c_o_sb = sem("c_o_sb")
        c_ot_ps = sem("c_ot_ps")
        c_ot_sb = sem("c_ot_sb")
        c_y_ps = sem("c_y_ps")
        c_y_sb = sem("c_y_sb")
        c_stored = [sem(f"c_stored{b}") for b in range(NB)]

        c_handed = sem("c_handed")
        c_rsum_set = sem("c_rsum_set")
        c_sums = sem("c_sums")
        c_sums_ps = sem("c_sums_ps")
        c_sums_sb = sem("c_sums_sb")
        c_flags = sem("c_flags")
        c_flags_read = sem("c_flags_read")
        r_side_ps = sem("r_side_ps")
        r_side_sb = sem("r_side_sb")
        r_best = sem("r_best")
        r_wexp = sem("r_wexp")
        r_rows_out = sem("r_rows_out")
        r_landed = [sem(f"r_landed{b}") for b in range(NB)]
        r_used = sem("r_used")
        r_kv = sem("r_kv")
        r_kt_ps = sem("r_kt_ps")
        r_kt_sb = sem("r_kt_sb")

        block = ctx.enter_context(nc.Block())

        def repair(eng, k, repaired, head):
            eng.wait_ge(c_flags, k + 1)
            eng.nop(nofuse=True)
            with eng.If(eng.value_load(flags[0:1, D:D + 1], min_val=0, max_val=1) > 0):
                for hd in range(D):
                    with eng.If(eng.value_load(flags[0:1, hd:hd + 1], min_val=0, max_val=1) > 0):
                        head(hd, eng.snap(repaired))
                        eng.reg_add(repaired, repaired, 1)
            eng.nop(nofuse=True).then_inc(c_flags_read, 1)

        def repaired_heads(eng):
            repaired = eng.alloc_register("repaired_heads")
            eng.reg_mov(repaired, 0)
            return repaired

        @block.sync
        def _(sp):
            sp.wait_ge(const_made, 1)
            sp.dma_start(w_tok2[0:E, 0:E], w_tok).then_inc(weights_in, 16)
            sp.dma_start(w_tok2[E:P, E:P], w_tok).then_inc(weights_in, 16)
            sp.dma_start(wqkv_s[:], w_qkv).then_inc(weights_in, 16)
            sp.dma_start(bqkv_s[:], b_qkv.to_broadcast([P, 3 * E])).then_inc(weights_in, 16)
            sp.dma_start(wqpk_s[:], wqpk_t.rearrange("(a p) e -> p a e", p=P)).then_inc(weights_in, 16)
            sp.dma_start(pk_s[:], pk_t.rearrange("(a p) e -> p a e", p=P)).then_inc(weights_in, 16)
            sp.dma_start(wq_s[:], w_q).then_inc(weights_in, 16)
            sp.dma_start(wo_s[:], w_o.rearrange("(a p) e -> p a e", p=P)).then_inc(weights_in, 16)
            with sp.Fori(0, R // 2) as r2:
                for u in range(2):
                    sp.wait_ge(a_raw_free, r2 * 2 + (u + 1))
                    sp.dma_start(raw[:, u].rearrange("x (b c) -> x b c", b=NB),
                                 x[r2 * 2 + u, :, :].rearrange("(b p q) f -> p b (q f)", b=NB, p=P)
                                 ).then_inc(a_raw_in[u], 16)
            sp.wait_ge(done_b, 3)
            sp.dma_start(kept.rearrange("r p c -> p r c"), arena[:, 0:8192].rearrange("x (r c) -> x r c", r=R)
                         ).then_inc(b_kept, 16)
            sp.wait_ge(b_kept, 16)
            with sp.Fori(0, R) as k:
                for n in range(D * CH // PIECE):
                    sp.wait_ge(c_mm, k * STEPS + PIECE * (n + 1))
                    hd, j = divmod(n, CH // PIECE)
                    sp.dma_start(table[:, n % 2], tables[hd, :, j * PIECE:(j + 1) * PIECE, :]
                                 ).then_inc(c_table_in[n % 2], 16)

        @block.gpsimd
        def _(pool):
            nc.gpsimd.memset(w_tok2[:], 0.0).then_inc(const_made, 1)
            nc.gpsimd.memset(ident[:], 0.0)
            nc.gpsimd.memset(causal[:], 0.0)
            nc.gpsimd.memset(ident16[:], 0.0)
            nc.gpsimd.memset(pick[:], 0.0)
            nc.gpsimd.memset(ones[:], 1.0)
            nc.gpsimd.memset(first_side[:, 0:NK], 1.0)
            nc.gpsimd.memset(first_side[:, NK:P], 0.0)
            nc.gpsimd.iota(cell_i[:], pattern=[[1, NC_]], base=0, channel_multiplier=0)
            nc.gpsimd.iota(head_i[:], pattern=[[NKV, G], [0, TOP]], base=D * NKV,
                           channel_multiplier=0).then_inc(const_made, 1)
            pool.wait_ge(const_made, 2)
            nc.gpsimd.affine_select(out=ident[:], in_=ident[:], compare_op=ALU.not_equal, fill=1.0, base=0,
                                    pattern=[[-1, P]], channel_multiplier=1).then_inc(const_made, 1)
            pool.wait_ge(const_made, 3)
            nc.gpsimd.affine_select(out=ident16[:], in_=ident16[:], compare_op=ALU.not_equal, fill=1.0, base=0,
                                    pattern=[[-1, P]], channel_multiplier=1).then_inc(const_made, 1)
            pool.wait_ge(const_made, 4)
            nc.gpsimd.affine_select(out=pick[0:NK], in_=pick[0:NK], compare_op=ALU.not_equal, fill=1.0, base=0,
                                    pattern=[[0, 2 * CH], [-1, NK]], channel_multiplier=1).then_inc(const_made, 1)
            pool.wait_ge(const_made, 5)
            nc.gpsimd.affine_select(out=pick[NK:P], in_=pick[NK:P], compare_op=ALU.not_equal, fill=1.0, base=0,
                                    pattern=[[-1, 2 * CH], [0, NK]], channel_multiplier=1).then_inc(const_made, 1)
            pool.wait_ge(const_made, 6)
            nc.gpsimd.affine_select(out=causal[:], in_=causal[:], compare_op=ALU.is_ge, fill=MASKED, base=0,
                                    pattern=[[-1, P]], channel_multiplier=1).then_inc(const_made, 1)
            with pool.Fori(0, R // 2) as r2:
                for u in range(2):
                    pool.wait_ge(a_exp, r2 * 2 + (u + 1))
                    pool.nop(nofuse=True)
                    nc.gpsimd.tensor_tensor(weighted[:, u], expd[:, u], raw[:, u], ALU.mult
                                            ).then_inc(a_weighted, 1)
            pool.wait_ge(done_b, 3)
            repaired = repaired_heads(pool)

            def repair_head(hd, n):
                pool.wait_ge(r_rows_out, n + 1)
                pool.nop(nofuse=True)
                for b in range(NB):
                    if b >= 2:
                        pool.wait_ge(r_used, n * NB + (b - 1))
                        pool.nop(nofuse=True)
                    for s in range(TOP):
                        at = b * TOP + s
                        pool.indirect_dma_start(
                            gathered[:, 2 + b % 2, s, :], None, keysvals[:, :],
                            bass.IndirectOffsetOnAxis(ap=r_rows[:, at:at + 1], axis=0)
                        ).then_inc(r_landed[b], 16)
                pool.wait_ge(r_used, n * NB + NB)
                pool.nop(nofuse=True)

            def gather(k, b, h):
                if h == 0:
                    pool.wait_ge(c_rows, k * NB + (b + 1))
                    pool.nop(nofuse=True)
                pool.wait_ge(c_gather_used, k * (NB * G) + (b * G + h + 1))
                pool.nop(nofuse=True)
                for s in range(TOP):
                    at = h * TOP + s
                    pool.indirect_dma_start(
                        gathered[:, h, s, :], None, keysvals[:, :],
                        bass.IndirectOffsetOnAxis(ap=rows[:, b, at:at + 1], axis=0)
                    ).then_inc(c_landed[h], 16)

            def row(k, more):
                for b in range(NB):
                    for h in range(2 if b == 0 else 0, G):
                        gather(k, b, h)
                if more:
                    gather(k + 1, 0, 0)
                    gather(k + 1, 0, 1)
                repair(pool, k, repaired, repair_head)

            gather(0, 0, 0)
            gather(0, 0, 1)
            with pool.Fori(0, R - 1) as k:
                row(k, True)
            row(R - 1, False)

        @block.tensor
        def _(pe):
            pe.wait_ge(const_made, 7)
            pe.wait_ge(weights_in, 16 * 8)
            for a in range(SIDES * H * DK // P):
                for g in range(P // DK):
                    lo = g * DK
                    last = nc.tensor.matmul(ps[0:E, g, a * NK:(a + 1) * NK], wqpk_s[lo:lo + DK, a, :],
                                            pk_s[lo:lo + DK, a, :], start=True, stop=True)
            last.then_inc(side_ps, 1)
            pe.wait_ge(side_sb, 1)

            with pe.Fori(0, R // 2) as r2:
                for u in range(2):
                    pe.wait_ge(a_raw_in[u], r2 * 16 + 16)
                    pe.nop(nofuse=True)
                    for j in range(8):
                        last = nc.tensor.transpose(ps[:, 4 * u + j // 4, (j % 4) * P:(j % 4 + 1) * P],
                                                   raw[:, u, j * P:(j + 1) * P], ident[:])
                    last.then_inc(a_t_ps, 1)
                    pe.wait_ge(a_t_sb, r2 * 2 + (u + 1))
                    pe.nop(nofuse=True)
                    pe.wait_ge(a_shifted, r2 * 2 + (u + 1))
                    pe.nop(nofuse=True)
                    for j in range(8):
                        last = nc.tensor.matmul(ps[:, 4 * u + 2 + j // 4, (j % 4) * P:(j % 4 + 1) * P],
                                                raw_t[:, u, j * P:(j + 1) * P], w_tok2[:],
                                                start=True, stop=True)
                    last.then_inc(a_scores, 1)

            pe.wait_ge(done_a, 1)
            with pe.Fori(0, NB) as cb:
                pe.wait_ge(b_normed, cb + 1)
                pe.nop(nofuse=True)
                for g in range(8):
                    if g >= 2:
                        pe.wait_ge(b_t_sb, cb * 8 + (g - 1))
                        pe.nop(nofuse=True)
                    for i in range(4):
                        last = nc.tensor.transpose(ps[0:E, g % 2, i * P:(i + 1) * P], normed[:, 4 * g + i, :],
                                                   ident[:])
                    last.then_inc(b_t_ps, 1)
                    pe.wait_ge(b_t_sb, cb * 8 + (g + 1))
                    pe.nop(nofuse=True)
                    if g >= 2:
                        pe.wait_ge(b_qkv_sb, cb * 8 + (g - 1))
                        pe.nop(nofuse=True)
                    for i in range(4):
                        o = ps[:, 2 + 2 * (g % 2) + i // 2, (i % 2) * 192:(i % 2 + 1) * 192]
                        last = nc.tensor.matmul(o, norm_t[0:E, g % 2, i * P:(i + 1) * P], wqkv_s[:],
                                                start=True, stop=True)
                    last.then_inc(b_qkv_ps, 1)
                pe.wait_ge(b_headmax, cb + 1)
                pe.nop(nofuse=True)
                for m in range(2):
                    last = nc.tensor.transpose(ps[:, 6, m * P:(m + 1) * P], k_headmax[:, m * P:(m + 1) * P],
                                               ident[:])
                last.then_inc(b_headmax_t, 1)
                pe.wait_ge(b_diag, cb + 1)
                pe.nop(nofuse=True)
                for f in range(2):
                    for m in range(2):
                        last = nc.tensor.matmul(ps[f * E:(f + 1) * E, 7, m * P:(m + 1) * P], ones[:, 0:E],
                                                diag_max[:, m, f, :], start=True, stop=True)
                last.then_inc(b_kmax, 1)
                pe.wait_ge(b_kexp, cb + 1)
                pe.nop(nofuse=True)
                for f in range(2):
                    half = slice(f * E, (f + 1) * E)
                    for m in range(2):
                        for h in range(H):
                            keys = qkv[half, 1, h, 16 * m:16 * (m + 1), :].rearrange("x r d -> x (r d)")
                            nc.tensor.matmul(ps[:, f, m * 256:(m + 1) * 256], keys,
                                             qkv[half, 2, h].rearrange("x r d -> x (r d)"),
                                             start=(h == 0), stop=(h == H - 1))
                        for h in range(H):
                            keys = qkv[half, 1, h, 16 * m:16 * (m + 1), :].rearrange("x r d -> x (r d)")
                            last = nc.tensor.matmul(ps[:, [2, 7][f], m:m + 1], keys, ones[half, 0:1],
                                                    start=(h == 0), stop=(h == H - 1))
                last.then_inc(b_ctx_ps, 1)
                pe.wait_ge(b_qnormed, cb + 1)
                pe.nop(nofuse=True)
                for m in range(2):
                    for hh in range(2):
                        for i in range(4):
                            h = 4 * hh + i
                            last = nc.tensor.transpose(ps[:, 3 + 2 * m + hh, i * P:(i + 1) * P],
                                                       qkv[:, 0, h, 16 * m:16 * (m + 1), :].rearrange("x r d -> x (r d)"),
                                                       ident[:])
                        last.then_inc(b_qt_ps, 1)
                pe.wait_ge(b_qt_sb, cb * 4 + 4)
                pe.nop(nofuse=True)
                pe.wait_ge(b_ctx_sb, cb + 1)
                pe.nop(nofuse=True)
                for f in range(2):
                    for b in range(NB):
                        bank = [[0, 1], [2, 7]][f][b // 2]
                        for m in range(2):
                            lo = f * E + 16 * b
                            last = nc.tensor.matmul(ps[:, bank, (b % 2) * 256:(b % 2 + 1) * 256],
                                                    q_t[:, m, lo:lo + 16, :].rearrange("x c h -> x (c h)"),
                                                    context[:, f, m, :], start=(m == 0), stop=(m == 1))
                last.then_inc(b_out_ps, 1)
            pe.wait_ge(done_b, 3)

            misc_out = []

            def use_misc(out, value):
                if misc_out:
                    pe.wait_ge(*misc_out.pop())
                    pe.nop(nofuse=True)
                misc_out.append((out, value))

            def transpose_tokens(k):
                pe.wait_ge(c_normed, k + 1)
                pe.nop(nofuse=True)
                use_misc(c_t_sb, k + 1)
                for b in range(NB):
                    last = nc.tensor.transpose(ps[0:E, MISC, b * P:(b + 1) * P], normed2[:, b, :], ident[:])
                last.then_inc(c_t_ps, 1)

            def score_sides(k, b, s):
                if b == 0 and s == 0:
                    pe.wait_ge(c_t_sb, k + 1)
                    pe.nop(nofuse=True)
                use_misc(c_side_sb, k * (NB * SIDES) + (b * SIDES + s + 1))
                nc.tensor.matmul(ps[:, MISC, :], norm2_t[:, b * P:(b + 1) * P], w_side[:, s * 512:(s + 1) * 512],
                                 start=True, stop=True).then_inc(c_side_ps, 1)

            def project_queries(k, g):
                use_misc(c_q_sb, k * 4 + (g + 1))
                nc.tensor.matmul(ps[:, MISC, :], wq_s[:, g * P:(g + 1) * P], norm_now[:],
                                 start=True, stop=True).then_inc(c_q_ps, 1)

            def transpose_keys(k, b):
                pe.wait_ge(c_kv, k * NB + (b + 1))
                pe.nop(nofuse=True)
                use_misc(c_kt_sb, k * NB + (b + 1))
                for g in range(G // 2):
                    last = nc.tensor.transpose(ps[:, MISC, g * P:(g + 1) * P],
                                               kk[:, b, 2 * g:2 * g + 2, :].rearrange("x h d -> x (h d)"), ident[:])
                last.then_inc(c_kt_ps, 1)

            def score_pair(k, hd):
                use_misc(c_rest1, k * D + (hd + 1))
                nc.tensor.matmul(ps[:, MISC, :], w_pair[:, hd, :, :].rearrange("x s k -> x (s k)"),
                                 norm2_t[:], start=True, stop=False)
                pe.wait_ge(c_diag, k * (2 * D) + (hd + 1))
                pe.nop(nofuse=True)
                for b in range(NB):
                    last = nc.tensor.matmul(ps[:, MISC, b * P:(b + 1) * P], first_side[:],
                                            diag[:, hd % 2, b, :], start=False, stop=(b == NB - 1))
                last.then_inc(c_pair_ps, 1)

            def sum_scores(k, c, first):
                if c % CH == 0:
                    pe.wait_ge(c_parts, k * D + (c // CH + 1))
                    pe.nop(nofuse=True)
                if c >= 2 or not first:
                    pe.wait_ge(c_expo, k * STEPS + (c - 1))
                    pe.nop(nofuse=True)
                for t in range(3):
                    last = nc.tensor.matmul(ps[:, U + c % 2, :], pick[:, c % CH, :], parts[:, c // CH, t, :],
                                            start=(t == 0), stop=(t == 2))
                last.then_inc(c_u, 1)

            def mix_dense(k, c, first):
                hd, n = c // CH, c // PIECE
                if c % PIECE == 0:
                    pe.wait_ge(c_table_in[n % 2], k * (8 * D * CH // PIECE) + 16 * (n // 2 + 1))
                    pe.nop(nofuse=True)
                if c % CH == 0 and (hd >= 2 or not first):
                    pe.wait_ge(c_dense, k * D + (hd - 1))
                    pe.nop(nofuse=True)
                pe.wait_ge(c_w, k * STEPS + (c + 1))
                pe.nop(nofuse=True)
                nc.tensor.matmul(ps[:, ACC + hd % 2, :], table[:, n % 2, c % PIECE, :], dense_w[:, c % WBUFS, :],
                                 start=(c % CH == 0), stop=(c % CH == CH - 1)).then_inc(c_mm, 1)

            def spread_sums(k, hd):
                pe.wait_ge(c_diag, k * (2 * D) + (D + hd + 1))
                pe.nop(nofuse=True)
                use_misc(c_rsum_sb, k * D + (hd + 1))
                for b in range(NB):
                    last = nc.tensor.matmul(ps[:, MISC, b * P:(b + 1) * P], ones[:], diag[:, hd % 2, b, :],
                                            start=True, stop=True)
                last.then_inc(c_rsum_ps, 1)

            def transpose_values(k, hd):
                pe.wait_ge(c_dense, k * D + (hd + 1))
                pe.nop(nofuse=True)
                use_misc(c_vt_sb, k * D + (hd + 1))
                half = slice(E, P) if hd % 2 == 0 else slice(0, E)
                for b in range(NB):
                    last = nc.tensor.transpose(ps[:, MISC, b * E:(b + 1) * E], v_dense[half, b * P:(b + 1) * P],
                                               ident[half, half])
                last.then_inc(c_vt_ps, 1)

            def sum_over_tokens(k):
                pe.wait_ge(c_sums, k + 1)
                pe.nop(nofuse=True)
                use_misc(c_sums_sb, k + 1)
                nc.tensor.matmul(ps[0:1, MISC, 0:2 * D], ones[:, 0:1], sums[:].rearrange("x t h -> x (t h)"),
                                 start=True, stop=True).then_inc(c_sums_ps, 1)

            def repair_head(hd, n):
                for b in range(NB):
                    last = nc.tensor.matmul(ps[:, MISC, b * P:(b + 1) * P], norm_now[:, b * P:(b + 1) * P],
                                            w_pair[:, hd, :, :].rearrange("x s k -> x (s k)"),
                                            start=True, stop=True)
                last.then_inc(r_side_ps, 1)
                pe.wait_ge(r_kv, n + 1)
                pe.nop(nofuse=True)
                for b in range(NB):
                    last = nc.tensor.transpose(ps[0:E, MISC, b * P:(b + 1) * P], r_keys[:, b, :], ident[:])
                last.then_inc(r_kt_ps, 1)
                pe.wait_ge(r_kt_sb, n + 1)
                pe.nop(nofuse=True)

            def similarities(k, s):
                b, h = divmod(s, H)
                half = slice((h % 2) * E, (h % 2 + 1) * E)
                w = (b + 1) * P
                if s == 0:
                    pe.wait_ge(c_handed, k + 1)
                else:
                    pe.wait_ge(c_probs, k * ATTEND + s)
                pe.nop(nofuse=True)
                nc.tensor.matmul(ps[:, SIM, 0:w], qt[half, h // 2, b * P:w], kt[half, h // 2, 0:w],
                                 start=True, stop=False)
                nc.tensor.matmul(ps[:, SIM, b * P:w], ident16[:], causal[:],
                                 start=False, stop=True).then_inc(c_sim, 1)

            def transpose_probs(k, s):
                b, h = divmod(s, H)
                pe.wait_ge(c_probs, k * ATTEND + (s + 1))
                pe.nop(nofuse=True)
                if s >= 1:
                    pe.wait_ge(c_pt_sb, k * ATTEND + s)
                    pe.nop(nofuse=True)
                for j in range(b + 1):
                    last = nc.tensor.transpose(ps[:, PT, j * P:(j + 1) * P],
                                               probs[:, s % 2, j * P:(j + 1) * P], ident[:])
                last.then_inc(c_pt_ps, 1)

            def attend(k, s):
                b, h = divmod(s, H)
                pe.wait_ge(c_pt_sb, k * ATTEND + (s + 1))
                pe.nop(nofuse=True)
                if h == 0 and b > 0:
                    pe.wait_ge(c_o_sb, k * NB + b)
                    pe.nop(nofuse=True)
                for j in range(b + 1):
                    last = nc.tensor.matmul(ps[:, O, h * E:(h + 1) * E], probs_t[:, s % 2, j * P:(j + 1) * P],
                                            vv[:, j, h, :], start=(j == 0), stop=(j == b))
                if h == H - 1:
                    last.then_inc(c_o_ps, 1)

            def project(k, b, part):
                if part == 0:
                    pe.wait_ge(c_o_sb, k * NB + (b + 1))
                    pe.nop(nofuse=True)
                    use_misc(c_ot_sb, k * NB + (b + 1))
                    for g in range(4):
                        last = nc.tensor.transpose(
                            ps[:, MISC, g * P:(g + 1) * P],
                            attended[:, 2 * g:2 * g + 2, :].rearrange("x h d -> x (h d)"), ident[:])
                    last.then_inc(c_ot_ps, 1)
                else:
                    pe.wait_ge(c_ot_sb, k * NB + (b + 1))
                    pe.nop(nofuse=True)
                    use_misc(c_y_sb, k * NB + (b + 1))
                    for g in range(4):
                        last = nc.tensor.matmul(ps[:, MISC, 0:E], attended_t[:, g, :], wo_s[:, g, :],
                                                start=(g == 0), stop=(g == 3))
                    last.then_inc(c_y_ps, 1)

            def attention_step(k, s):
                if s < ATTEND:
                    similarities(k, s)
                if 1 <= s <= ATTEND:
                    transpose_probs(k, s - 1)
                if s >= H + 3 and (s - 3) % H == 0:
                    project(k, (s - 3) // H - 1, 0)
                if s >= H + 4 and (s - 4) % H == 0:
                    project(k, (s - 4) // H - 1, 1)

            def attend_step(k, s):
                if 2 <= s <= ATTEND + 1:
                    attend(k, s - 2)

            def beside(k, c, more):
                if more and c == KEEP:
                    transpose_tokens(k + 1)
                for b in range(NB):
                    for side in range(SIDES):
                        if more and c == CHOOSE[b] - 4 + 2 * side:
                            score_sides(k + 1, b, side)
                    if c == KEYS[b]:
                        transpose_keys(k, b)
                for hd in range(D):
                    if c == CH * hd + 20:
                        spread_sums(k, hd)
                    if c == CH * (hd + 1) + 7:
                        transpose_values(k, hd)
                    if more and c == PAIR[hd]:
                        score_pair(k + 1, hd)
                if c in QUERY:
                    project_queries(k, QUERY.index(c))
                if c == SUMS:
                    sum_over_tokens(k)
                if c == REPAIR:
                    pe.wait_ge(*misc_out.pop())
                    pe.nop(nofuse=True)
                    repair(pe, k, repaired, repair_head)

            def end_row(k, c, more):
                if c < LAG:
                    mix_dense(k, STEPS - LAG + c, False)
                beside(k, STEPS + c, more)

            def row(k, first, more):
                for c in range(STEPS):
                    sum_scores(k, c, first)
                    if c >= LAG:
                        mix_dense(k, c - LAG, first)
                    if not first and c < WRAP:
                        end_row(k - 1, c, True)
                    if not first and c in AT:
                        attention_step(k - 1, AT[c])
                    if not first and c - 1 in AT:
                        attend_step(k - 1, AT[c - 1])
                    beside(k, c, more)

            repaired = repaired_heads(pe)
            transpose_tokens(0)
            for b in range(NB):
                for s in range(SIDES):
                    score_sides(0, b, s)
            for hd in range(D):
                score_pair(0, hd)
            row(0, True, True)
            with pe.Fori(1, R - 1) as k:
                misc_out[:] = [(c_rest1, k * D + (PAIRS_BEFORE + 1))]
                row(k, False, True)
            misc_out[:] = [(c_rest1, (R - 1) * D + (PAIRS_BEFORE + 1))]
            row(R - 1, False, False)
            for c in range(WRAP):
                end_row(R - 1, c, False)
            for s in range(ATTEND + 6):
                attention_step(R - 1, s)
                attend_step(R - 1, s)

        @block.scalar
        def _(act):
            act.wait_ge(side_ps, 1)
            nc.scalar.copy(w_side[:].rearrange("x (a g k) -> x a g k", a=4, g=4),
                           ps[0:E, 0:4, 0:4 * NK].rearrange("x g (a k) -> x a g k", a=4))
            nc.scalar.drain()
            nc.scalar.copy(w_pair[:], w_side[:].rearrange("x (s h k) -> x h s k", s=SIDES, h=H)[:, 0:D]
                           ).then_inc(side_sb, 1)

            with act.Fori(0, R // 2) as r2:
                for u in range(2):
                    act.wait_ge(a_t_ps, r2 * 2 + (u + 1))
                    act.nop(nofuse=True)
                    nc.scalar.copy(raw_t[:, u], ps[:, 4 * u:4 * u + 2, :].rearrange("x s c -> x (s c)")
                                   ).then_inc(a_t_sb, 1)
                for u in range(2):
                    act.wait_ge(a_shifted, r2 * 2 + (u + 3))
                    act.nop(nofuse=True)
                    nc.scalar.activation(expd[:, u], shifted[:, u], ACT.Exp).then_inc(a_exp, 1)

            act.wait_ge(done_a, 1)
            with act.Fori(0, NB) as cb:
                act.wait_ge(b_var, cb + 1)
                act.nop(nofuse=True)
                nc.scalar.activation(ln_b, ln_a, ACT.Sqrt).then_inc(b_std, 1)
                for g in range(8):
                    act.wait_ge(b_t_ps, cb * 8 + (g + 1))
                    act.nop(nofuse=True)
                    nc.scalar.copy(norm_t[0:E, g % 2, :], ps[0:E, g % 2, :]).then_inc(b_t_sb, 1)
                act.wait_ge(b_qshift, cb + 1)
                act.nop(nofuse=True)
                nc.scalar.activation(qkv[:, 0], qkv[:, 0], ACT.Exp).then_inc(b_qexp, 1)
                act.wait_ge(b_kshift, cb + 1)
                act.nop(nofuse=True)
                nc.scalar.activation(qkv[:, 1], qkv[:, 1], ACT.Exp).then_inc(b_kexp, 1)
                for m in range(2):
                    for hh in range(2):
                        act.wait_ge(b_qt_ps, cb * 4 + (2 * m + hh + 1))
                        act.nop(nofuse=True)
                        nc.scalar.copy(q_t[:, m, :, 4 * hh:4 * hh + 4].rearrange("x c h -> x h c"),
                                       ps[:, 3 + 2 * m + hh, :].rearrange("x (h c) -> x h c", h=4)
                                       ).then_inc(b_qt_sb, 1)

            act.wait_ge(done_b, 3)
            act.wait_ge(b_kept, 16)

            def load_row(k, dst, landed):
                act.dma_start(dst.rearrange("x b e -> x (b e)"),
                              kept[bass.ds(k, 1), :, :].rearrange("r p c -> (r p) c")).then_inc(landed, 16)

            def norm(k):
                act.wait_ge(c_var, k + 1)
                nc.scalar.activation(ln2[:, 1], ln2[:, 0], ACT.Sqrt).then_inc(c_std, 1)

            def transpose_tokens(k):
                act.wait_ge(c_t_ps, k + 1)
                nc.scalar.copy(norm2_t[:], ps[0:E, MISC, :]).then_inc(c_t_sb, 1)

            def score_sides(k, b, s):
                act.wait_ge(c_side_ps, k * (NB * SIDES) + (b * SIDES + s + 1))
                if s == 0:
                    act.wait_ge(c_side_used, k * NB + (b + 1))
                nc.scalar.copy(sides[:, s].rearrange("x h k -> x (h k)"), ps[:, MISC, :]).then_inc(c_side_sb, 1)

            def weights(k, b):
                act.wait_ge(c_best, k * NB + (b + 1))
                nc.scalar.activation(weight_in[:], weight_in[:], ACT.Exp).then_inc(c_wexp, 1)

            def project_queries(k, g):
                act.wait_ge(c_q_ps, k * 4 + (g + 1))
                nc.scalar.mul(qt[:, g, :], ps[:, MISC, :], float(E) ** -0.5).then_inc(c_q_sb, 1)

            def split_pair(k, hd, part):
                if part == 0:
                    act.wait_ge(c_pair_ps, k * D + (hd + 1))
                    nc.scalar.copy(parts[:, hd, 0, :], ps[:, MISC, :]).then_inc(c_part1, 1)
                else:
                    act.wait_ge(c_rest1, k * D + (hd + 1))
                    nc.scalar.copy(parts[:, hd, 1, :], rest[:, hd % 2, :]).then_inc(c_part2, 1)

            def exponentials(k, c, first):
                act.wait_ge(c_u, k * STEPS + (c + 1))
                if c >= BUFS or not first:
                    act.wait_ge(c_w, k * STEPS + (c - BUFS + 1))
                nc.scalar.activation(expo[:, c % BUFS, :], ps[:, U + c % 2, :], ACT.Exp).then_inc(c_expo, 1)

            def weigh(k, b, h, s):
                if s == 0:
                    act.wait_ge(c_landed[h], k * (NB * TOP * 16) + (b + 1) * TOP * 16)
                g = nc.scalar.mul(gathered[:, h, s, :], gathered[:, h, s, :], weight[:, b, h, s:s + 1])
                if s == TOP - 1:
                    g.then_inc(c_scaled, 1)

            def transpose_keys(k, b):
                act.wait_ge(c_kt_ps, k * NB + (b + 1))
                nc.scalar.copy(kt_next[:, D // 2:, b * P:(b + 1) * P],
                               ps[:, MISC, 0:256].rearrange("x (g c) -> x g c", g=2)).then_inc(c_kt_sb, 1)

            def spread(k, hd, kind, first=False):
                if kind == 0:
                    act.wait_ge(c_best, k * NB + NB)
                else:
                    act.wait_ge(c_rsum_set, k + 1)
                if hd >= 2:
                    act.wait_ge([c_pair_ps, c_rsum_ps][kind], k * D + (hd - 1))
                elif kind == 1:
                    act.wait_ge(c_pair_ps, k * D + (hd + 3))
                elif not first:
                    act.wait_ge(c_rsum_ps, k * D + (hd - 1))
                v = [neg_thr, rsum][kind]
                for b in range(NB):
                    last = nc.scalar.mul(diag[:, hd % 2, b, :], ident[:], v[:, hd, b:b + 1])
                last.then_inc(c_diag, 1)

            def spread_sums(k, hd):
                act.wait_ge(c_rsum_ps, k * D + (hd + 1))
                if hd > 0:
                    act.wait_ge(c_dense, k * D + hd)
                nc.scalar.copy(rsum_wide[:], ps[:, MISC, :]).then_inc(c_rsum_sb, 1)

            def transpose_values(k, hd):
                act.wait_ge(c_vt_ps, k * D + (hd + 1))
                nc.scalar.copy(vv_next[:, :, hd, :], ps[:, MISC, 0:256].rearrange("x (b d) -> x b d", b=NB)
                               ).then_inc(c_vt_sb, 1)

            def attention_probs(k, s):
                if s < ATTEND:
                    b, h = divmod(s, H)
                    w = (b + 1) * P
                    act.wait_ge(c_max, k * ATTEND + (s + 1))
                    act.nop(nofuse=True)
                    if s >= 2:
                        act.wait_ge(c_pt_ps, k * ATTEND + (s - 1))
                        act.nop(nofuse=True)
                    nc.scalar.activation(probs[:, s % 2, 0:w], ps[:, SIM, 0:w], ACT.Exp,
                                         bias=neg_max[:, s % 4:s % 4 + 1],
                                         accum_out=den[:, b % 2, h:h + 1]).then_inc(c_probs, 1)

            def attention_copies(k, s):
                if 1 <= s <= ATTEND:
                    w = ((s - 1) // H + 1) * P
                    act.wait_ge(c_pt_ps, k * ATTEND + s)
                    act.nop(nofuse=True)
                    nc.scalar.copy(probs_t[:, (s - 1) % 2, 0:w], ps[:, PT, 0:w]).then_inc(c_pt_sb, 1)
                if s >= H + 3 and (s - 3) % H == 0:
                    b = (s - 3) // H - 1
                    act.wait_ge(c_ot_ps, k * NB + (b + 1))
                    act.nop(nofuse=True)
                    nc.scalar.copy(attended_t[:].rearrange("x g c -> x (g c)"), ps[:, MISC, :]
                                   ).then_inc(c_ot_sb, 1)
                if s >= H + 5 and (s - 5) % H == 0:
                    b = (s - 5) // H - 1
                    act.wait_ge(c_y_sb, k * NB + (b + 1))
                    act.dma_start(out[bass.ds(k, 1), b * P:(b + 1) * P, :].rearrange("o p e -> (o p) e"),
                                  result[:, b, :]).then_inc(c_stored[b], 16)

            def repair_head(hd, n):
                act.wait_ge(r_side_ps, n + 1)
                act.nop(nofuse=True)
                for s in range(SIDES):
                    last = nc.scalar.copy(sides[:, s, D:H, :],
                                          ps[:, MISC, :].rearrange("x (b s k) -> x b s k", b=NB, s=SIDES)[:, :, s])
                last.then_inc(r_side_sb, 1)
                act.wait_ge(r_best, n + 1)
                act.nop(nofuse=True)
                nc.scalar.activation(weight_in[:, D:H], weight_in[:, D:H], ACT.Exp).then_inc(r_wexp, 1)
                act.wait_ge(r_kt_ps, n + 1)
                act.nop(nofuse=True)
                half = slice((hd % 2) * E, (hd % 2 + 1) * E)
                nc.scalar.copy(kt_next[half, hd // 2, :], ps[0:E, MISC, :])
                nc.scalar.copy(kt[half, hd // 2, :], ps[0:E, MISC, :]).then_inc(r_kt_sb, 1)

            def keep_tokens():
                nc.scalar.copy(norm_now[:], norm2_t[:])
                nc.scalar.drain()

            def hand_over(n):
                low, done = slice(0, E), (NB - 1) * P
                nc.scalar.drain()
                if n == 0:
                    nc.scalar.copy(kt[:, 0, :], kt_next[:, 0, :])
                elif n == 1:
                    nc.scalar.copy(kt[low, 1, :], kt_next[low, 1, :])
                elif n == 2:
                    nc.scalar.copy(kt[:, D // 2:, 0:done], kt_next[:, D // 2:, 0:done])
                elif n == 3:
                    nc.scalar.copy(vv[:, :, 0:D - 1, :], vv_next[:, :, 0:D - 1, :])
                elif n == 4:
                    nc.scalar.copy(vv[:, 0:NB - 1, D:H, :], vv_next[:, 0:NB - 1, D:H, :])

            def hand_over_rest():
                high, done = slice(E, P), (NB - 1) * P
                nc.scalar.drain()
                nc.scalar.copy(kt[high, 1, :], kt_next[high, 1, :])
                nc.scalar.copy(kt[:, D // 2:, done:N], kt_next[:, D // 2:, done:N])
                nc.scalar.copy(vv[:, :, D - 1, :], vv_next[:, :, D - 1, :])
                nc.scalar.copy(vv[:, NB - 1, D:H, :], vv_next[:, NB - 1, D:H, :])
                nc.scalar.drain().then_inc(c_handed, 1)

            def beside(k, c, more):
                if more and c == 0:
                    load_row(k + 1, row_ln[:], c_ln_in)
                if more and c == KEEP - 3:
                    norm(k + 1)
                if c == KEEP:
                    keep_tokens()
                if more and c == KEEP + 1:
                    transpose_tokens(k + 1)
                for b in range(NB):
                    for side in range(SIDES):
                        if more and c == CHOOSE[b] - 3 + 2 * side:
                            score_sides(k + 1, b, side)
                    if more and c == CHOOSE[b] + 20:
                        weights(k + 1, b)
                    if c == KEYS[b] + 1:
                        transpose_keys(k, b)
                for hd in range(D):
                    if c == CH * hd + 14:
                        spread(k, hd, 1)
                    if more and c == PAIR[hd] - 1:
                        spread(k + 1, hd, 0)
                    if c == CH * hd + 21:
                        spread_sums(k, hd)
                    if c == CH * (hd + 1) + 8:
                        transpose_values(k, hd)
                    if more and c == PAIR[hd] + 1:
                        split_pair(k + 1, hd, 0)
                    if more and c == PAIR[hd] + 3:
                        split_pair(k + 1, hd, 1)
                if 0 <= c - HAND < 5:
                    hand_over(c - HAND)
                if c - 1 in QUERY:
                    project_queries(k, QUERY.index(c - 1))
                if c == REPAIR:
                    repair(act, k, repaired, repair_head)
                if c == HAND_REST:
                    hand_over_rest()

            def row(k, first, more):
                for c in range(STEPS):
                    b, j = divmod(c, QUARTER)
                    exponentials(k, c, first)
                    for s in range(2 * j, 2 * j + 2):
                        weigh(k, b, s // TOP, s % TOP)
                    if not first and c < WRAP:
                        beside(k - 1, STEPS + c, True)
                    if not first and c == WRAP - 1:
                        load_row(k - 1, row_add[:], c_add_in)
                    if not first and c - 1 in AT:
                        attention_probs(k - 1, AT[c - 1])
                    if not first and c - 1 in AT:
                        attention_copies(k - 1, AT[c - 1])
                    beside(k, c, more)

            repaired = repaired_heads(act)
            load_row(0, row_ln[:], c_ln_in)
            norm(0)
            transpose_tokens(0)
            for b in range(NB):
                for s in range(SIDES):
                    score_sides(0, b, s)
                weights(0, b)
            for hd in range(D):
                spread(0, hd, 0, True)
                split_pair(0, hd, 0)
                split_pair(0, hd, 1)
            row(0, True, True)
            with act.Fori(1, R - 1) as k:
                row(k, False, True)
            row(R - 1, False, False)
            for c in range(WRAP):
                beside(R - 1, STEPS + c, False)
            load_row(R - 1, row_add[:], c_add_in)
            for s in range(ATTEND + 6):
                attention_probs(R - 1, s)
                attention_copies(R - 1, s)
            for b in range(NB):
                act.wait_ge(c_stored[b], 16 + 16 * R)

        @block.vector
        def _(dve):
            tt, ts, red = nc.vector.tensor_tensor, nc.vector.tensor_scalar, nc.vector.tensor_reduce
            drain = nc.vector.drain
            dve.wait_ge(const_made, 7)
            nc.vector.tensor_copy(cell_no[:], cell_i[:])
            nc.vector.tensor_copy(head_base[:], head_i[:])
            drain().then_inc(a_raw_free, 2)
            drain().then_inc(a_shifted, 2)

            with dve.Fori(0, R // 2) as r2:
                for u in range(2):
                    scores = ps[:, 4 * u + 2:4 * u + 4, :].rearrange("x s (b c) -> x (s b) c", c=256)
                    dve.wait_ge(a_scores, r2 * 2 + (u + 1))
                    dve.nop(nofuse=True)
                    gmax = group_max[:, u].rearrange("x (b g) -> x b g", b=NB)
                    red(gmax, scores.rearrange("x b (q g) -> x b g q", q=POOL), AX.X, ALU.max)
                    drain()
                    tt(shifted[:, u].rearrange("x (b q g) -> x b q g", b=NB, q=POOL),
                       scores.rearrange("x b (q g) -> x b q g", q=POOL),
                       gmax.unsqueeze(2).to_broadcast([P, NB, POOL, E]), ALU.subtract).then_inc(a_shifted, 1)
                for u in range(2):
                    dve.wait_ge(a_exp, r2 * 2 + (u + 1))
                    dve.nop(nofuse=True)
                    gden = group_den[:, u].rearrange("x (b g) -> x b g", b=NB)
                    gnum = group_num[:, u].rearrange("x (b g) -> x b g", b=NB)
                    red(gden, expd[:, u].rearrange("x (b q g) -> x b g q", b=NB, q=POOL), AX.X, ALU.add)
                    drain()
                    nc.vector.reciprocal(gden, gden)
                    dve.wait_ge(a_weighted, r2 * 2 + (u + 1))
                    dve.nop(nofuse=True)
                    red(gnum, weighted[:, u].rearrange("x (b q g) -> x b g q", b=NB, q=POOL), AX.X, ALU.add
                        ).then_inc(a_raw_free, 1)
                    drain()
                    tt(pooled[:, r2 * 2 + u, :, :], gnum, gden, ALU.mult)
            drain().then_inc(done_a, 1)

            def wide(v, shape, axis):
                return v.unsqueeze(axis).to_broadcast(shape)

            with dve.Fori(0, NB) as cb:
                src = pooled[:, :, bass.ds(cb, 1), :].rearrange("x r o e -> x r (o e)")
                red(ln_a, src, AX.X, ALU.add)
                drain()
                ts(ln_a, ln_a, 1.0 / E, None, ALU.mult)
                drain()
                tt(normed[:], src, wide(ln_a, [P, R, E], 2), ALU.subtract)
                drain()
                tt(squares, normed[:], normed[:], ALU.mult)
                drain()
                red(ln_a, squares, AX.X, ALU.add)
                drain()
                ts(ln_a, ln_a, 1.0 / E, EPS, ALU.mult, ALU.add).then_inc(b_var, 1)
                dve.wait_ge(b_std, cb + 1)
                dve.nop(nofuse=True)
                nc.vector.reciprocal(ln_b, ln_b)
                drain()
                tt(normed[:], normed[:], wide(ln_b, [P, R, E], 2), ALU.mult).then_inc(b_normed, 1)
                for g in range(8):
                    dve.wait_ge(b_qkv_ps, cb * 8 + (g + 1))
                    dve.nop(nofuse=True)
                    bank = 2 + 2 * (g % 2)
                    for t in range(3):
                        for s in range(2):
                            r0 = 4 * g + 2 * s
                            last = tt(qkv[:, t, :, r0:r0 + 2, :].rearrange("x h r d -> x r h d"),
                                      ps[:, bank + s, 0:384].rearrange("x (i t h d) -> x i t h d", i=2, t=3, h=H)
                                      [:, :, t],
                                      bqkv_s[:, t * E:(t + 1) * E].rearrange("x (h d) -> x h d", h=H)
                                      .unsqueeze(1).to_broadcast([P, 2, H, HD]), ALU.add)
                    last.then_inc(b_qkv_sb, 1)
                drain()
                keys = qkv[:, 1].rearrange("x h r d -> x h (r d)")
                red(k_headmax, qkv[:, 1].rearrange("x h r d -> x (r d) h"), AX.X, ALU.max).then_inc(b_headmax, 1)
                queries = qkv[:, 0].rearrange("x h r d -> x h (r d)")
                red(q_max, queries, AX.X, ALU.max)
                drain()
                tt(queries, queries, wide(q_max, [P, H, R * HD], 2),
                   ALU.subtract).then_inc(b_qshift, 1)
                dve.wait_ge(b_headmax_t, cb + 1)
                dve.nop(nofuse=True)
                red(max_t, ps[:, 6, 0:256].rearrange("x (m f c) -> x m f c", m=2, f=2), AX.X, ALU.max)
                drain()
                tt(diag_max.rearrange("x m f c -> x (m f) c"), wide(ident[:], [P, 4, P], 1),
                   wide(max_t.rearrange("x m f -> x (m f)"), [P, 4, P], 2), ALU.mult).then_inc(b_diag, 1)
                dve.wait_ge(b_kmax, cb + 1)
                dve.nop(nofuse=True)
                tt(keys, keys, wide(ps[:, 7, 0:256], [P, H, R * HD], 1),
                   ALU.subtract).then_inc(b_kshift, 1)
                dve.wait_ge(b_qexp, cb + 1)
                dve.nop(nofuse=True)
                red(q_sum, queries, AX.X, ALU.add)
                drain()
                nc.vector.reciprocal(q_sum, q_sum)
                drain()
                tt(queries, queries, wide(q_sum, [P, H, R * HD], 2),
                   ALU.mult).then_inc(b_qnormed, 1)
                dve.wait_ge(b_ctx_ps, cb + 1)
                dve.nop(nofuse=True)
                for f in range(2):
                    nc.vector.reciprocal(k_rsum[:, 2 * f:2 * f + 2], ps[:, [2, 7][f], 0:2])
                drain()
                for f in range(2):
                    for m in range(2):
                        last = ts(context[:, f, m, :], ps[:, f, m * 256:(m + 1) * 256],
                                  k_rsum[:, 2 * f + m:2 * f + m + 1], float(R * HD) ** 0.5, ALU.mult, ALU.mult)
                last.then_inc(b_ctx_sb, 1)
                dve.wait_ge(b_out_ps, cb + 1)
                dve.nop(nofuse=True)
                for f in range(2):
                    for b in range(NB):
                        bank = [[0, 1], [2, 7]][f][b // 2]
                        lo = cb * (2 * HD) + f * HD
                        tt(tokens[:, :, b, bass.ds(lo, HD)],
                           ps[:, bank, (b % 2) * 256:(b % 2 + 1) * 256].rearrange("x (r d) -> x r d", r=R),
                           pooled[:, :, b, bass.ds(lo, HD)], ALU.add)
            drain().then_inc(done_b, 3)
            drain().then_inc(c_gather_used, G)
            drain().then_inc(c_mm, 2 * PIECE)
            for b in range(NB):
                drain().then_inc(c_stored[b], 16)
            drain().then_inc(c_side_used, 1)

            dve.wait_ge(b_kept, 16)

            def layer_norm(k):
                dve.wait_ge(c_ln_in, k * 16 + 16)
                normalise(row_ln, c_var, c_std, k, c_normed)

            def normalise(src, var, std, n, normed):
                mean = ln2[:, 0]
                red(mean, src[:], AX.X, ALU.add)
                drain()
                ts(mean, mean, 1.0 / E, None, ALU.mult)
                drain()
                tt(normed2[:], src[:], wide(mean, [P, NB, E], 2), ALU.subtract)
                drain()
                tt(sq2[:], normed2[:], normed2[:], ALU.mult)
                drain()
                red(mean, sq2[:], AX.X, ALU.add)
                drain()
                ts(mean, mean, 1.0 / E, EPS, ALU.mult, ALU.add).then_inc(var, 1)
                dve.wait_ge(std, n + 1)
                nc.vector.reciprocal(ln2[:, 1], ln2[:, 1])
                drain()
                tt(normed2[:], normed2[:], wide(ln2[:, 1], [P, NB, E], 2), ALU.mult).then_inc(normed, 1)

            def replace(lists, rest, largest, values):
                for at in lists:
                    nc.vector.match_replace(out=rest[(slice(None),) + at], imm_value=LOWEST,
                                            in_to_replace=largest[(slice(None),) + at][:, 0:8],
                                            in_values=values[(slice(None),) + at])

            def choose(k, b, n, repaired=None):
                first = D if repaired is not None else 0
                heads = slice(first, H)
                side = [[(s, h) for h in range(first, H)] for s in range(SIDES)]
                if n in (0, 1) and repaired is None:
                    dve.wait_ge(c_side_sb, k * (NB * SIDES) + (b * SIDES + n + 1))
                    dve.nop(nofuse=True)
                if n in (0, 1):
                    for s, h in side[n]:
                        nc.vector.max(top[:, s, h, 0:8], sides[:, s, h, :])
                elif n in (2, 3):
                    if n == 2:
                        drain()
                    replace(side[n - 2], sides_rest, top, sides)
                elif n == 4:
                    for s in range(SIDES):
                        for g in range(G):
                            last = nc.vector.max_index(top_at[:, s, g, 0:8], top[:, s, D + g, 0:8],
                                                       sides[:, s, D + g, :])
                    if repaired is None:
                        last.then_inc(c_side_used, 1)
                elif n in (5, 6):
                    if n == 5:
                        drain()
                    for s, h in side[n - 5]:
                        nc.vector.max(top[:, s, h, 8:16], sides_rest[:, s, h, :])
                elif n == 7:
                    drain()
                    for s in range(SIDES):
                        for g in range(G):
                            nc.vector.max_index(top_at[:, s, g, 8:16], top[:, s, D + g, 8:16],
                                                sides_rest[:, s, D + g, :])
                elif n == 8:
                    drain()
                    if repaired is None:
                        tt(code[:, 0], top_at[:, 0], head_base[:], ALU.add)
                    else:
                        ts(code[:, 0], top_at[:, 0], float(repaired * NKV), None, ALU.add)
                    ts(code[:, 1], top_at[:, 1], float(NK), None, ALU.mult)
                elif n in (9, 10):
                    drain()
                    at = 0
                    nh = H - first if n == 9 else G
                    out_, in_ = (cand[:, heads], top[:, :, heads]) if n == 9 else (cand_code, code)
                    for i0, ni, nj in CELLS:
                        tt(out_[:, :, at:at + ni * nj].rearrange("x h (i j) -> x h i j", i=ni),
                           in_[:, 0, :, i0:i0 + ni].unsqueeze(3).to_broadcast([P, nh, ni, nj]),
                           in_[:, 1, :, 0:nj].unsqueeze(2).to_broadcast([P, nh, ni, nj]), ALU.add)
                        at += ni * nj
                elif n == 11:
                    drain()
                    for h in range(first, H):
                        nc.vector.max(best[:, h, 0:8], cand[:, h, :])
                elif n == 12:
                    drain()
                    replace([(h,) for h in range(first, H)], cand_rest, best, cand)
                elif n == 13:
                    for g in range(G):
                        nc.vector.max_index(best_at[:, g, 0:8], best[:, D + g, 0:8], cand[:, D + g, :])
                    drain()
                    for h in range(first, H):
                        nc.vector.max(best[:, h, 8:16], cand_rest[:, h, :])
                elif n == 14:
                    drain()
                    for g in range(G):
                        nc.vector.max_index(best_at[:, g, 8:16], best[:, D + g, 8:16], cand_rest[:, D + g, :])
                    if repaired is None:
                        red(size[:], top[:, :, 0:D, 0:TOP:TOP - 1].rearrange("x s h t -> x h s t"), AX.XY,
                            ALU.add, apply_absolute_value=True)
                    nc.vector.tensor_copy(base[:, D:H], best[:, D:H, 0])
                    drain()
                    nc.vector.tensor_copy(best_atf[:], best_at[:])
                elif n == 15 and repaired is None:
                    nc.vector.scalar_tensor_tensor(out=base[:, 0:D], in0=size[:], scalar=-SLACK,
                                                   in1=best[:, 0:D, TOP - 1], op0=ALU.mult, op1=ALU.add)
                    drain()
                    ts(neg_thr[:, :, b], base[:, 0:D], -1.0, None, ALU.mult)
                elif n == 16:
                    tt(weight_in[:, heads], best[:, heads], wide(base[:, heads], [P, H - first, TOP], 2),
                       ALU.subtract).then_inc(c_best if repaired is None else r_best, 1)
                elif n >= 17:
                    g, m = divmod(n - 17, 3)
                    if m == 0:
                        drain()
                        tt(onehot[:], best_atf[:, g, :].unsqueeze(2).to_broadcast([P, TOP, NC_]),
                           wide(cell_no[:], [P, TOP, NC_], 1), ALU.is_equal)
                    elif m == 1:
                        drain()
                        tt(onehot[:], onehot[:], wide(cand_code[:, g, :], [P, TOP, NC_], 1), ALU.mult)
                    else:
                        drain()
                        red(best_code[:, g, :], onehot[:], AX.X, ALU.add)

            def settle(k, b):
                dve.wait_ge(c_wexp, k * NB + (b + 1))
                red(weight_sum[:], weight_in[:], AX.X, ALU.add)
                drain()
                nc.vector.tensor_copy(chosen_sum[:, 1, :, b], weight_sum[:, 0:D])
                drain()
                nc.vector.reciprocal(weight_sum[:], weight_sum[:])
                drain()
                tt(weight[:, b], weight_in[:, D:H], wide(weight_sum[:, D:H], [P, G, TOP], 2), ALU.mult)
                nc.vector.tensor_copy(rsum_next[:, :, b], weight_sum[:, 0:D])
                drain()
                nc.vector.tensor_copy(rows[:, b], best_code[:].rearrange("x h s -> x (h s)")).then_inc(c_rows, 1)

            def add_up(k, b, g, t):
                src = gathered[:, g, :, t * E:(t + 1) * E].rearrange("x s d -> x d s")
                if t == 0:
                    dve.wait_ge(c_scaled, k * (NB * G) + (b * G + g + 1))
                    red(kk[:, b, g, :], src, AX.X, ALU.add)
                else:
                    red(vv_next[:, b, D + g, :], src, AX.X, ALU.add).then_inc(c_gather_used, 1)
                    if g == G - 1:
                        drain().then_inc(c_kv, 1)

            def split_pair(k, hd, part):
                if part == 0:
                    dve.wait_ge(c_part1, k * D + (hd + 1))
                    tt(rest[:, hd % 2, :], ps[:, MISC, :], parts[:, hd, 0, :], ALU.subtract).then_inc(c_rest1, 1)
                else:
                    dve.wait_ge(c_part2, k * D + (hd + 1))
                    tt(parts[:, hd, 2, :], rest[:, hd % 2, :], parts[:, hd, 1, :], ALU.subtract).then_inc(c_parts, 1)

            def next_sums():
                nc.vector.tensor_copy(rsum[:], rsum_next[:]).then_inc(c_rsum_set, 1)
                nc.vector.tensor_copy(chosen_sum[:, 0], chosen_sum[:, 1])

            def select(k, c, first):
                dve.wait_ge(c_expo, k * STEPS + (c + 1))
                if c >= WBUFS or not first:
                    dve.wait_ge(c_mm, k * STEPS + (2 * PIECE + c - WBUFS + 1))
                e = expo[:, c % BUFS, :]
                nc.vector.scalar_tensor_tensor(out=dense_w[:, c % WBUFS, :], in0=e, scalar=1.0, in1=e,
                                               op0=ALU.is_ge, op1=ALU.mult,
                                               accum_out=dense_sum[:, c:c + 1]).then_inc(c_w, 1)

            def check_sums(k, part):
                if part == 0:
                    drain()
                    red(sums[:, 0], dense_sum[:].rearrange("x (h c) -> x h c", h=D), AX.X, ALU.add)
                    red(sums[:, 1], chosen_sum[:, 0], AX.X, ALU.add).then_inc(c_sums, 1)
                    drain()
                else:
                    dve.wait_ge(c_sums_ps, k + 1)
                    nc.vector.tensor_copy(checks[:, 0:2].rearrange("x t h -> x (t h)"), ps[0:1, MISC, 0:2 * D]
                                          ).then_inc(c_sums_sb, 1)
                    drain()
                    tt(checks[:, 0], checks[:, 0], checks[:, 1], ALU.subtract)
                    ts(checks[:, 2], checks[:, 1], SUM_LIMIT, None, ALU.is_lt)
                    drain()
                    tt(checks[:, 0], checks[:, 0], checks[:, 0], ALU.mult)
                    drain()
                    ts(checks[:, 0], checks[:, 0], SUM_ERROR ** 2, None, ALU.is_lt)
                    drain()
                    tt(checks[:, 2], checks[:, 2], checks[:, 0], ALU.mult)
                    drain()
                    red(checks[:, 1, 0:1], checks[:, 2], AX.X, ALU.min)
                    dve.wait_ge(c_flags_read, k * READERS + 2)
                    ts(flags[:, 0:D], checks[:, 2], 0.5, None, ALU.is_lt)
                    drain()
                    ts(flags[:, D:D + 1], checks[:, 1, 0:1], 0.5, None, ALU.is_lt).then_inc(c_flags, 1)

            def repair_head(hd, n):
                dve.wait_ge(r_side_sb, n + 1)
                dve.nop(nofuse=True)
                for part in range(CHOICES):
                    choose(None, None, part, repaired=hd)
                drain()
                nc.vector.tensor_copy(r_rows[:], best_code[:].rearrange("x h s -> x (h s)")).then_inc(r_rows_out, 1)
                dve.wait_ge(r_wexp, n + 1)
                dve.nop(nofuse=True)
                red(weight_sum[:, D:H], weight_in[:, D:H], AX.X, ALU.add)
                drain()
                nc.vector.reciprocal(weight_sum[:, D:H], weight_sum[:, D:H])
                drain()
                tt(r_weight[:], weight_in[:, D:H], wide(weight_sum[:, D:H], [P, G, TOP], 2), ALU.mult)
                for b in range(NB):
                    got = gathered[:, 2 + b % 2]
                    dve.wait_ge(r_landed[b], n * (TOP * 16) + TOP * 16)
                    dve.nop(nofuse=True)
                    drain()
                    tt(got, got, wide(r_weight[:, b], [P, TOP, KV], 2), ALU.mult)
                    drain()
                    red(r_keys[:, b, :], got[:, :, 0:E].rearrange("x s d -> x d s"), AX.X, ALU.add)
                    red(vv_next[:, b, hd, :], got[:, :, E:KV].rearrange("x s d -> x d s"), AX.X, ALU.add
                        ).then_inc(r_used, 1)
                drain()
                nc.vector.tensor_copy(vv[:, :, hd, :], vv_next[:, :, hd, :])
                drain().then_inc(r_kv, 1)

            def finish_dense(k, hd):
                keys, vals = (slice(0, E), slice(E, P)) if hd % 2 == 0 else (slice(E, P), slice(0, E))
                dve.wait_ge(c_mm, k * STEPS + (2 * PIECE + CH * (hd + 1)))
                dve.wait_ge(c_rsum_sb, k * D + (hd + 1))
                tt(kt_next[keys, hd // 2, :], ps[keys, ACC + hd % 2, :], rsum_wide[keys, :], ALU.mult)
                if hd > 0:
                    dve.wait_ge(c_vt_ps, k * D + hd)
                tt(v_dense[vals, :], ps[vals, ACC + hd % 2, :], rsum_wide[vals, :], ALU.mult).then_inc(c_dense, 1)

            def normalise_output(k, s):
                if s >= H + 2 and (s - 2) % H == 0:
                    b = (s - 2) // H - 1
                    dve.wait_ge(c_o_ps, k * NB + (b + 1))
                    nc.vector.reciprocal(rden[:], den[:, b % 2, :])
                    drain()
                    tt(attended[:], ps[:, O, :].rearrange("x (h d) -> x h d", h=H),
                       wide(rden[:], [P, H, E], 2), ALU.mult).then_inc(c_o_sb, 1)

            def attention_step(k, s):
                if s < ATTEND:
                    b, h = divmod(s, H)
                    dve.wait_ge(c_sim, k * ATTEND + (s + 1))
                    red(neg_max[:, s % 4:s % 4 + 1], ps[:, SIM, 0:(b + 1) * P], AX.X, ALU.max,
                        negate=True).then_inc(c_max, 1)
                if s >= H + 4 and (s - 4) % H == 0:
                    b = (s - 4) // H - 1
                    if b == 0:
                        dve.wait_ge(c_add_in, k * 16 + 16)
                    dve.wait_ge(c_y_ps, k * NB + (b + 1))
                    dve.wait_ge(c_stored[b], k * 16 + 16)
                    tt(result[:, b, :], ps[:, MISC, 0:E], row_add[:, b, :], ALU.add).then_inc(c_y_sb, 1)

            def beside(k, c, more):
                if more and c == KEEP - 4:
                    layer_norm(k + 1)
                for b in range(NB):
                    for h in range(G):
                        for t in range(2):
                            if c == QUARTER * b + QUARTER // G * (h + 1) - 1 + 3 * t:
                                add_up(k, b, h, t)
                    if more and c == CHOOSE[b] + CHOICES:
                        settle(k + 1, b)
                    if more and 0 <= c - CHOOSE[b] < CHOICES:
                        choose(k + 1, b, c - CHOOSE[b])
                for hd in range(D):
                    if c == CH * (hd + 1) + LAG - AHEAD:
                        finish_dense(k, hd)
                    if more and c == PAIR[hd] + 4 - AHEAD:
                        split_pair(k + 1, hd, 1)
                    if more and c == PAIR[hd] + 2 - AHEAD:
                        split_pair(k + 1, hd, 0)
                if more and c == NEXT_SUMS:
                    drain()
                    next_sums()
                if c == STEPS - 1:
                    check_sums(k, 0)
                if c == SUMS - AHEAD + 1:
                    check_sums(k, 1)
                if c == REPAIR:
                    repair(dve, k, repaired, repair_head)

            def row(k, first, more):
                for c in range(STEPS):
                    select(k, c, first)
                    if not first and c + AHEAD in AT:
                        normalise_output(k - 1, AT[c + AHEAD])
                        attention_step(k - 1, AT[c + AHEAD])
                    if not first and c < WRAP:
                        beside(k - 1, STEPS + c, True)
                    beside(k, c, more)

            repaired = repaired_heads(dve)
            dve.nop(nofuse=True).then_inc(c_flags_read, 2)
            layer_norm(0)
            for b in range(NB):
                for n in range(CHOICES):
                    choose(0, b, n)
                settle(0, b)
            drain()
            next_sums()
            for hd in range(D):
                split_pair(0, hd, 0)
                split_pair(0, hd, 1)
            row(0, True, True)
            with dve.Fori(1, R - 1) as k:
                row(k, False, True)
            row(R - 1, False, False)
            for c in range(WRAP):
                beside(R - 1, STEPS + c, False)
            for s in range(ATTEND + 6):
                normalise_output(R - 1, s)
                attention_step(R - 1, s)


def kernel(**inputs):
    import concourse.bacc as bacc
    from concourse.bass_utils import run_bass_kernel_spmd

    def arr(name):
        return np.asarray(inputs[name])

    arrays = {
        "x": arr("x"),
        "keysvals": np.concatenate([arr("L0_ffn_keys_table"), arr("L0_ffn_values_table")], axis=1),
        "tables": np.stack([
            np.concatenate([t[h * NKV:(h + 1) * NKV] for t in
                            ((arr("L0_ffn_keys_table"), arr("L0_ffn_values_table")) if h % 2 == 0 else
                             (arr("L0_ffn_values_table"), arr("L0_ffn_keys_table")))], axis=1)
            .reshape(CH, P, KV).transpose(1, 0, 2) for h in range(D)]),
        "w_tok": arr("L0_tok_W"),
        "w_qkv": np.concatenate([arr("L0_attn_Wq").T, arr("L0_attn_Wk").T, arr("L0_attn_Wv").T], axis=1),
        "b_qkv": np.concatenate([arr("L0_attn_bq"), arr("L0_attn_bk"), arr("L0_attn_bv")])[None, :],
        "wqpk_t": arr("L0_ffn_Wq_pk").T,
        "pk_t": arr("L0_ffn_pk_keys").transpose(0, 2, 3, 1).reshape(SIDES * H * DK, NK),
        "w_q": arr("L0_ffn_Wq"),
        "w_o": arr("L0_ffn_Wo"),
    }
    arrays = {n: np.ascontiguousarray(a) for n, a in arrays.items()}
    nc = bacc.Bacc("TRN2", target_bir_lowering=False, num_devices=1)
    args = [nc.dram_tensor(n, a.shape, F32, kind="ExternalInput").ap() for n, a in arrays.items()]
    out = nc.dram_tensor("out", (R, N, E), F32, kind="ExternalOutput").ap()
    kept = nc.dram_tensor("kept", (R, P, NB * E), F32, kind="Internal").ap()
    build(nc, *args, kept, out)
    return run_bass_kernel_spmd(nc, [arrays], core_ids=[0]).results[0]["out"]
```
